# Optimizing a Trainium2 kernel written in Bass

```python
import numpy as np
import jax
import jax.numpy as jnp

def _softmax(x, axis=-1):
    return jax.nn.softmax(x, axis=axis)

def _gelu(x):
    return jax.nn.gelu(x, approximate=True)

def _silu(x):
    return jax.nn.silu(x)

def _sigmoid(x):
    return jax.nn.sigmoid(x)

def _layernorm(x, axis=-1, eps=1e-05):
    m = jnp.mean(x, axis=axis, keepdims=True)
    v = jnp.var(x, axis=axis, keepdims=True)
    return (x - m) / jnp.sqrt(v + eps)

def _scatter_add(tgt, idx, src, axis=0):
    return tgt.at[idx].add(src)

def _segment_sum(src, seg, n):
    return jax.ops.segment_sum(src, seg, n)
kernel_name = 'mk_adaln_ffn_d2_seqx_r2_535917'

def setup_inputs(seed: int=0):
    np.random.seed(seed)
    _w = jnp.asarray

    def _rec_inputs():
        import jax
        import jax.numpy as jnp
        _rk = jax.random.key(seed)
        x = -0.0002928 + 1 * jax.random.normal(jax.random.fold_in(_rk, 1), (32, 128, 512), jnp.float32)
        _lenS = 128 - jax.random.randint(jax.random.fold_in(_rk, 7), (32,), 0, max(1, 128 // 4) + 1, jnp.int32)
        _lenS2 = 128 - jax.random.randint(jax.random.fold_in(_rk, 8), (32,), 0, max(1, 128 // 4) + 1, jnp.int32)
        cond_1024 = 0.000887014 + 1.03683 * jax.random.normal(jax.random.fold_in(_rk, 11), (32, 512), jnp.float32)
        itok_BxS_2_50255 = jax.random.randint(jax.random.fold_in(_rk, 12), (32, 128), 2, 25128, jnp.int32)
        return (x, cond_1024, itok_BxS_2_50255)
    x, cond_1024, itok_BxS_2_50255 = _rec_inputs()

    def _L0_cond_setup():
        import jax, jax.numpy as jnp
        import numpy as np
        TOP_K = 2
        N_EXPERTS = 8
        N_SHARED = 1
        EPS = 1e-09
        key = jax.random.key(seed)
        ks = jax.random.split(key, 10)
        B, T, d = (2, 1024, 512)
        h_s, h_r, E = (1024, 256, N_EXPERTS)
        return {'x': jax.random.normal(ks[0], (B, T, d), jnp.float32), 't_emb': jax.random.normal(ks[1], (B, d), jnp.float32), 'router_w': jax.random.normal(ks[2], (E, d), jnp.float32) * 0.01, 'router_t_w': jax.random.normal(ks[3], (E, d), jnp.float32) * 0.01, 'router_bias': jnp.zeros((E,), jnp.float32), 'sw1': jax.random.normal(ks[4], (h_s, d), jnp.float32) * 0.02, 'sw3': jax.random.normal(ks[5], (h_s, d), jnp.float32) * 0.02, 'sw2': jax.random.normal(ks[6], (d, h_s), jnp.float32) * 0.02, 'rw1': jax.random.normal(ks[7], (E, h_r, d), jnp.float32) * 0.02, 'rw2': jax.random.normal(ks[8], (E, d, h_r), jnp.float32) * 0.02}
    _L0_cond_all = _L0_cond_setup()
    _L0_cond_in = {k: v for k, v in _L0_cond_all.items() if k in ('router_w', 'router_t_w', 'router_bias', 'sw1', 'sw3', 'sw2', 'rw1', 'rw2')}
    del _L0_cond_all

    def _L0_ffn_setup():
        import jax, jax.numpy as jnp
        import numpy as np
        B, S, H = (8, 2048, 512)
        NAV = 128
        E = 8
        F = 2 * H
        key = jax.random.key(seed)
        ks = jax.random.split(key, 12)

        def w(k, shape, fan_in):
            return jax.random.normal(k, shape, dtype=jnp.float32) / np.sqrt(fan_in)
        return {'hidden_states': jax.random.normal(ks[0], (B, S, H), dtype=jnp.float32), 'Wp1': w(ks[1], (H, NAV), H), 'bp1': jnp.zeros((NAV,), jnp.float32), 'Wp2': w(ks[2], (NAV, E), NAV), 'bp2': jnp.zeros((E,), jnp.float32), 'W1': w(ks[3], (E, H, F), H), 'b1': jnp.zeros((E, F), jnp.float32), 'W2': w(ks[4], (E, F, H), F), 'b2': jnp.zeros((E, H), jnp.float32), 'Wo': w(ks[5], (H, H), H), 'bo': jnp.zeros((H,), jnp.float32)}
    _L0_ffn_all = _L0_ffn_setup()
    _L0_ffn_in = {k: v for k, v in _L0_ffn_all.items() if k in ('Wp1', 'bp1', 'Wp2', 'bp2', 'W1', 'b1', 'W2', 'b2', 'Wo', 'bo')}
    del _L0_ffn_all

    def _L1_cond_setup():
        import jax, jax.numpy as jnp
        import numpy as np
        HASH_PRIME = 5099
        MIN_CAPACITY = 4
        key = jax.random.key(seed)
        ks = jax.random.split(key, 8)
        B, T, D, F, E = (8, 1024, 512, 1024, 16)
        return {'x': jax.random.normal(ks[0], (B, T, D), dtype=jnp.float32), 'token_ids': jax.random.randint(ks[1], (B, T), 0, 50257, dtype=jnp.int32), 'shift_state': jax.random.normal(ks[2], (B, D), dtype=jnp.float32), 'time_maa_k': jax.random.uniform(ks[3], (D,), dtype=jnp.float32), 'time_maa_r': jax.random.uniform(ks[4], (D,), dtype=jnp.float32), 'w_recept': jax.random.normal(ks[5], (D, D), dtype=jnp.float32) * 0.02, 'w_key': jax.random.normal(ks[6], (E, D, F), dtype=jnp.float32) * 0.02, 'w_value': jax.random.normal(ks[7], (E, F, D), dtype=jnp.float32) * 0.02}
    _L1_cond_all = _L1_cond_setup()
    _L1_cond_in = {k: v for k, v in _L1_cond_all.items() if k in ('time_maa_k', 'time_maa_r', 'w_recept', 'w_key', 'w_value')}
    del _L1_cond_all

    def _L1_ffn_setup():
        import jax, jax.numpy as jnp
        import numpy as np
        from jax import lax
        T, B, I, M, O = (128, 64, 512, 512, 512)

        def _xavier(key, shape):
            fan_out, fan_in = shape
            limit = float(np.sqrt(6.0 / (fan_in + fan_out)))
            return jax.random.uniform(key, shape, jnp.float32, -limit, limit)
        key = jax.random.key(seed)
        ks = jax.random.split(key, 9)
        x = jax.random.normal(ks[0], (T, B, I), jnp.float32)
        return {'x': x, 'wf': _xavier(ks[1], (M, I)), 'uf': _xavier(ks[2], (M, M)), 'bf': jnp.zeros((M,), jnp.float32), 'wi': _xavier(ks[3], (M, I)), 'ui': _xavier(ks[4], (M, M)), 'bi': jnp.zeros((M,), jnp.float32), 'wc': _xavier(ks[5], (M, I)), 'uc': _xavier(ks[6], (M, M)), 'bc': jnp.zeros((M,), jnp.float32), 'wo': _xavier(ks[7], (O, I)), 'uo': _xavier(ks[8], (O, M)), 'bo': jnp.zeros((O,), jnp.float32), 'in_c': jnp.zeros((M,), jnp.float32)}
    _L1_ffn_all = _L1_ffn_setup()
    _L1_ffn_in = {k: v for k, v in _L1_ffn_all.items() if k in ('wf', 'uf', 'bf', 'wi', 'ui', 'bi', 'wc', 'uc', 'bc', 'wo', 'uo', 'bo', 'in_c')}
    del _L1_ffn_all
    return {'x': x, 'cond_1024': cond_1024, 'itok_BxS_2_50255': itok_BxS_2_50255, 'L0_cond_router_w': _L0_cond_in['router_w'], 'L0_cond_router_t_w': _L0_cond_in['router_t_w'], 'L0_cond_router_bias': _L0_cond_in['router_bias'], 'L0_cond_sw1': _L0_cond_in['sw1'], 'L0_cond_sw3': _L0_cond_in['sw3'], 'L0_cond_sw2': _L0_cond_in['sw2'], 'L0_cond_rw1': _L0_cond_in['rw1'], 'L0_cond_rw2': _L0_cond_in['rw2'], 'L0_ffn_Wp1': _L0_ffn_in['Wp1'], 'L0_ffn_bp1': _L0_ffn_in['bp1'], 'L0_ffn_Wp2': _L0_ffn_in['Wp2'], 'L0_ffn_bp2': _L0_ffn_in['bp2'], 'L0_ffn_W1': _L0_ffn_in['W1'], 'L0_ffn_b1': _L0_ffn_in['b1'], 'L0_ffn_W2': _L0_ffn_in['W2'], 'L0_ffn_b2': _L0_ffn_in['b2'], 'L0_ffn_Wo': _L0_ffn_in['Wo'], 'L0_ffn_bo': _L0_ffn_in['bo'], 'L1_cond_time_maa_k': _L1_cond_in['time_maa_k'], 'L1_cond_time_maa_r': _L1_cond_in['time_maa_r'], 'L1_cond_w_recept': _L1_cond_in['w_recept'], 'L1_cond_w_key': _L1_cond_in['w_key'], 'L1_cond_w_value': _L1_cond_in['w_value'], 'L1_ffn_wf': _L1_ffn_in['wf'], 'L1_ffn_uf': _L1_ffn_in['uf'], 'L1_ffn_bf': _L1_ffn_in['bf'], 'L1_ffn_wi': _L1_ffn_in['wi'], 'L1_ffn_ui': _L1_ffn_in['ui'], 'L1_ffn_bi': _L1_ffn_in['bi'], 'L1_ffn_wc': _L1_ffn_in['wc'], 'L1_ffn_uc': _L1_ffn_in['uc'], 'L1_ffn_bc': _L1_ffn_in['bc'], 'L1_ffn_wo': _L1_ffn_in['wo'], 'L1_ffn_uo': _L1_ffn_in['uo'], 'L1_ffn_bo': _L1_ffn_in['bo'], 'L1_ffn_in_c': _L1_ffn_in['in_c']}

def reference(x, cond_1024, itok_BxS_2_50255, L0_cond_router_w, L0_cond_router_t_w, L0_cond_router_bias, L0_cond_sw1, L0_cond_sw3, L0_cond_sw2, L0_cond_rw1, L0_cond_rw2, L0_ffn_Wp1, L0_ffn_bp1, L0_ffn_Wp2, L0_ffn_bp2, L0_ffn_W1, L0_ffn_b1, L0_ffn_W2, L0_ffn_b2, L0_ffn_Wo, L0_ffn_bo, L1_cond_time_maa_k, L1_cond_time_maa_r, L1_cond_w_recept, L1_cond_w_key, L1_cond_w_value, L1_ffn_wf, L1_ffn_uf, L1_ffn_bf, L1_ffn_wi, L1_ffn_ui, L1_ffn_bi, L1_ffn_wc, L1_ffn_uc, L1_ffn_bc, L1_ffn_wo, L1_ffn_uo, L1_ffn_bo, L1_ffn_in_c):
    import jax
    import jax.numpy as jnp

    def _L0_cond_ref(x, t_emb, router_w, router_t_w, router_bias, sw1, sw3, sw2, rw1, rw2):
        import jax, jax.numpy as jnp
        import numpy as np
        TOP_K = 2
        N_EXPERTS = 8
        N_SHARED = 1
        EPS = 1e-09
        B, T, C = x.shape
        N = B * T
        x_flat = x.reshape(N, C)
        shared_out = jnp.einsum('nh,dh->nd', jax.nn.silu(x_flat @ sw1.T) * (x_flat @ sw3.T), sw2)
        t_bias = t_emb @ router_t_w.T
        t_bias_flat = jnp.broadcast_to(t_bias[:, None, :], (B, T, N_EXPERTS)).reshape(N, N_EXPERTS)
        s = jax.nn.sigmoid((x_flat @ router_w.T + t_bias_flat).astype(jnp.float32))
        sel_scores = s + router_bias
        _, topk_idx = jax.lax.top_k(sel_scores, TOP_K)
        s_sel = jnp.take_along_axis(s, topk_idx, axis=1)
        denom = jnp.sum(s_sel, axis=1, keepdims=True)
        gates = jnp.where(denom > EPS, s_sel / (denom + EPS), 1.0 / TOP_K).astype(x.dtype)
        combine = jnp.sum(gates[:, :, None] * jax.nn.one_hot(topk_idx, N_EXPERTS, dtype=x.dtype), axis=1)
        H = jax.nn.gelu(jnp.einsum('nd,ehd->enh', x_flat, rw1), approximate=False)
        O = jnp.einsum('enh,edh->end', H, rw2)
        routed_out = jnp.einsum('end,ne->nd', O, combine)
        out = (shared_out + routed_out) / (N_SHARED + TOP_K)
        return out.reshape(B, T, C)

    def _L0_ffn_ref(hidden_states, Wp1, bp1, Wp2, bp2, W1, b1, W2, b2, Wo, bo):
        import jax, jax.numpy as jnp
        import numpy as np
        B, S, H = (8, 2048, 512)
        NAV = 128
        E = 8
        F = 2 * H
        last = hidden_states[:, -1, :]
        logits = jax.nn.gelu(last @ Wp1 + bp1, approximate=False) @ Wp2 + bp2
        action_probs = jax.nn.softmax(logits, axis=-1)
        sel = jnp.argmax(action_probs, axis=-1)
        w1 = W1[sel]
        w2 = W2[sel]
        h = jax.nn.gelu(jnp.einsum('bsh,bhf->bsf', hidden_states, w1) + b1[sel][:, None, :], approximate=False)
        reasoned = jnp.einsum('bsf,bfh->bsh', h, w2) + b2[sel][:, None, :]
        out = reasoned @ Wo + bo
        return hidden_states + 0.3 * out

    def _L1_cond_ref(x, token_ids, shift_state, time_maa_k, time_maa_r, w_recept, w_key, w_value):
        import jax, jax.numpy as jnp
        import numpy as np
        HASH_PRIME = 5099
        MIN_CAPACITY = 4
        B, T, D = x.shape
        E = w_key.shape[0]
        N = B * T
        C = max(MIN_CAPACITY, N // E)
        xprev = jnp.concatenate([shift_state[:, None, :], x[:, :-1]], axis=1)
        dxprev = xprev - x
        xk = x + dxprev * time_maa_k
        xr = x + dxprev * time_maa_r
        e_idx = token_ids.reshape(N).astype(jnp.int32) * HASH_PRIME % E
        onehot = (e_idx[:, None] == jnp.arange(E, dtype=jnp.int32)[None, :]).astype(jnp.int32)
        pos = jnp.take_along_axis(jnp.cumsum(onehot, axis=0), e_idx[:, None], axis=1)[:, 0] - 1
        keep = pos < C
        slot = jnp.where(keep, e_idx * C + pos, E * C)
        xk_flat = xk.reshape(N, D)
        buf = jnp.zeros((E * C + 1, D), dtype=x.dtype).at[slot].set(xk_flat)
        expert_in = buf[:E * C].reshape(E, C, D)
        h = jnp.square(jax.nn.relu(jnp.einsum('ecd,edf->ecf', expert_in, w_key)))
        expert_out = jnp.einsum('ecf,efd->ecd', h, w_value)
        out_pad = jnp.concatenate([expert_out.reshape(E * C, D), jnp.zeros((1, D), dtype=x.dtype)], axis=0)
        y = out_pad[slot].reshape(B, T, D)
        r = jax.nn.sigmoid(jnp.einsum('btd,ed->bte', xr, w_recept))
        return r * y

    def _L1_ffn_ref(x, wf, uf, bf, wi, ui, bi, wc, uc, bc, wo, uo, bo, in_c):
        import jax, jax.numpy as jnp
        import numpy as np
        from jax import lax
        T, B, I, M, O = (128, 64, 512, 512, 512)

        def _xavier(key, shape):
            fan_out, fan_in = shape
            limit = float(np.sqrt(6.0 / (fan_in + fan_out)))
            return jax.random.uniform(key, shape, jnp.float32, -limit, limit)
        batch = x.shape[1]
        c0 = jnp.broadcast_to(in_c, (batch, in_c.shape[0]))

        def step(c, xt):
            ft = jax.nn.sigmoid(xt @ wf.T + c @ uf.T + bf)
            it = jax.nn.sigmoid(xt @ wi.T + c @ ui.T + bi)
            gt = jnp.tanh(xt @ wc.T + c @ uc.T + bc)
            c = ft * c + it * gt
            return (c, None)
        c_final, _ = lax.scan(step, c0, x)
        h = jnp.tanh(jnp.einsum('tbi,oi->tbo', x, wo) + c_final @ uo.T + bo)
        return h
    x = x + _L0_ffn_ref(_L0_cond_ref(x, cond_1024, L0_cond_router_w, L0_cond_router_t_w, L0_cond_router_bias, L0_cond_sw1, L0_cond_sw3, L0_cond_sw2, L0_cond_rw1, L0_cond_rw2), L0_ffn_Wp1, L0_ffn_bp1, L0_ffn_Wp2, L0_ffn_bp2, L0_ffn_W1, L0_ffn_b1, L0_ffn_W2, L0_ffn_b2, L0_ffn_Wo, L0_ffn_bo)
    x = x + _L1_ffn_ref(_L1_cond_ref(x, itok_BxS_2_50255, cond_1024, L1_cond_time_maa_k, L1_cond_time_maa_r, L1_cond_w_recept, L1_cond_w_key, L1_cond_w_value), L1_ffn_wf, L1_ffn_uf, L1_ffn_bf, L1_ffn_wi, L1_ffn_ui, L1_ffn_bi, L1_ffn_wc, L1_ffn_uc, L1_ffn_bc, L1_ffn_wo, L1_ffn_uo, L1_ffn_bo, L1_ffn_in_c)
    return x

_drawn_inputs = setup_inputs


def setup_inputs(seed=0):
    import zlib

    import numpy as np

    out = dict(_drawn_inputs(seed))
    spreads = {'L0_cond_router_bias': (0.0, 0.434),
     'L0_ffn_bp1': (0.0, 0.1),
     'L0_ffn_bp2': (0.0, 0.1),
     'L0_ffn_b1': (0.0, 0.568),
     'L0_ffn_b2': (0.0, 0.268),
     'L0_ffn_bo': (0.0, 0.27),
     'L1_ffn_bf': (0.0, 0.1),
     'L1_ffn_bi': (0.0, 0.302),
     'L1_ffn_bc': (0.0, 0.1),
     'L1_ffn_bo': (0.0, 0.1),
     'L1_ffn_in_c': (0.0, 0.305)}
    factors = {'cond_1024': 3.667,
     'L0_cond_router_w': 5.308,
     'L0_cond_router_t_w': 3.873,
     'L0_ffn_Wp1': 3.877,
     'L0_ffn_W1': 8.0,
     'L0_ffn_W2': 3.856,
     'L1_cond_time_maa_r': 8.0,
     'L1_cond_w_recept': 4.668,
     'L1_ffn_wf': 8.0,
     'L1_ffn_wi': 8.0}
    for name, (base, spread) in spreads.items():
        noise = np.random.default_rng([zlib.crc32(name.encode()), seed]).standard_normal(out[name].shape)
        drawn = base * np.exp(spread * noise) if base else spread * noise
        out[name] = jnp.asarray(drawn.astype(out[name].dtype))
    for name, factor in factors.items():
        out[name] = (out[name] * factor).astype(out[name].dtype)
    return out
```

```python
import concourse.bass as bass
from concourse import mybir
from contextlib import ExitStack

FP32 = mybir.dt.float32
FP32R = mybir.dt.float32r
BF16 = mybir.dt.bfloat16
I32 = mybir.dt.int32
U32 = mybir.dt.uint32
ALU = mybir.AluOpType
ACT = mybir.ActivationFunctionType
AX = mybir.AxisListType.X

P = 128
NB = 32
NTOK = NB * P
D = 512
DC = D // P
HS = 1024
HC = HS // P
HR = 256
RC = HR // P
ER = 8
EH = 16
CAP = NTOK // EH
RT = 2 * NTOK // P + ER
NSLOT = RT * P
SLOT1, SLOT2, SLOTH, GATE1, GATE2, TOKEN = range(6)
REC = 6
EPS = 1e-9
DVE_BIG = 3.0e38


def wait_for(eng, sem, n):
    if isinstance(n, int) and n <= 0:
        return
    eng.wait_ge(sem, n)


def wait_apart(eng, sem, n):
    if isinstance(n, int) and n <= 0:
        return
    eng.wait_ge(sem, n)
    eng.nop(nofuse=True)


def software_pipeline(eng, tiles, stages, unroll=1):
    depth = max(lag for lag, _ in stages)
    head = -(-(depth + unroll) // unroll) * unroll

    def step(j, par, block=None):
        for lag, stage in stages:
            i = j - lag
            n = (par - lag) % unroll
            if not isinstance(i, int):
                stage(*((i, n, block + (par - lag - n) // unroll) if unroll > 1 else (i,)))
            elif 0 <= i < tiles:
                stage(*((i, n, i // unroll) if unroll > 1 else (i,)))

    for j in range(head):
        step(j, j % unroll)
    with eng.Fori(head // unroll, tiles // unroll) as block:
        for par in range(unroll):
            step(block * unroll + par, par, block)
    for j in range(tiles, tiles + depth):
        step(j, j % unroll)


def product(pe, out, a, w, first, last):
    (a_hi, a_lo), (w_hi, w_lo) = a, w
    pe.matmul(out, a_hi, w_hi, start=first, stop=False, skip_group_check=True)
    pe.matmul(out, a_hi, w_lo, start=False, stop=False, skip_group_check=True)
    return pe.matmul(out, a_lo, w_hi, start=False, stop=last, skip_group_check=True)


def sems(nc, ctx, prefix, names):
    own = {n[1:]: nc.alloc_semaphore(prefix + n[1:]) for n in names.split() if n[0] == "~"}
    names = " ".join(n for n in names.split() if n[0] != "~")
    made = {n: ctx.enter_context(nc.semaphore(prefix + n)) for n in names.split()}

    def clear():
        for sem in made.values():
            nc.sync.sem_clear(sem)

    ctx.callback(clear)
    return made | own



def stage_shared(nc, ins, d, keep):
    G = 8
    TG = NB // G
    NU = 12
    with ExitStack() as ctx:
        sb = lambda n, s, t=FP32: ctx.enter_context(nc.sbuf_tensor("s1_" + n, s, t))
        ps = lambda n, s, t=FP32: ctx.enter_context(nc.psum_tensor("s1_" + n, s, t))
        S = sems(nc, ctx, "s1_", "const ids x_in0 x_in1 x_used w_in0 w_in1 w_hi w_lo bias_prod sig dve pe_rank "
                 "~rec_out ~rec_in ~tokens_sent0 ~tokens_sent1 zeroed ~zero_out "
                 "xt_in xt_hi xt_lo gu silu hmul th h_hi h_lo mm2 o_ready o_out ~lists hash_members hash_total_read hash_rank_read "
                 "rank_read members rec_done")

        x_grp = sb("x_grp", [P, 2, TG, DC, P])
        w_raw = sb("w_raw", [P, 2, HS])
        w_hi = sb("w_hi", [P, NU, HS], FP32R)
        w_lo = sb("w_lo", [P, NU, HS], FP32R)
        sw2_hi = w_hi[:, 8:12, :].rearrange("p u (a n) -> p (u a) n", a=2)
        sw2_lo = w_lo[:, 8:12, :].rearrange("p u (a n) -> p (u a) n", a=2)
        ident = keep["ident"]
        tri_f = sb("tri_f", [P, P])
        tri = sb("tri", [P, P], BF16)
        ones = sb("ones", [P, P], BF16)
        ones_f = sb("ones_f", [P, P])
        expert_no = sb("expert_no", [P, EH, NB])
        new_run = sb("new_run", [P, EH, NB])
        tile_no = sb("tile_no", [P, RT, ER])
        token_no = sb("token_no", [P, NB], I32)
        ids = sb("ids", [P, NB], I32)
        hash_id = sb("hash_id", [P, NB], I32)
        cond_t = sb("cond_t", [P, DC, NB])
        rt_w = sb("rt_w", [P, DC, ER])
        r_w = sb("r_w", [P, DC, ER])
        r_bias = sb("r_bias", [P, ER])
        prod = sb("prod", [P, DC, ER, NB])
        score = sb("score", [P, ER, NB])
        sel = sb("sel", [P, ER, NB])
        t1 = sb("t1", [P, EH, NB])
        t2 = sb("t2", [P, EH, NB])
        oh1 = sb("oh1", [P, EH, NB])
        oh2 = sb("oh2", [P, ER, NB])
        member = sb("member", [P, EH, NB], BF16)
        col = sb("col", [P, 8, NB])
        cnt_i = sb("cnt_i", [P, ER], I32)
        cnt_f = sb("cnt_f", [P, 4, ER])
        tile_ge = sb("tile_ge", [P, RT, ER])
        tile_e = sb("tile_e", [P, 3, RT])
        rec = sb("rec", [P, NB, REC], I32)
        rec_f = rec[:].bitcast(FP32)
        rec_tile = sb("rec_tile", [P, 2, REC], I32)
        zero = sb("zero", [P, D])
        izero = sb("izero", [P, RT], I32)

        xt_raw = sb("xt_raw", [P, DC, P])
        xt_hi = sb("xt_hi", [P, DC, P], FP32R)
        xt_lo = sb("xt_lo", [P, DC, P], FP32R)
        sg = sb("sg", [P, 2, D])
        h = sb("h", [P, 2, D])
        ht_hi = sb("ht_hi", [P, HC, P], FP32R)
        ht_lo = sb("ht_lo", [P, HC, P], FP32R)
        o_sb = sb("o_sb", [P, D])

        gate_ps = [ps(f"gate{n}", [P, D]) for n in range(2)]
        up_ps = [ps(f"up{n}", [P, D]) for n in range(2)]
        th_ps = [ps(f"th{n}", [P, DC, P]) for n in range(2)]
        o_ps = ps("o", [P, D])
        aux_ps = ps("aux", [P, 512])
        lg_ps = aux_ps[:, 0:ER * NB].rearrange("p (e i) -> p e i", e=ER)
        aux_h = aux_ps[:, :].rearrange("p (e i) -> p e i", e=EH)
        rank_ps = aux_ps[:, 0:256].rearrange("p (e i) -> p e i", e=ER)
        tot_ps = aux_ps[:, 256:512].rearrange("p (e i) -> p e i", e=ER)

        n_const = 11

        block = ctx.enter_context(nc.Block())

        @block.sync
        def _(sp):
            for dst, src in ((ids[:], ins["ids"]), (tri_f[:], ins["c_tri"]), (ident[:], ins["c_ident"]),
                             (expert_no[:], ins["c_expert"]), (new_run[:], ins["c_run"]), (tile_no[:], ins["c_tile"]),
                             (token_no[:], ins["c_token"]), (cond_t[:], ins["cond_t"]), (rt_w[:], ins["rt_w"]),
                             (r_w[:], ins["r_w"]), (r_bias[:], ins["r_bias"].partition_broadcast(P))):
                sp.dma_start(dst, src).then_inc(S["const"], 16)
            def group_pair(g2):
                for k in range(2):
                    g = g2 * 2 + k
                    wait_for(sp, S["x_used"], g - 1)
                    sp.dma_start(x_grp[:, k], ins["xt_groups"][g]).then_inc(S[f"x_in{k}"], 16)
                units(g2 + 1)

            def units(u2):
                for n in range(2):
                    wait_for(sp, S["w_lo"], u2 * 2 + n - 1)
                    sp.dma_start(w_raw[:, n], ins["sw"][u2 * 2 + n]).then_inc(S[f"w_in{n}"], 16)

            units(0)
            group_pair(0)
            with sp.Fori(1, G // 2) as g2:
                group_pair(g2)
            units(NU // 2 - 1)

            def load_x(i):
                wait_for(sp, S["xt_lo"], i)
                sp.dma_start(xt_raw[:], ins["xt_tiles"][i]).then_inc(S["xt_in"], 16)

            def store_o(i):
                sp.wait_ge(S["o_ready"], i + 1)
                sp.dma_start(d["shared"][i], o_sb[:]).then_inc(S["o_out"], 16)

            software_pipeline(sp, NB, [(0, load_x), (2, store_o)])
            sp.wait_ge(S["o_out"], 16 * NB)

        @block.gpsimd
        def _(pool):
            pool.memset(zero[:], 0.0).then_inc(S["zeroed"], 1)
            pool.memset(izero[:], 0).then_inc(S["zeroed"], 1)
            pool.wait_ge(S["zeroed"], 2)
            pool.dma_start(d["slot_token"].rearrange("(p j) o -> p (j o)", j=RT), izero[:]).then_inc(S["lists"], 16)
            pool.dma_start(d["hash_in"].rearrange("(p r) n -> p r n", p=P),
                           zero[:, None, :].to_broadcast([P, NTOK // P, D])).then_inc(S["zero_out"], 16)
            pool.dma_start(d["hash_out"][NTOK:NTOK + 1, :], zero[0:1, :]).then_inc(S["zero_out"], 16)
            pool.wait_ge(S["lists"], 16)
            pool.wait_ge(S["rec_done"], 1)
            pool.dma_start(d["rec"].rearrange("i p c -> p i c"), rec[:]).then_inc(S["rec_out"], 16)
            pool.wait_ge(S["rec_out"], 16)

            def enter_tokens(i2, first):
                for k in range(2):
                    if not first:
                        pool.wait_ge(S[f"tokens_sent{k}"], i2 * 32)
                    pool.dma_start(rec_tile[:, k], d["rec"][i2 * 2 + k]).then_inc(S["rec_in"], 16)
                    wait_apart(pool, S["rec_in"], i2 * 32 + 16 * k + 16)
                    for c in (SLOT1, SLOT2):
                        pool.indirect_dma_start(
                            d["slot_token"], bass.IndirectOffsetOnAxis(rec_tile[:, k, c:c + 1].bitcast(U32), 0),
                            rec_tile[:, k, TOKEN:TOKEN + 1], None).then_inc(S[f"tokens_sent{k}"], 16)

            enter_tokens(0, True)
            with pool.Fori(1, NB // 2) as i2:
                enter_tokens(i2, False)
            for k in range(2):
                pool.wait_ge(S[f"tokens_sent{k}"], 16 * NB)
            pool.wait_ge(S["zero_out"], 32)

        @block.scalar
        def _(act):
            with act.Fori(0, NU // 2) as u2:
                for n in range(2):
                    act.wait_ge(S[f"w_in{n}"], u2 * 16 + 16)
                    act.activation(w_hi[:, u2 * 2 + n, :], w_raw[:, n, :], ACT.Copy).then_inc(S["w_hi"], 1)
            act.wait_ge(S["x_used"], G)
            act.activation(score[:], lg_ps, ACT.Sigmoid).then_inc(S["sig"], 1)

            def x_hi(i):
                act.wait_ge(S["xt_in"], i * 16 + 16)
                wait_for(act, S["gu"], 2 * i)
                act.activation(xt_hi[:], xt_raw[:], ACT.Copy).then_inc(S["xt_hi"], 1)

            def silu(i):
                for n in range(2):
                    act.wait_ge(S["gu"], 2 * i + n + 1)
                    wait_for(act, S["hmul"], 2 * i + n - 1)
                    act.activation(sg[:, n], gate_ps[n][:], ACT.Silu).then_inc(S["silu"], 1)

            def h_hi(i):
                for n in range(2):
                    act.wait_ge(S["th"], 2 * i + n + 1)
                    wait_for(act, S["mm2"], i)
                    act.activation(ht_hi[:, n * DC:(n + 1) * DC], th_ps[n][:], ACT.Copy).then_inc(S["h_hi"], 1)

            def o_out(i):
                act.wait_ge(S["mm2"], i + 1)
                wait_for(act, S["o_out"], i * 16)
                act.activation(o_sb[:], o_ps[:], ACT.Copy, scale=1.0 / 3.0).then_inc(S["o_ready"], 1)

            software_pipeline(act, NB, [(1, silu), (0, x_hi), (2, o_out), (1, h_hi)])

        @block.vector
        def _(dve):
            done = [0]

            def op(ins_):
                done[0] += 1
                ins_.then_inc(S["dve"], 1)
                dve.wait_ge(S["dve"], done[0])

            def signal(ins_, name):
                ins_.then_inc(S[name], 1)
                dve.wait_ge(S[name], 1)

            def ranks(experts, rank, off, incl, last_step):
                op(dve.tensor_tensor_scan(incl.rearrange("p e i -> p (e i)"),
                                          new_run[:, 0:experts].rearrange("p e i -> p (e i)"),
                                          off.rearrange("p e i -> p (e i)"), 0.0, ALU.mult, ALU.add))
                op(dve.tensor_tensor(off, incl, off, ALU.subtract))
                signal(dve.tensor_tensor(off, off, rank, ALU.add), last_step)

            dve.wait_ge(S["const"], 16 * n_const)
            dve.memset(ones[:], 1.0).then_inc(S["bias_prod"], 1)
            dve.memset(ones_f[:], 1.0).then_inc(S["bias_prod"], 1)
            dve.tensor_copy(tri[:], tri_f[:]).then_inc(S["bias_prod"], 1)
            for k in range(DC):
                dve.tensor_tensor(prod[:, k], cond_t[:, k, None, :].to_broadcast([P, ER, NB]),
                                  rt_w[:, k, :, None].to_broadcast([P, ER, NB]), ALU.mult).then_inc(S["bias_prod"], 1)

            low = col[:, 0]
            hid = hash_id[:]
            op(dve.tensor_scalar(hid, ids[:], 15, None, ALU.bitwise_and))
            op(dve.tensor_copy(low, hid))
            op(dve.tensor_scalar(low, low, 11.0, None, ALU.mult))
            op(dve.tensor_copy(hid, low))
            op(dve.tensor_scalar(hid, hid, 15, None, ALU.bitwise_and))
            op(dve.tensor_copy(low, hid))
            op(dve.tensor_tensor(oh1[:], expert_no[:], low[:, None, :].to_broadcast([P, EH, NB]), ALU.is_equal))
            signal(dve.tensor_copy(member[:], oh1[:]), "hash_members")
            dve.wait_ge(S["pe_rank"], 1)
            signal(dve.tensor_copy(t1[:], aux_h), "hash_total_read")
            dve.wait_ge(S["pe_rank"], 2)
            ranks(EH, aux_h, t1[:], t2[:], "hash_rank_read")
            op(dve.tensor_tensor(t1[:], t1[:], oh1[:], ALU.mult))
            pos, keep_, slot = col[:, 2], col[:, 3], col[:, 4]
            op(dve.tensor_reduce(pos, t1[:].rearrange("p e i -> p i e"), AX, ALU.add))
            op(dve.tensor_scalar(keep_, pos, float(CAP), None, ALU.is_lt))
            op(dve.scalar_tensor_tensor(slot, low, float(CAP), pos, ALU.mult, ALU.add))
            op(dve.scalar_tensor_tensor(slot, slot, -float(NTOK), keep_, ALU.add, ALU.mult))
            op(dve.tensor_scalar(slot, slot, float(NTOK), None, ALU.add))
            op(dve.tensor_copy(rec[:, :, SLOTH], slot))
            op(dve.tensor_copy(rec[:, :, TOKEN], token_no[:]))
            
            with dve.Fori(0, NU // 2) as u2:
                for n in range(2):
                    u = u2 * 2 + n
                    dve.wait_ge(S["w_hi"], u + 1)
                    dve.tensor_tensor(w_lo[:, u, :], w_raw[:, n, :], w_hi[:, u, :],
                                      ALU.subtract).then_inc(S["w_lo"], 1)

            def x_lo(i):
                dve.wait_ge(S["xt_hi"], i + 1)
                dve.tensor_tensor(xt_lo[:], xt_raw[:], xt_hi[:], ALU.subtract).then_inc(S["xt_lo"], 1)

            def h_mul(i):
                for n in range(2):
                    dve.wait_ge(S["silu"], 2 * i + n + 1)
                    wait_for(dve, S["th"], 2 * i + n - 1)
                    dve.tensor_tensor(h[:, n], sg[:, n], up_ps[n][:], ALU.mult).then_inc(S["hmul"], 1)

            def h_lo(i):
                for n in range(2):
                    dve.wait_ge(S["h_hi"], 2 * i + n + 1)
                    dve.tensor_tensor(ht_lo[:, n * DC:(n + 1) * DC], th_ps[n][:], ht_hi[:, n * DC:(n + 1) * DC],
                                      ALU.subtract).then_inc(S["h_lo"], 1)

            dve.wait_ge(S["sig"], 1)
            no8 = expert_no[:, 0:ER]
            op(dve.tensor_tensor(sel[:], score[:], r_bias[:, :, None].to_broadcast([P, ER, NB]), ALU.add))
            gate = []
            for c, one in ((0, oh1[:, 0:ER]), (1, oh2[:])):
                best, idx, g = col[:, c], col[:, 2 + c], col[:, 4 + c]
                op(dve.tensor_reduce(best, sel[:].rearrange("p e i -> p i e"), AX, ALU.max))
                op(dve.tensor_tensor(t1[:, 0:ER], sel[:], best[:, None, :].to_broadcast([P, ER, NB]), ALU.is_lt))
                op(dve.scalar_tensor_tensor(t1[:, 0:ER], t1[:, 0:ER], float(ER), no8, ALU.mult, ALU.add))
                op(dve.tensor_reduce(idx, t1[:, 0:ER].rearrange("p e i -> p i e"), AX, ALU.min))
                op(dve.tensor_tensor(one, no8, idx[:, None, :].to_broadcast([P, ER, NB]), ALU.is_equal))
                op(dve.tensor_tensor(t1[:, 0:ER], one, score[:], ALU.mult))
                op(dve.tensor_reduce(g, t1[:, 0:ER].rearrange("p e i -> p i e"), AX, ALU.add))
                if c == 0:
                    op(dve.scalar_tensor_tensor(sel[:], one, -DVE_BIG, sel[:], ALU.mult, ALU.add))
                gate.append(g)
            signal(dve.tensor_tensor(member[:, 0:ER], oh1[:, 0:ER], oh2[:], ALU.add), "members")

            def after_ranks():
                den, inv, above = col[:, 0], col[:, 1], col[:, 2]
                op(dve.tensor_tensor(den, gate[0], gate[1], ALU.add))
                op(dve.tensor_scalar(above, den, EPS, None, ALU.is_gt))
                op(dve.tensor_scalar(den, den, EPS, None, ALU.add))
                op(dve.reciprocal(inv, den))
                for c, g in enumerate(gate):
                    op(dve.tensor_tensor(g, g, inv, ALU.mult))
                    op(dve.scalar_tensor_tensor(g, g, -0.5, above, ALU.add, ALU.mult))
                    op(dve.tensor_scalar(g, g, 0.5, 1.0 / 3.0, ALU.add, ALU.mult))
                    op(dve.tensor_copy(rec_f[:, :, GATE1 + c], g))
                dve.wait_ge(S["pe_rank"], 3)
                op(dve.tensor_copy(t1[:, 0:ER], tot_ps))
                ranks(ER, rank_ps, t1[:, 0:ER], t2[:, 0:ER], "rank_read")
                tiles_f, end, base = cnt_f[:, 0], cnt_f[:, 1], cnt_f[:, 2]
                op(dve.tensor_scalar(tiles_f, t2[:, 0:ER, NB - 1], float(P - 1), None, ALU.add))
                op(dve.tensor_copy(cnt_i[:], tiles_f))
                op(dve.tensor_scalar(cnt_i[:], cnt_i[:], 7, None, ALU.arith_shift_right))
                op(dve.tensor_copy(tiles_f, cnt_i[:]))
                op(dve.tensor_tensor_scan(end, ones_f[:, 0:ER], tiles_f, 0.0, ALU.mult, ALU.add))
                op(dve.tensor_tensor(base, end, tiles_f, ALU.subtract))
                op(dve.tensor_scalar(base, base, float(P), None, ALU.mult))
                op(dve.tensor_tensor(t1[:, 0:ER], t1[:, 0:ER], base[:, :, None].to_broadcast([P, ER, NB]), ALU.add))
                for c, one in ((0, oh1[:, 0:ER]), (1, oh2[:])):
                    op(dve.tensor_tensor(t2[:, 0:ER], t1[:, 0:ER], one, ALU.mult))
                    op(dve.tensor_reduce(col[:, c], t2[:, 0:ER].rearrange("p e i -> p i e"), AX, ALU.add))
                    (op, lambda x: signal(x, "rec_done"))[c](dve.tensor_copy(rec[:, :, SLOT1 + c], col[:, c]))
                op(dve.tensor_tensor(tile_ge[:], tile_no[:], end[:, None, :].to_broadcast([P, RT, ER]), ALU.is_ge))
                te, new = tile_e[:, 0], tile_e[:, 1]
                op(dve.tensor_reduce(te, tile_ge[:], AX, ALU.add))
                op(dve.tensor_scalar(te, te, float(ER - 1), None, ALU.min))
                op(dve.memset(new, 1.0))
                op(dve.tensor_tensor(new[:, 2:RT], te[:, 2:RT], te[:, 0:RT - 2], ALU.not_equal))
                op(dve.tensor_copy(keep["route"][:, 0], te))
                op(dve.tensor_copy(keep["route"][:, 1], new))

            after_ranks()
            software_pipeline(dve, NB, [(1, h_mul), (0, x_lo), (1, h_lo)])

        @block.tensor
        def _(pe):
            pe.wait_ge(S["bias_prod"], 3 + DC)
            pe.wait_ge(S["hash_members"], 1)
            flat = member[:].rearrange("p e i -> p (e i)")
            pe.matmul(aux_ps[:, :], ones[:], flat, start=True, stop=True).then_inc(S["pe_rank"], 1)
            pe.wait_ge(S["hash_total_read"], 1)
            pe.matmul(aux_ps[:, :], tri[:], flat, start=True, stop=True).then_inc(S["pe_rank"], 1)
            pe.wait_ge(S["hash_rank_read"], 1)
            for k in range(DC):
                pe.matmul(aux_ps[:, 0:ER * NB], ones_f[:], prod[:, k].rearrange("p e i -> p (e i)"),
                          start=(k == 0), stop=False, skip_group_check=True)

            with pe.Fori(0, G // 2) as g2:
                for n in range(2):
                    g = g2 * 2 + n
                    pe.wait_ge(S[f"x_in{n}"], g2 * 16 + 16)
                    for tt in range(TG):
                        for k in range(DC):
                            mm = pe.matmul(lg_ps[:, :, g * TG + tt], x_grp[:, n, tt, k], r_w[:, k],
                                           start=False, stop=(k == DC - 1), skip_group_check=True)
                    mm.then_inc(S["x_used"], 1)

            def gate_up(i):
                pe.wait_ge(S["xt_lo"], i + 1)
                for n in range(2):
                    wait_for(pe, S["hmul"], 2 * i + n - 1)
                    for out, u0 in ((gate_ps[n], 0), (up_ps[n], 4)):
                        for k in range(DC):
                            mm = product(pe, out[:], (xt_hi[:, k], xt_lo[:, k]),
                                         (w_hi[:, u0 + k, n * D:(n + 1) * D], w_lo[:, u0 + k, n * D:(n + 1) * D]),
                                         k == 0, k == DC - 1)
                    mm.then_inc(S["gu"], 1)

            def turn_h(i):
                for n in range(2):
                    pe.wait_ge(S["hmul"], 2 * i + n + 1)
                    wait_for(pe, S["h_lo"], 2 * i + n - 1)
                    for k in range(DC):
                        mm = pe.transpose(th_ps[n][:, k], h[:, n, k * P:(k + 1) * P], ident[:])
                    mm.then_inc(S["th"], 1)

            def down(i):
                pe.wait_ge(S["h_lo"], 2 * i + 2)
                wait_for(pe, S["o_ready"], i)
                for k in range(HC):
                    mm = product(pe, o_ps[:], (ht_hi[:, k], ht_lo[:, k]), (sw2_hi[:, k], sw2_lo[:, k]),
                                 k == 0, k == HC - 1)
                mm.then_inc(S["mm2"], 1)

            pe.wait_ge(S["w_lo"], NU)
            pe.wait_ge(S["members"], 1)
            flat8 = member[:, 0:ER].rearrange("p e i -> p (e i)")
            pe.matmul(aux_ps[:, 0:256], tri[:], flat8, start=True, stop=True)
            pe.matmul(aux_ps[:, 256:512], ones[:], flat8, start=True, stop=True,
                      skip_group_check=True).then_inc(S["pe_rank"], 1)
            software_pipeline(pe, NB, [(1, gate_up), (2, down), (1, turn_h)])




def stage_routed(nc, ins, d, keep):
    with ExitStack() as ctx:
        sb = lambda n, s, t=FP32: ctx.enter_context(nc.sbuf_tensor("s2_" + n, s, t))
        ps = lambda n, s, t=FP32: ctx.enter_context(nc.psum_tensor("s2_" + n, s, t))
        S = sems(nc, ctx, "s2_", "idx_in0 idx_in1 ~x_in0 ~x_in1 w_in0 w_in1 w1_hi w1_lo w2_hi w2_lo tx x_hi x_lo mm1 "
                 "gelu th h_hi h_lo mm2 o_ready o_out0 o_out1")
        W1, W2 = DC * HR, RC * D
        route = keep["route"]
        ident = keep["ident"]
        idx = sb("idx", [P, 2, 1], I32)
        x = sb("x", [P, 2, D])
        w_raw = sb("w_raw", [P, 2, W1 + W2])
        w_hi = sb("w_hi", [P, 2, W1 + W2], FP32R)
        w_lo = sb("w_lo", [P, 2, W1 + W2], FP32R)
        x_hi = sb("x_hi", [P, 2, DC, P], FP32R)
        x_lo = sb("x_lo", [P, 2, DC, P], FP32R)
        h = sb("h", [P, 2, HR])
        ht_hi = sb("ht_hi", [P, 2, RC, P], FP32R)
        ht_lo = sb("ht_lo", [P, 2, RC, P], FP32R)
        o_sb = sb("o_sb", [P, 2, D])
        tx_ps = [ps(f"tx{n}", [P, DC, P]) for n in range(2)]
        h_ps = [ps(f"h{n}", [P, HR]) for n in range(2)]
        th_ps = [ps(f"th{n}", [P, RC, P]) for n in range(2)]
        o_ps = [ps(f"o{n}", [P, D]) for n in range(2)]

        block = ctx.enter_context(nc.Block())

        @block.sync
        def _(sp):
            def load(i, n, turn):
                expert = sp.value_load(route[0:1, 0, bass.ds(i, 1)], min_val=0, max_val=ER - 1)
                new = sp.value_load(route[0:1, 1, bass.ds(i, 1)], min_val=0, max_val=1)
                wait_for(sp, S[f"x_in{n}"], turn * 16)
                sp.dma_start(idx[:, n], d["slot_token"][bass.ds(i * P, P)]).then_inc(S[f"idx_in{n}"], 16)
                wait_for(sp, S["w2_lo"], i - 1)
                sp.dma_start(w_raw[:, n], ins["rw"][expert], cond=new > 0).then_inc(S[f"w_in{n}"], 16)

            def store(i, n, turn):
                sp.wait_ge(S["o_ready"], i + 1)
                sp.dma_start(d["routed"][bass.ds(i * P, P)], o_sb[:, n]).then_inc(S[f"o_out{n}"], 16)

            software_pipeline(sp, RT, [(0, load), (3, store)], 2)
            for n in range(2):
                sp.wait_ge(S[f"o_out{n}"], 16 * RT // 2)

        @block.gpsimd
        def _(pool):
            def gather(i, n, turn):
                wait_for(pool, S[f"idx_in{n}"], turn * 16 + 16)
                wait_apart(pool, S["tx"], i - 1)
                pool.indirect_dma_start(x[:, n], None, ins["x_rows"],
                                        bass.IndirectOffsetOnAxis(idx[:, n].bitcast(U32), 0)).then_inc(S[f"x_in{n}"], 16)

            software_pipeline(pool, RT, [(0, gather)], 2)

        @block.scalar
        def _(act):
            def w1_hi(i, n, turn):
                act.wait_ge(S[f"w_in{n}"], turn * 16 + 16)
                wait_for(act, S["mm1"], i - 1)
                act.activation(w_hi[:, n, 0:W1], w_raw[:, n, 0:W1], ACT.Copy).then_inc(S["w1_hi"], 1)

            def w2_hi(i, n, turn):
                wait_for(act, S["mm2"], i - 1)
                act.activation(w_hi[:, n, W1:], w_raw[:, n, W1:], ACT.Copy).then_inc(S["w2_hi"], 1)

            def x_hi_(i, n, turn):
                act.wait_ge(S["tx"], i + 1)
                wait_for(act, S["mm1"], i - 1)
                act.activation(x_hi[:, n], tx_ps[n][:], ACT.Copy).then_inc(S["x_hi"], 1)

            def gelu(i, n, turn):
                act.wait_ge(S["mm1"], i + 1)
                wait_for(act, S["th"], i - 1)
                act.activation(h[:, n], h_ps[n][:], ACT.Gelu).then_inc(S["gelu"], 1)

            def h_hi(i, n, turn):
                act.wait_ge(S["th"], i + 1)
                wait_for(act, S["mm2"], i - 1)
                act.activation(ht_hi[:, n], th_ps[n][:], ACT.Copy).then_inc(S["h_hi"], 1)

            software_pipeline(act, RT, [(1, w2_hi), (0, w1_hi), (1, gelu), (0, x_hi_), (1, h_hi)], 2)

        @block.vector
        def _(dve):
            def w1_lo(i, n, turn):
                dve.wait_ge(S["w1_hi"], i + 1)
                dve.tensor_tensor(w_lo[:, n, 0:W1], w_raw[:, n, 0:W1], w_hi[:, n, 0:W1],
                                  ALU.subtract).then_inc(S["w1_lo"], 1)

            def w2_lo(i, n, turn):
                dve.wait_ge(S["w2_hi"], i + 1)
                dve.tensor_tensor(w_lo[:, n, W1:], w_raw[:, n, W1:], w_hi[:, n, W1:],
                                  ALU.subtract).then_inc(S["w2_lo"], 1)

            def x_lo_(i, n, turn):
                dve.wait_ge(S["x_hi"], i + 1)
                dve.tensor_tensor(x_lo[:, n], tx_ps[n][:], x_hi[:, n], ALU.subtract).then_inc(S["x_lo"], 1)

            def h_lo(i, n, turn):
                dve.wait_ge(S["h_hi"], i + 1)
                dve.tensor_tensor(ht_lo[:, n], th_ps[n][:], ht_hi[:, n], ALU.subtract).then_inc(S["h_lo"], 1)

            def o_copy(i, n, turn):
                dve.wait_ge(S["mm2"], i + 1)
                wait_for(dve, S[f"o_out{n}"], turn * 16)
                dve.tensor_copy(o_sb[:, n], o_ps[n][:]).then_inc(S["o_ready"], 1)

            software_pipeline(dve, RT, [(1, w2_lo), (0, w1_lo), (0, x_lo_), (2, o_copy), (1, h_lo)], 2)

        @block.tensor
        def _(pe):
            def turn_x(i, n, turn):
                pe.wait_ge(S[f"x_in{n}"], turn * 16 + 16)
                wait_for(pe, S["x_lo"], i - 1)
                for k in range(DC):
                    mm = pe.transpose(tx_ps[n][:, k], x[:, n, k * P:(k + 1) * P], ident[:])
                mm.then_inc(S["tx"], 1)

            def up(i, n, turn):
                pe.wait_ge(S["x_lo"], i + 1)
                pe.wait_ge(S["w1_lo"], i + 1)
                wait_for(pe, S["gelu"], i - 1)
                for k in range(DC):
                    c = slice(k * HR, (k + 1) * HR)
                    mm = product(pe, h_ps[n][:], (x_hi[:, n, k], x_lo[:, n, k]), (w_hi[:, n, c], w_lo[:, n, c]),
                                 k == 0, k == DC - 1)
                mm.then_inc(S["mm1"], 1)

            def turn_h(i, n, turn):
                pe.wait_ge(S["gelu"], i + 1)
                wait_for(pe, S["h_lo"], i - 1)
                for k in range(RC):
                    mm = pe.transpose(th_ps[n][:, k], h[:, n, k * P:(k + 1) * P], ident[:])
                mm.then_inc(S["th"], 1)

            def down(i, n, turn):
                pe.wait_ge(S["h_lo"], i + 1)
                pe.wait_ge(S["w2_lo"], i + 1)
                wait_for(pe, S["o_ready"], i - 1)
                for k in range(RC):
                    c = slice(W1 + k * D, W1 + (k + 1) * D)
                    mm = product(pe, o_ps[n][:], (ht_hi[:, n, k], ht_lo[:, n, k]), (w_hi[:, n, c], w_lo[:, n, c]),
                                 k == 0, k == RC - 1)
                mm.then_inc(S["mm2"], 1)

            software_pipeline(pe, RT, [(1, up), (0, turn_x), (2, down), (1, turn_h)], 2)



def stage_choose(nc, ins, d, keep):
    with ExitStack() as ctx:
        sb = lambda n, s, t=FP32: ctx.enter_context(nc.sbuf_tensor("s3_" + n, s, t))
        ps = lambda n, s, t=FP32: ctx.enter_context(nc.psum_tensor("s3_" + n, s, t))
        S = sems(nc, ctx, "s3_", "y_ready rec_in params_in ~rows_in dve turned turned_read nav nav_gelu logits shifted prob_e "
                 "key key_turned")
        ident = keep["ident"]
        order = keep["order"]
        rec = sb("rec", [NB, REC], I32)
        rec_f = rec[:].bitcast(FP32)
        shared = sb("shared", [NB, D])
        routed = [sb(f"routed{n}", [NB, D]) for n in range(2)]
        y = sb("y", [NB, D])
        y_t = sb("y_t", [P, DC, NB])
        wp1 = sb("wp1", [P, DC, P])
        wp2 = sb("wp2", [P, ER])
        bp1 = sb("bp1", [P, 1])
        bp2 = sb("bp2", [NB, ER])
        nav = sb("nav", [P, NB])
        number = sb("number", [NB, ER])
        batch_no = sb("batch_no", [NB, 1])
        v = sb("v", [NB, 4, ER])
        c = sb("c", [NB, 6])
        keys = sb("keys", [1, 2, NB])
        best = sb("best", [1, NB])
        key_i = sb("key_i", [1, 3, NB], I32)
        turned_ps = ps("turned", [P, DC, NB])
        nav_ps = ps("nav_ps", [P, NB])
        logit_ps = ps("logits_ps", [NB, ER])
        key_ps = ps("key_ps", [1, NB])

        block = ctx.enter_context(nc.Block())

        @block.sync
        def _(sp):
            sp.dma_start(rec[:], d["rec"][:, P - 1, :]).then_inc(S["rec_in"], 16)
            sp.dma_start(shared[:], d["shared"][:, P - 1, :]).then_inc(S["params_in"], 16)
            for dst, src in ((wp1[:], ins["wp1"]), (wp2[:], ins["wp2"]), (bp1[:], ins["bp1"]),
                             (bp2[:], ins["bp2"].partition_broadcast(NB)), (number[:], ins["c_eight"]),
                             (batch_no[:], ins["c_batch"])):
                sp.dma_start(dst, src).then_inc(S["params_in"], 16)

        @block.gpsimd
        def _(pool):
            pool.wait_ge(S["rec_in"], 16)
            for n, slot in enumerate((SLOT1, SLOT2)):
                pool.indirect_dma_start(routed[n][:], None, d["routed"],
                                        bass.IndirectOffsetOnAxis(rec[:, slot:slot + 1].bitcast(U32), 0)
                                        ).then_inc(S["rows_in"], 16)

        @block.scalar
        def _(act):
            act.wait_ge(S["nav"], 1)
            act.activation(nav[:], nav_ps[:], ACT.Gelu, bias=bp1[:]).then_inc(S["nav_gelu"], 1)
            act.wait_ge(S["shifted"], 1)
            act.activation(v[:, 1], v[:, 0], ACT.Exp, accum_out=c[:, 1:2]).then_inc(S["prob_e"], 1)

        @block.vector
        def _(dve):
            done = [0]

            def op(ins_):
                done[0] += 1
                ins_.then_inc(S["dve"], 1)
                dve.wait_ge(S["dve"], done[0])

            def signal(ins_, name):
                ins_.then_inc(S[name], 1)
                dve.wait_ge(S[name], 1)

            dve.wait_ge(S["params_in"], 16 * 7)
            dve.wait_ge(S["rows_in"], 32)
            op(dve.scalar_tensor_tensor(y[:], routed[0][:], rec_f[:, GATE1:GATE1 + 1], shared[:], ALU.mult, ALU.add))
            signal(dve.scalar_tensor_tensor(y[:], routed[1][:], rec_f[:, GATE2:GATE2 + 1], y[:], ALU.mult, ALU.add),
                   "y_ready")
            dve.wait_ge(S["turned"], 1)
            signal(dve.tensor_copy(y_t[:], turned_ps[:]), "turned_read")
            dve.wait_ge(S["logits"], 1)
            op(dve.tensor_tensor(v[:, 2], logit_ps[:], bp2[:], ALU.add))
            op(dve.tensor_reduce(c[:, 0:1], v[:, 2], AX, ALU.max))
            signal(dve.tensor_scalar(v[:, 0], v[:, 2], c[:, 0:1], None, ALU.subtract), "shifted")
            dve.wait_ge(S["prob_e"], 1)
            op(dve.reciprocal(c[:, 2:3], c[:, 1:2]))
            op(dve.tensor_scalar(v[:, 3], v[:, 1], c[:, 2:3], None, ALU.mult))
            op(dve.tensor_reduce(c[:, 3:4], v[:, 3], AX, ALU.max))
            op(dve.tensor_scalar(v[:, 2], v[:, 3], c[:, 3:4], float(ER), ALU.is_lt, ALU.mult))
            op(dve.tensor_tensor(v[:, 2], v[:, 2], number[:], ALU.add))
            op(dve.tensor_reduce(c[:, 4:5], v[:, 2], AX, ALU.min))
            signal(dve.scalar_tensor_tensor(c[:, 5:6], c[:, 4:5], float(NB), batch_no[:], ALU.mult, ALU.add), "key")
            dve.wait_ge(S["key_turned"], 1)
            op(dve.tensor_copy(keys[:, 0], key_ps[:]))
            for r in range(NB // 8):
                eight = best[:, 8 * r:8 * r + 8]
                op(dve.max(eight, keys[:, r % 2]))
                if r < NB // 8 - 1:
                    op(dve.match_replace(keys[:, 1 - r % 2], eight, keys[:, r % 2], -1.0))
            op(dve.tensor_copy(key_i[:, 0], best[:]))
            op(dve.tensor_scalar(order[:, 0], key_i[:, 0], 5, None, ALU.arith_shift_right))
            op(dve.tensor_scalar(order[:, 1], key_i[:, 0], NB - 1, None, ALU.bitwise_and))
            op(dve.memset(order[:, 2], 1))
            op(dve.tensor_tensor(order[:, 2, 1:NB], order[:, 0, 1:NB], order[:, 0, 0:NB - 1], ALU.not_equal))

        @block.tensor
        def _(pe):
            pe.wait_ge(S["y_ready"], 1)
            for k in range(DC):
                mm = pe.transpose(turned_ps[:, k], y[:, k * P:(k + 1) * P], ident[0:NB, 0:NB])
            mm.then_inc(S["turned"], 1)
            pe.wait_ge(S["turned_read"], 1)
            for k in range(DC):
                mm = pe.matmul(nav_ps[:], wp1[:, k], y_t[:, k], start=(k == 0), stop=(k == DC - 1))
            mm.then_inc(S["nav"], 1)
            pe.wait_ge(S["nav_gelu"], 1)
            pe.matmul(logit_ps[:], nav[:], wp2[:], start=True, stop=True).then_inc(S["logits"], 1)
            pe.wait_ge(S["key"], 1)
            pe.transpose(key_ps[:], c[:, 5:6], ident[0:NB, 0:NB]).then_inc(S["key_turned"], 1)



def stage_ffn(nc, ins, d, keep):
    with ExitStack() as ctx:
        sb = lambda n, s, t=FP32: ctx.enter_context(nc.sbuf_tensor("s4_" + n, s, t))
        ps = lambda n, s, t=FP32: ctx.enter_context(nc.psum_tensor("s4_" + n, s, t))
        S = sems(nc, ctx, "s4_", "params_in rec_in hrec_in shared_in x_in ~routed1_in ~routed2_in b1_in b2_in w1_in "
                 "w2_in wo_hi wo_lo w1_hi w1_lo w2_hi w2_lo part_y y base x_plus_y bo_scaled ty y_hi y_lo h_ps h_add gelu th h_hi "
                 "h_lo mm2 z_add tz z_hi z_lo mmo x1_part x1 x1_out prev_in dx k_part xk r_part xr ~xk_sent txr xr_hi "
                 "xr_lo mmr r_ready r_out")
        ident = keep["ident"]
        order = keep["order"]
        rec = sb("rec", [P, REC], I32)
        rec_f = rec[:].bitcast(FP32)
        hrec = sb("hrec", [P, REC], I32)
        shared = sb("shared", [P, D])
        x = sb("x", [P, D])
        routed = [sb(f"routed{n}", [P, D]) for n in range(2)]
        y_part = sb("y_part", [P, D])
        y = sb("y", [P, D])
        base_part = sb("base_part", [P, D])
        base = sb("base", [P, 2, D])
        b1 = sb("b1", [P, HS])
        b2 = sb("b2", [P, D])
        bo = sb("bo", [P, D])
        maa_k = sb("maa_k", [P, D])
        maa_r = sb("maa_r", [P, D])
        w1_raw = sb("w1_raw", [P, DC, HS])
        w2_raw = sb("w2_raw", [P, DC, HS])
        w1_hi = sb("w1_hi", [P, DC, HS], FP32R)
        w1_lo = sb("w1_lo", [P, DC, HS], FP32R)
        w2_hi = sb("w2_hi", [P, DC, HS], FP32R)
        w2_lo = sb("w2_lo", [P, DC, HS], FP32R)
        wo_hi = sb("wo_hi", [P, 2, DC, D], FP32R)
        wo_lo = sb("wo_lo", [P, 2, DC, D], FP32R)
        y_hi = sb("y_hi", [P, DC, P], FP32R)
        y_lo = sb("y_lo", [P, DC, P], FP32R)
        h_pre = sb("h_pre", [P, 2, D])
        h = sb("h", [P, 2, D])
        ht_hi = sb("ht_hi", [P, HC, P], FP32R)
        ht_lo = sb("ht_lo", [P, HC, P], FP32R)
        z = sb("z", [P, D])
        z_hi = sb("z_hi", [P, DC, P], FP32R)
        z_lo = sb("z_lo", [P, DC, P], FP32R)
        x1 = sb("x1", [P, D])
        prev = sb("prev", [P, D])
        dx = sb("dx", [P, D])
        k_part = sb("k_part", [P, D])
        xk = sb("xk", [P, D])
        xr = sb("xr", [P, D])
        xr_hi = sb("xr_hi", [P, DC, P], FP32R)
        xr_lo = sb("xr_lo", [P, DC, P], FP32R)
        r = sb("r", [P, D])
        h_ps = [ps(f"h_ps{n}", [P, D]) for n in range(2)]
        th_ps = [ps(f"th_ps{n}", [P, DC, P]) for n in range(2)]
        ty_ps = ps("ty_ps", [P, DC, P])
        tz_ps = ps("tz_ps", [P, DC, P])
        out_ps = ps("out_ps", [P, D])
        r_ps = ps("r_ps", [P, D])
        wo_raw = [w1_raw, w2_raw]

        block = ctx.enter_context(nc.Block())
        w2_chunk = lambda w, k: w[:, k // 2, (k % 2) * D:(k % 2 + 1) * D]

        @block.sync
        def _(sp):
            sp.dma_start(wo_raw[0][:, 0:2, :], ins["wo"]).then_inc(S["params_in"], 16)
            sp.dma_start(wo_raw[1][:, 0:2, :], ins["w_recept"]).then_inc(S["params_in"], 16)
            for dst, src in ((bo, "bo"), (maa_k, "maa_k"), (maa_r, "maa_r")):
                sp.dma_start(dst[:], ins[src].partition_broadcast(P)).then_inc(S["params_in"], 16)
            sp.dma_start(d["x1"][:, 0, :], ins["cond"]).then_inc(S["params_in"], 16)

            def batch(i):
                return sp.value_load(order[0:1, 1, bass.ds(i, 1)], min_val=0, max_val=NB - 1)

            def expert(i):
                return sp.value_load(order[0:1, 0, bass.ds(i, 1)], min_val=0, max_val=ER - 1)

            def is_new(i):
                return sp.value_load(order[0:1, 2, bass.ds(i, 1)], min_val=0, max_val=1) > 0

            def load_rows(i):
                b = batch(i)
                wait_for(sp, S["y"], i)
                sp.dma_start(rec[:], d["rec"][b]).then_inc(S["rec_in"], 16)
                sp.dma_start(shared[:], d["shared"][b]).then_inc(S["shared_in"], 16)
                wait_for(sp, S["base"], i)
                sp.dma_start(x[:], ins["x_rows"].rearrange("(b p) n -> b p n", p=P)[b]).then_inc(S["x_in"], 16)

            def load_w1(i):
                e, new = expert(i), is_new(i)
                if isinstance(i, int) and i == 0:
                    sp.wait_ge(S["wo_lo"], 2)
                wait_apart(sp, S["w1_lo"], i * DC)
                sp.dma_start(w1_raw[:], ins["w1"][e], cond=new).then_inc(S["w1_in"], 16)

            def load_w2(i):
                e, new = expert(i), is_new(i)
                wait_apart(sp, S["w2_lo"], i * DC)
                sp.dma_start(w2_raw[:], ins["w2"][e], cond=new).then_inc(S["w2_in"], 16)
                wait_for(sp, S["h_add"], 2 * i)
                sp.dma_start(b1[:], ins["b1"][e].partition_broadcast(P)).then_inc(S["b1_in"], 16)

            def load_b2(i):
                e = expert(i)
                wait_for(sp, S["z_add"], i)
                sp.dma_start(b2[:], ins["b2"][e].partition_broadcast(P)).then_inc(S["b2_in"], 16)

            def store_x1(i):
                b = batch(i)
                sp.wait_ge(S["x1"], i + 1)
                sp.dma_start(d["x1"][b, 1:P + 1], x1[:]).then_inc(S["x1_out"], 16)
                wait_for(sp, S["xk_sent"], i * 16)
                sp.dma_start(hrec[:], d["rec"][b]).then_inc(S["hrec_in"], 16)
                wait_apart(sp, S["dx"], i)
                if isinstance(i, int) and i == 0:
                    sp.wait_ge(S["params_in"], 96)
                wait_apart(sp, S["x1_out"], i * 16 + 16)
                sp.dma_start(prev[:], d["x1"][b, 0:P]).then_inc(S["prev_in"], 16)

            def store_r(i):
                b = batch(i)
                sp.wait_ge(S["r_ready"], i + 1)
                sp.dma_start(d["r"][b], r[:]).then_inc(S["r_out"], 16)

            software_pipeline(sp, NB, [(1, load_b2), (0, load_w1), (0, load_rows), (0, load_w2), (2, store_x1),
                                       (3, store_r)])
            sp.wait_ge(S["r_out"], 16 * NB)

        @block.gpsimd
        def _(pool):
            def gather(i):
                pool.wait_ge(S["rec_in"], i * 16 + 16)
                for n, slot in enumerate((SLOT1, SLOT2)):
                    wait_apart(pool, S[("part_y", "y")[n]], i)
                    pool.indirect_dma_start(routed[n][:], None, d["routed"],
                                            bass.IndirectOffsetOnAxis(rec[:, slot:slot + 1].bitcast(U32), 0)
                                            ).then_inc(S[f"routed{n + 1}_in"], 16)

            def add_base(i):
                pool.wait_ge(S["x_in"], i * 16 + 16)
                pool.wait_ge(S["y"], i + 1)
                pool.tensor_tensor(base_part[:], x[:], y[:], ALU.add).then_inc(S["x_plus_y"], 1)
                pool.wait_ge(S["x_plus_y"], i + 1)
                wait_for(pool, S["x1"], i - 1)
                pool.tensor_tensor(base[:, i % 2], base_part[:], bo[:], ALU.add).then_inc(S["base"], 1)

            def mix(i):
                pool.wait_ge(S["prev_in"], i * 16 + 16)
                pool.tensor_tensor(dx[:], prev[:], x1[:], ALU.subtract).then_inc(S["dx"], 1)
                pool.wait_ge(S["dx"], i + 1)
                pool.tensor_tensor(k_part[:], dx[:], maa_r[:], ALU.mult).then_inc(S["r_part"], 1)
                pool.wait_ge(S["r_part"], i + 1)
                wait_for(pool, S["txr"], i)
                pool.tensor_tensor(xr[:], k_part[:], x1[:], ALU.add).then_inc(S["xr"], 1)
                pool.wait_ge(S["xr"], i + 1)
                pool.tensor_tensor(k_part[:], dx[:], maa_k[:], ALU.mult).then_inc(S["k_part"], 1)
                pool.wait_ge(S["k_part"], i + 1)
                wait_for(pool, S["xk_sent"], i * 16)
                pool.tensor_tensor(xk[:], k_part[:], x1[:], ALU.add).then_inc(S["xk"], 1)
                pool.wait_ge(S["hrec_in"], i * 16 + 16)
                wait_apart(pool, S["xk"], i + 1)
                pool.indirect_dma_start(d["hash_in"], bass.IndirectOffsetOnAxis(hrec[:, SLOTH:SLOTH + 1].bitcast(U32), 0),
                                        xk[:], None, bounds_check=NTOK - 1, oob_is_err=False).then_inc(S["xk_sent"], 16)

            pool.wait_ge(S["params_in"], 96)
            pool.tensor_scalar(bo[:], bo[:], 0.3, None, ALU.mult).then_inc(S["bo_scaled"], 1)
            pool.wait_ge(S["bo_scaled"], 1)
            software_pipeline(pool, NB, [(0, gather), (2, mix), (0, add_base)])
            pool.wait_ge(S["xk_sent"], 16 * NB)

        @block.scalar
        def _(act):
            for n in range(2):
                act.wait_ge(S["params_in"], 96)
                act.activation(wo_hi[:, n].rearrange("p k n -> p (k n)"),
                               wo_raw[n][:, 0:2].rearrange("p k n -> p (k n)"), ACT.Copy).then_inc(S["wo_hi"], 1)

            def split_w(name, raw, hi, mm, per, c0, c1):
                def stage(i):
                    if c0 == 0:
                        act.wait_ge(S[name + "_in"], i * 16 + 16)
                        wait_for(act, S[mm], i * per)
                    for c in range(c0, c1):
                        act.activation(hi[:, c], raw[:, c], ACT.Copy).then_inc(S[name + "_hi"], 1)
                return stage

            def gelu(n):
                def stage(i):
                    act.wait_ge(S["h_add"], 2 * i + n + 1)
                    wait_for(act, S["th"], 2 * i + n - 1)
                    act.activation(h[:, n], h_pre[:, n], ACT.Gelu).then_inc(S["gelu"], 1)
                return stage

            def h_hi(n):
                def stage(i):
                    act.wait_ge(S["th"], 2 * i + n + 1)
                    wait_for(act, S["mm2"], i)
                    act.activation(ht_hi[:, n * DC:(n + 1) * DC], th_ps[n][:], ACT.Copy).then_inc(S["h_hi"], 1)
                return stage

            def part_hi(dst, src, turned, used, name):
                def stage(i):
                    act.wait_ge(S[turned], i + 1)
                    wait_for(act, S[used], i if used != "h_ps" else 2 * i)
                    act.activation(dst[:], src[:], ACT.Copy).then_inc(S[name], 1)
                return stage

            def copy_r(i):
                act.wait_ge(S["mmr"], i + 1)
                wait_for(act, S["r_out"], i * 16)
                act.activation(r[:], r_ps[:], ACT.Copy).then_inc(S["r_ready"], 1)

            w1 = lambda c0, c1: split_w("w1", w1_raw, w1_hi, "h_ps", 2, c0, c1)
            w2 = lambda c0, c1: split_w("w2", w2_raw, w2_hi, "mm2", 1, c0, c1)
            software_pipeline(act, NB, [
                (1, w2(0, 2)), (1, gelu(0)), (2, part_hi(z_hi, tz_ps, "tz", "mmo", "z_hi")), (1, gelu(1)),
                (1, w2(2, 3)), (1, h_hi(0)), (3, part_hi(xr_hi, ty_ps, "txr", "mmr", "xr_hi")), (1, w2(3, 4)),
                (1, h_hi(1)), (0, w1(0, 2)), (0, part_hi(y_hi, ty_ps, "ty", "h_ps", "y_hi")), (0, w1(2, 4)),
                (3, copy_r)])

        @block.vector
        def _(dve):
            for n in range(2):
                dve.wait_ge(S["wo_hi"], n + 1)
                dve.tensor_tensor(wo_lo[:, n].rearrange("p k n -> p (k n)"),
                                  wo_raw[n][:, 0:2].rearrange("p k n -> p (k n)"),
                                  wo_hi[:, n].rearrange("p k n -> p (k n)"), ALU.subtract).then_inc(S["wo_lo"], 1)

            def split_w(name, raw, hi, lo, c0, c1):
                def stage(i):
                    for c in range(c0, c1):
                        dve.wait_ge(S[name + "_hi"], i * DC + c + 1)
                        dve.tensor_tensor(lo[:, c], raw[:, c], hi[:, c], ALU.subtract).then_inc(S[name + "_lo"], 1)
                return stage

            def h_add(n):
                def stage(i):
                    dve.wait_ge(S["h_ps"], 2 * i + n + 1)
                    if n == 0:
                        dve.wait_ge(S["b1_in"], i * 16 + 16)
                    wait_for(dve, S["gelu"], 2 * i + n - 1)
                    dve.tensor_tensor(h_pre[:, n], h_ps[n][:], b1[:, n * D:(n + 1) * D],
                                      ALU.add).then_inc(S["h_add"], 1)
                return stage

            def h_lo(n):
                def stage(i):
                    dve.wait_ge(S["h_hi"], 2 * i + n + 1)
                    dve.tensor_tensor(ht_lo[:, n * DC:(n + 1) * DC], th_ps[n][:], ht_hi[:, n * DC:(n + 1) * DC],
                                      ALU.subtract).then_inc(S["h_lo"], 1)
                return stage

            def part_lo(dst, src, hi, hi_done, name):
                def stage(i):
                    dve.wait_ge(S[hi_done], i + 1)
                    dve.tensor_tensor(dst[:], src[:], hi[:], ALU.subtract).then_inc(S[name], 1)
                return stage

            def z_add(i):
                dve.wait_ge(S["mm2"], i + 1)
                dve.wait_ge(S["b2_in"], i * 16 + 16)
                wait_for(dve, S["tz"], i)
                dve.tensor_tensor(z[:], out_ps[:], b2[:], ALU.add).then_inc(S["z_add"], 1)

            def x1_(i):
                dve.wait_ge(S["mmo"], i + 1)
                dve.wait_ge(S["base"], i + 1)
                wait_for(dve, S["xk"], i)
                wait_for(dve, S["x1_out"], i * 16)
                dve.scalar_tensor_tensor(x1[:], out_ps[:], 0.3, base[:, i % 2], ALU.mult, ALU.add).then_inc(S["x1"], 1)

            def combine(i):
                dve.wait_ge(S["rec_in"], i * 16 + 16)
                dve.wait_ge(S["shared_in"], i * 16 + 16)
                dve.wait_ge(S["routed1_in"], i * 16 + 16)
                dve.scalar_tensor_tensor(y_part[:], routed[0][:], rec_f[:, GATE1:GATE1 + 1], shared[:],
                                         ALU.mult, ALU.add).then_inc(S["part_y"], 1)
                dve.wait_ge(S["part_y"], i + 1)
                dve.wait_ge(S["routed2_in"], i * 16 + 16)
                wait_for(dve, S["ty"], i)
                wait_for(dve, S["x_plus_y"], i)
                dve.scalar_tensor_tensor(y[:], routed[1][:], rec_f[:, GATE2:GATE2 + 1], y_part[:],
                                         ALU.mult, ALU.add).then_inc(S["y"], 1)

            w1 = lambda c0, c1: split_w("w1", w1_raw, w1_hi, w1_lo, c0, c1)
            w2 = lambda c0, c1: split_w("w2", w2_raw, w2_hi, w2_lo, c0, c1)
            software_pipeline(dve, NB, [
                (1, w2(0, 2)), (1, h_add(0)), (2, part_lo(z_lo, tz_ps, z_hi, "z_hi", "z_lo")), (1, h_add(1)),
                (1, w2(2, 3)), (1, h_lo(0)), (3, part_lo(xr_lo, ty_ps, xr_hi, "xr_hi", "xr_lo")), (1, w2(3, 4)),
                (0, combine), (2, x1_), (1, h_lo(1)), (0, w1(0, 2)), (0, part_lo(y_lo, ty_ps, y_hi, "y_hi", "y_lo")),
                (0, w1(2, 4)), (1, z_add)])

        @block.tensor
        def _(pe):
            def up(n):
                def stage(i):
                    if n == 0:
                        pe.wait_ge(S["y_lo"], i + 1)
                        pe.wait_ge(S["w1_lo"], i * DC + DC)
                    wait_for(pe, S["h_add"], 2 * i + n - 1)
                    for k in range(DC):
                        mm = product(pe, h_ps[n][:], (y_hi[:, k], y_lo[:, k]),
                                     (w1_hi[:, k, n * D:(n + 1) * D], w1_lo[:, k, n * D:(n + 1) * D]),
                                     k == 0, k == DC - 1)
                    mm.then_inc(S["h_ps"], 1)
                return stage

            def turn_h(n):
                def stage(i):
                    pe.wait_ge(S["gelu"], 2 * i + n + 1)
                    wait_for(pe, S["h_lo"], 2 * i + n - 1)
                    for k in range(DC):
                        mm = pe.transpose(th_ps[n][:, k], h[:, n, k * P:(k + 1) * P], ident[:])
                    mm.then_inc(S["th"], 1)
                return stage

            def turn(src, ready, dst, free, free_lag, name):
                def stage(i):
                    pe.wait_ge(S[ready], i + 1)
                    wait_for(pe, S[free], min(i - free_lag, NB) if isinstance(i, int) else i - free_lag)
                    for k in range(DC):
                        mm = pe.transpose(dst[:, k], src[:, k * P:(k + 1) * P], ident[:])
                    mm.then_inc(S[name], 1)
                return stage

            def down(i):
                pe.wait_ge(S["h_lo"], 2 * i + 2)
                pe.wait_ge(S["w2_lo"], i * DC + DC)
                wait_for(pe, S["x1"], i)
                for k in range(HC):
                    mm = product(pe, out_ps[:], (ht_hi[:, k], ht_lo[:, k]), (w2_chunk(w2_hi, k), w2_chunk(w2_lo, k)),
                                 k == 0, k == HC - 1)
                mm.then_inc(S["mm2"], 1)

            def square(n, parts, ready, dst, free, name):
                def stage(i):
                    pe.wait_ge(S[ready], i + 1)
                    if n == 0:
                        pe.wait_ge(S["z_add"], i + 1)
                    wait_for(pe, S[free], i)
                    for k in range(DC):
                        mm = product(pe, dst[:], (parts[0][:, k], parts[1][:, k]), (wo_hi[:, n, k], wo_lo[:, n, k]),
                                     k == 0, k == DC - 1)
                    mm.then_inc(S[name], 1)
                return stage

            pe.wait_ge(S["wo_lo"], 2)
            software_pipeline(pe, NB, [
                (1, up(0)), (2, turn(z, "z_add", tz_ps, "z_lo", 0, "tz")), (1, up(1)),
                (3, turn(xr, "xr", ty_ps, "y_lo", -3, "txr")), (1, turn_h(0)),
                (2, square(0, (z_hi, z_lo), "z_lo", out_ps, "x1", "mmo")), (1, turn_h(1)),
                (3, square(1, (xr_hi, xr_lo), "xr_lo", r_ps, "r_ready", "mmr")),
                (0, turn(y, "y", ty_ps, "xr_lo", 2, "ty")), (1, down)])



def stage_hashed(nc, ins, d, keep):
    with ExitStack() as ctx:
        sb = lambda n, s, t=FP32: ctx.enter_context(nc.sbuf_tensor("s5_" + n, s, t))
        ps = lambda n, s, t=FP32: ctx.enter_context(nc.psum_tensor("s5_" + n, s, t))
        S = sems(nc, ctx, "s5_", "x_in0 x_in1 w1_in w2_in w1_hi w1_lo w2_hi w2_lo tx0 tx1 x_hi0 x_hi1 x_lo0 x_lo1 "
                 "h_ps pos relu th h_hi h_lo mm2 o_ready0 o_ready1 o_out0 o_out1")
        ident = keep["ident"]
        w1_raw = sb("w1_raw", [P, DC, HS])
        w2_raw = sb("w2_raw", [P, DC, HS])
        w1_hi = sb("w1_hi", [P, DC, HS], FP32R)
        w1_lo = sb("w1_lo", [P, DC, HS], FP32R)
        w2_hi = sb("w2_hi", [P, DC, HS], FP32R)
        w2_lo = sb("w2_lo", [P, DC, HS], FP32R)
        x = sb("x", [P, 2, D])
        x_hi = sb("x_hi", [P, 2, DC, P], FP32R)
        x_lo = sb("x_lo", [P, 2, DC, P], FP32R)
        pos = sb("pos", [P, 2, D])
        h = sb("h", [P, 2, 2, D])
        ht_hi = sb("ht_hi", [P, 2, HC, P], FP32R)
        ht_lo = sb("ht_lo", [P, 2, HC, P], FP32R)
        o_sb = sb("o_sb", [P, 2, D])
        h_ps = [ps(f"h_ps{n}", [P, D]) for n in range(2)]
        th_ps = [ps(f"th_ps{n}", [P, DC, P]) for n in range(2)]
        tx_ps = [ps(f"tx_ps{n}", [P, DC, P]) for n in range(2)]
        o_ps = [ps(f"o_ps{n}", [P, D]) for n in range(2)]
        w2_chunk = lambda w, k: w[:, k // 2, (k % 2) * D:(k % 2 + 1) * D]

        block = ctx.enter_context(nc.Block())

        @block.sync
        def _(sp):
            def load_x(m):
                def stage(e):
                    wait_for(sp, S[f"tx{m}"], e)
                    sp.dma_start(x[:, m], d["hash_in"][bass.ds(e * CAP + m * P, P)]).then_inc(S[f"x_in{m}"], 16)
                return stage

            def load_w(name, raw):
                def stage(e):
                    wait_for(sp, S[name + "_lo"], e * DC)
                    sp.dma_start(raw[:], ins[name + "h"][e]).then_inc(S[name + "_in"], 16)
                return stage

            def store(m):
                def stage(e):
                    sp.wait_ge(S[f"o_ready{m}"], e + 1)
                    sp.dma_start(d["hash_out"][bass.ds(e * CAP + m * P, P)], o_sb[:, m]).then_inc(S[f"o_out{m}"], 16)
                return stage

            software_pipeline(sp, EH, [(0, load_w("w1", w1_raw)), (0, load_x(0)), (0, load_x(1)), (2, store(1)),
                                       (0, load_w("w2", w2_raw)), (1, store(0))])
            for m in range(2):
                sp.wait_ge(S[f"o_out{m}"], 16 * EH)

        @block.scalar
        def _(act):
            def split_w(name, raw, hi, used, per, c0, c1):
                def stage(e):
                    if c0 == 0:
                        act.wait_ge(S[name + "_in"], e * 16 + 16)
                        wait_for(act, S[used], e * per)
                    for c in range(c0, c1):
                        act.activation(hi[:, c], raw[:, c], ACT.Copy).then_inc(S[name + "_hi"], 1)
                return stage

            def x_hi_(m):
                def stage(e):
                    act.wait_ge(S[f"tx{m}"], e + 1)
                    wait_for(act, S["h_ps"], 4 * e - 2 + 2 * m)
                    act.activation(x_hi[:, m], tx_ps[m][:], ACT.Copy).then_inc(S[f"x_hi{m}"], 1)
                return stage

            def h_hi(m, n):
                def stage(e):
                    act.wait_ge(S["th"], 4 * e + 2 * m + n + 1)
                    wait_for(act, S["mm2"], 2 * e + m - 1)
                    act.activation(ht_hi[:, m, n * DC:(n + 1) * DC], th_ps[n][:], ACT.Copy).then_inc(S["h_hi"], 1)
                return stage

            def relu(m, n):
                def stage(e):
                    t = 4 * e + 2 * m + n
                    act.wait_ge(S["h_ps"], t + 1)
                    wait_for(act, S["relu"], t - 1)
                    act.activation(pos[:, n], h_ps[n][:], ACT.Relu).then_inc(S["pos"], 1)
                return stage

            def out(m):
                def stage(e):
                    act.wait_ge(S["mm2"], 2 * e + m + 1)
                    wait_for(act, S[f"o_out{m}"], e * 16)
                    act.activation(o_sb[:, m], o_ps[m][:], ACT.Copy).then_inc(S[f"o_ready{m}"], 1)
                return stage

            w1 = lambda c0, c1: split_w("w1", w1_raw, w1_hi, "h_ps", 4, c0, c1)
            w2 = lambda c0, c1: split_w("w2", w2_raw, w2_hi, "mm2", 2, c0, c1)
            software_pipeline(act, EH, [
                (2, out(1)), (1, w2(0, 2)), (1, relu(0, 0)), (1, w2(2, 3)), (1, relu(0, 1)), (1, w2(3, 4)),
                (1, relu(1, 0)), (1, h_hi(0, 0)), (1, h_hi(0, 1)), (1, relu(1, 1)), (0, x_hi_(0)), (1, h_hi(1, 0)),
                (0, w1(0, 4)), (1, out(0)), (1, h_hi(1, 1)), (0, x_hi_(1))])

        @block.vector
        def _(dve):
            def split_w(name, raw, hi, lo, c0, c1):
                def stage(e):
                    for c in range(c0, c1):
                        dve.wait_ge(S[name + "_hi"], e * DC + c + 1)
                        dve.tensor_tensor(lo[:, c], raw[:, c], hi[:, c], ALU.subtract).then_inc(S[name + "_lo"], 1)
                return stage

            def relu2(m, n):
                def stage(e):
                    t = 4 * e + 2 * m + n
                    dve.wait_ge(S["pos"], t + 1)
                    wait_for(dve, S["th"], t - 3)
                    dve.tensor_tensor(h[:, m, n], pos[:, n], h_ps[n][:], ALU.mult).then_inc(S["relu"], 1)
                return stage

            def h_lo(m, n):
                def stage(e):
                    dve.wait_ge(S["h_hi"], 4 * e + 2 * m + n + 1)
                    dve.tensor_tensor(ht_lo[:, m, n * DC:(n + 1) * DC], th_ps[n][:], ht_hi[:, m, n * DC:(n + 1) * DC],
                                      ALU.subtract).then_inc(S["h_lo"], 1)
                return stage

            def x_lo_(m):
                def stage(e):
                    dve.wait_ge(S[f"x_hi{m}"], e + 1)
                    dve.tensor_tensor(x_lo[:, m], tx_ps[m][:], x_hi[:, m], ALU.subtract).then_inc(S[f"x_lo{m}"], 1)
                return stage

            w1 = lambda c0, c1: split_w("w1", w1_raw, w1_hi, w1_lo, c0, c1)
            w2 = lambda c0, c1: split_w("w2", w2_raw, w2_hi, w2_lo, c0, c1)
            software_pipeline(dve, EH, [
                (1, w2(0, 2)), (1, relu2(0, 0)), (1, w2(2, 3)), (1, relu2(0, 1)), (1, w2(3, 4)), (1, relu2(1, 0)),
                (1, h_lo(0, 0)), (1, h_lo(0, 1)), (1, relu2(1, 1)), (0, x_lo_(0)), (1, h_lo(1, 0)), (0, w1(0, 4)),
                (1, h_lo(1, 1)), (0, x_lo_(1))])

        @block.tensor
        def _(pe):
            def turn_x(m):
                def stage(e):
                    pe.wait_ge(S[f"x_in{m}"], e * 16 + 16)
                    wait_for(pe, S[f"x_lo{m}"], e)
                    for k in range(DC):
                        mm = pe.transpose(tx_ps[m][:, k], x[:, m, k * P:(k + 1) * P], ident[:])
                    mm.then_inc(S[f"tx{m}"], 1)
                return stage

            def up(m, n):
                def stage(e):
                    if n == 0:
                        pe.wait_ge(S[f"x_lo{m}"], e + 1)
                        pe.wait_ge(S["w1_lo"], e * DC + DC)
                    wait_for(pe, S["relu"], 4 * e + 2 * m + n - 1)
                    for k in range(DC):
                        mm = product(pe, h_ps[n][:], (x_hi[:, m, k], x_lo[:, m, k]),
                                     (w1_hi[:, k, n * D:(n + 1) * D], w1_lo[:, k, n * D:(n + 1) * D]),
                                     k == 0, k == DC - 1)
                    mm.then_inc(S["h_ps"], 1)
                return stage

            def turn_h(m, n):
                def stage(e):
                    t = 4 * e + 2 * m + n
                    pe.wait_ge(S["relu"], t + 1)
                    wait_for(pe, S["h_lo"], t - 1)
                    for k in range(DC):
                        mm = pe.transpose(th_ps[n][:, k], h[:, m, n, k * P:(k + 1) * P], ident[:])
                    mm.then_inc(S["th"], 1)
                return stage

            def down(m):
                def stage(e):
                    pe.wait_ge(S["w2_lo"], e * DC + DC)
                    wait_for(pe, S[f"o_ready{m}"], e)
                    for k in range(HC):
                        if k % DC == 0:
                            pe.wait_ge(S["h_lo"], 4 * e + 2 * m + k // DC + 1)
                        mm = product(pe, o_ps[m][:], (ht_hi[:, m, k], ht_lo[:, m, k]),
                                     (w2_chunk(w2_hi, k), w2_chunk(w2_lo, k)), k == 0, k == HC - 1)
                    mm.then_inc(S["mm2"], 1)
                return stage

            software_pipeline(pe, EH, [
                (1, up(0, 0)), (1, up(0, 1)), (1, up(1, 0)), (1, turn_h(0, 0)), (1, turn_h(0, 1)), (1, up(1, 1)),
                (0, turn_x(0)), (1, turn_h(1, 0)), (1, down(0)), (1, turn_h(1, 1)), (0, turn_x(1)), (1, down(1))])



def stage_recurrent(nc, ins, d, keep, out):
    with ExitStack() as ctx:
        sb = lambda n, s, t=FP32: ctx.enter_context(nc.sbuf_tensor("s6_" + n, s, t))
        ps = lambda n, s, t=FP32: ctx.enter_context(nc.psum_tensor("s6_" + n, s, t))
        S = sems(nc, ctx, "s6_", "params_in w_in0 w_in1 w_hi w_lo rec_in ~y_in r_in r_sig x2 tx x_raw x_hi x_lo xpart "
                 "gates added acted ig fc c tc c_hi c_lo uo_in ct_ready const_ps const "
                 "p_hi p_lo p_ps p_add p_tanh x1_in0 x1_in1 p_out out0 out1")
        NG = 3
        G_G, G_I, G_F = range(NG)
        ident = keep["ident"]
        NU = 4 * NG
        w_hi = sb("w_hi", [P, 2 * NG, DC, D], FP32R)
        w_lo = sb("w_lo", [P, 2 * NG, DC, D], FP32R)
        unit = lambda w, u: w[:].rearrange("p m k n -> p (m k n)")[:, u * HS:(u + 1) * HS] if isinstance(u, int) else \
            w[:].rearrange("p m k n -> p (m k n)")[:, bass.ds(u * HS, HS)]
        raw = sb("raw", [P, 2, HS])
        x2t = sb("x2t", [P, NB, DC, P])
        bias = sb("bias", [P, NG, D])
        bo = sb("bo", [P, D])
        gate = sb("gate", [P, NG, D])
        c = sb("c", [P, D])
        c_hi = sb("c_hi", [P, DC, P], FP32R)
        c_lo = sb("c_lo", [P, DC, P], FP32R)
        x_hi = sb("x_hi", [P, 2, DC, P], FP32R)
        x_lo = sb("x_lo", [P, 2, DC, P], FP32R)
        rec = sb("rec", [P, REC], I32)
        y = sb("y", [P, D])
        r = sb("r", [P, D])
        x2 = sb("x2", [P, D])
        ct = x2
        g_ps = [[ps(f"g{n}_{g}", [P, D]) for g in range(NG)] for n in range(2)]
        tx_ps = ps("tx_ps", [P, DC, P])
        tc_ps = ps("tc_ps", [P, DC, P])

        c_x1 = [gate[:, 0], gate[:, 1]]
        p_out = [r[:], y[:]]
        p_sum = [x2[:], gate[:, 2]]

        block = ctx.enter_context(nc.Block())

        @block.sync
        def _(sp):
            for g in range(NG):
                sp.dma_start(bias[:, g], ins["gate_bias"][g].partition_broadcast(P)).then_inc(S["params_in"], 16)
            sp.dma_start(bo[:], ins["bo_r"].partition_broadcast(P)).then_inc(S["params_in"], 16)
            sp.dma_start(c[:], ins["in_c"].partition_broadcast(P)).then_inc(S["params_in"], 16)

            def load_units(u2):
                for n in range(2):
                    wait_for(sp, S["w_lo"], u2 * 2 + n - 1)
                    sp.dma_start(raw[:, n], ins["gate_w"][u2 * 2 + n]).then_inc(S[f"w_in{n}"], 16)

            def load(i):
                wait_for(sp, S["x2"], i)
                sp.dma_start(rec[:], d["rec"][i]).then_inc(S["rec_in"], 16)
                sp.dma_start(r[:], d["r"][i]).then_inc(S["r_in"], 16)

            load_units(0)
            load(0)
            with sp.Fori(1, NU // 2) as u2:
                load_units(u2)
            with sp.Fori(1, NB) as i:
                load(i)
            load_units(NU // 2)
            sp.wait_ge(S["w_lo"], NU + 2)
            sp.dma_start(raw[:].rearrange("p u n -> p (u n)"), ins["uo"]).then_inc(S["uo_in"], 16)

            def load_x1(i, n, turn):
                wait_for(sp, S["p_out"], i - 1)
                sp.dma_start(c_x1[n], d["x1"][i, 1:P + 1]).then_inc(S[f"x1_in{n}"], 16)

            def store(i, n, turn):
                sp.wait_ge(S["p_out"], i + 1)
                sp.dma_start(out[i], p_out[n]).then_inc(S[f"out{n}"], 16)

            sp.wait_ge(S["const"], 1)
            software_pipeline(sp, NB, [(0, load_x1), (3, store)], 2)
            for n in range(2):
                sp.wait_ge(S[f"out{n}"], 16 * NB // 2)

        @block.gpsimd
        def _(pool):
            def fetch(i):
                pool.wait_ge(S["rec_in"], i * 16 + 16)
                wait_apart(pool, S["x2"], i)
                pool.indirect_dma_start(y[:], None, d["hash_out"],
                                        bass.IndirectOffsetOnAxis(rec[:, SLOTH:SLOTH + 1].bitcast(U32), 0)
                                        ).then_inc(S["y_in"], 16)
                pool.wait_ge(S["y_in"], i * 16 + 16)
                pool.wait_ge(S["r_sig"], i + 1)
                wait_for(pool, S["tx"], i)
                pool.tensor_tensor(x2[:], y[:], r[:], ALU.mult).then_inc(S["x2"], 1)

            fetch(0)
            with pool.Fori(1, NB) as i:
                fetch(i)

        @block.scalar
        def _(act):
            def units(u2, first=None):
                for n in range(2):
                    act.wait_ge(S[f"w_in{n}"], u2 * 16 + 16)
                    act.activation(unit(w_hi, u2 * 2 + n if first is None else first + n), raw[:, n],
                                   ACT.Copy).then_inc(S["w_hi"], 1)

            def r_sigmoid(i):
                act.wait_ge(S["r_in"], i * 16 + 16)
                act.activation(r[:], r[:], ACT.Sigmoid).then_inc(S["r_sig"], 1)

            def x_parts(i):
                act.wait_ge(S["tx"], i + 1)
                act.activation(x2t[:, i], tx_ps[:], ACT.Copy).then_inc(S["x_raw"], 1)
                act.wait_ge(S["x_raw"], i + 1)
                wait_apart(act, S["xpart"], i * NG)
                act.activation(x_hi[:, 0], x2t[:, i], ACT.Copy).then_inc(S["x_hi"], 1)

            def gates(i, n, turn):
                for g, f in ((G_G, ACT.Tanh), (G_I, ACT.Sigmoid), (G_F, ACT.Sigmoid)):
                    act.wait_ge(S["added"], i * NG + g + 1)
                    act.activation(gate[:, g], gate[:, g], f).then_inc(S["acted"], 1)

            def c_part(s):
                act.wait_ge(S["tc"], s + 1)
                act.activation(c_hi[:], tc_ps[:], ACT.Copy).then_inc(S["c_hi"], 1)

            with act.Fori(0, NU // 2) as u2:
                units(u2)
            c_part(0)
            software_pipeline(act, NB, [
                (0, lambda i, n, turn: r_sigmoid(i)), (2, gates), (2, lambda i, n, turn: c_part(i + 1)),
                (0, lambda i, n, turn: x_parts(i))], 2)
            act.wait_ge(S["xpart"], NB * NG)
            units(NU // 2, 0)
            act.wait_ge(S["c_lo"], NB + 1)
            act.activation(ct[:], tc_ps[:].rearrange("p k n -> p (k n)"), ACT.Copy).then_inc(S["ct_ready"], 1)

            def p_hi(i, n, turn):
                wait_apart(act, S["p_ps"], i - 1)
                act.activation(x_hi[:, n], x2t[:, i], ACT.Copy).then_inc(S["p_hi"], 1)

            def p_tanh(i, n, turn):
                act.wait_ge(S["p_add"], i + 1)
                act.activation(p_sum[n], p_sum[n], ACT.Tanh).then_inc(S["p_tanh"], 1)

            act.wait_ge(S["x_raw"], NB)
            software_pipeline(act, NB, [(0, p_hi), (1, p_tanh)], 2)

        @block.vector
        def _(dve):
            def units(u2, first=None):
                for n in range(2):
                    u = u2 * 2 + n
                    dve.wait_ge(S["w_hi"], u + 1)
                    v = u if first is None else first + n
                    dve.tensor_tensor(unit(w_lo, v), raw[:, n], unit(w_hi, v), ALU.subtract).then_inc(S["w_lo"], 1)

            def x_lo_(i, n, turn):
                dve.wait_ge(S["x_hi"], i + 1)
                dve.tensor_tensor(x_lo[:, 0], x2t[:, i], x_hi[:, 0], ALU.subtract).then_inc(S["x_lo"], 1)

            def gates(i, n, turn):
                for g in (G_G, G_I, G_F):
                    dve.wait_ge(S["gates"], i * NG + g + 1)
                    dve.wait_ge(S["c"], i + 1)
                    dve.tensor_tensor(gate[:, g], g_ps[n][g][:], bias[:, g], ALU.add).then_inc(S["added"], 1)
                dve.wait_ge(S["acted"], i * NG + 2)
                dve.tensor_tensor(gate[:, G_I], gate[:, G_I], gate[:, G_G], ALU.mult).then_inc(S["ig"], 1)
                dve.wait_ge(S["acted"], i * NG + 3)
                dve.tensor_tensor(gate[:, G_F], gate[:, G_F], c[:], ALU.mult).then_inc(S["fc"], 1)
                dve.wait_ge(S["ig"], i + 1)
                dve.wait_ge(S["fc"], i + 1)
                dve.wait_ge(S["tc"], i + 1)
                dve.tensor_tensor(c[:], gate[:, G_F], gate[:, G_I], ALU.add).then_inc(S["c"], 1)

            def c_part(s):
                dve.wait_ge(S["c_hi"], s + 1)
                dve.tensor_tensor(c_lo[:], tc_ps[:], c_hi[:], ALU.subtract).then_inc(S["c_lo"], 1)

            with dve.Fori(0, NU // 2) as u2:
                units(u2)
            dve.wait_ge(S["params_in"], 80)
            dve.tensor_copy(c[:], c[:]).then_inc(S["c"], 1)
            c_part(0)
            software_pipeline(dve, NB, [(2, gates), (2, lambda i, n, turn: c_part(i + 1)), (0, x_lo_)], 2)
            units(NU // 2, 0)
            dve.wait_ge(S["const_ps"], 1)
            dve.tensor_tensor(bo[:], g_ps[0][2][:], bo[:], ALU.add).then_inc(S["const"], 1)
            dve.wait_ge(S["const"], 1)

            def p_lo(i, n, turn):
                dve.wait_ge(S["p_hi"], i + 1)
                dve.tensor_tensor(x_lo[:, n], x2t[:, i], x_hi[:, n], ALU.subtract).then_inc(S["p_lo"], 1)

            def p_add(i, n, turn):
                dve.wait_ge(S["p_ps"], i + 1)
                wait_for(dve, S["p_out"], i - 1)
                dve.tensor_tensor(p_sum[n], g_ps[n][0][:], bo[:], ALU.add).then_inc(S["p_add"], 1)

            def p_out_(i, n, turn):
                dve.wait_ge(S["p_tanh"], i + 1)
                dve.wait_ge(S[f"x1_in{n}"], turn * 16 + 16)
                wait_for(dve, S[f"out{n}"], turn * 16)
                dve.tensor_tensor(p_out[n], p_sum[n], c_x1[n], ALU.add).then_inc(S["p_out"], 1)

            software_pipeline(dve, NB, [(0, p_lo), (1, p_add), (2, p_out_)], 2)

        @block.tensor
        def _(pe):
            def turn_x(i, n, turn):
                pe.wait_ge(S["x2"], i + 1)
                wait_for(pe, S["x_raw"], i)
                for k in range(DC):
                    mm = pe.transpose(tx_ps[:, k], x2[:, k * P:(k + 1) * P], ident[:])
                mm.then_inc(S["tx"], 1)

            def x_part(gs):
                def stage(i, n, turn):
                    pe.wait_ge(S["x_lo"], i + 1)
                    for g in gs:
                        wait_for(pe, S["added"], (i - 2) * NG + g + 1)
                        for k in range(DC):
                            mm = product(pe, g_ps[n][g][:], (x_hi[:, 0, k], x_lo[:, 0, k]),
                                         (w_hi[:, g, k], w_lo[:, g, k]), k == 0, False)
                        mm.then_inc(S["xpart"], 1)
                return stage

            def c_part(i, n, turn):
                pe.wait_ge(S["c_lo"], i + 1)
                for g in range(NG):
                    for k in range(DC):
                        mm = product(pe, g_ps[n][g][:], (c_hi[:, k], c_lo[:, k]),
                                     (w_hi[:, NG + g, k], w_lo[:, NG + g, k]), False, k == DC - 1)
                    mm.then_inc(S["gates"], 1)

            def turn_c(s):
                pe.wait_ge(S["c"], s + 1)
                wait_for(pe, S["c_lo"], s)
                for k in range(DC):
                    mm = pe.transpose(tc_ps[:, k], c[:, k * P:(k + 1) * P], ident[:])
                mm.then_inc(S["tc"], 1)

            turn_c(0)
            pe.wait_ge(S["w_lo"], NU)
            software_pipeline(pe, NB, [
                (2, c_part), (1, x_part((0, 1))), (2, lambda i, n, turn: turn_c(i + 1)), (1, x_part((2,))),
                (0, turn_x)], 2)
            pe.wait_ge(S["ct_ready"], 1)
            pe.wait_ge(S["uo_in"], 16)
            for k in range(DC):
                mm = pe.matmul(g_ps[0][2][:], ct[:, k * P:(k + 1) * P], raw[:].rearrange("p u (k n) -> p (u k) n", n=D)[:, k],
                               start=(k == 0), stop=(k == DC - 1))
            mm.then_inc(S["const_ps"], 1)

            def p(i, n, turn):
                pe.wait_ge(S["p_lo"], i + 1)
                wait_for(pe, S["p_add"], i - 1)
                for k in range(DC):
                    mm = product(pe, g_ps[n][0][:], (x_hi[:, n, k], x_lo[:, n, k]), (w_hi[:, 0, k], w_lo[:, 0, k]),
                                 k == 0, k == DC - 1)
                mm.then_inc(S["p_ps"], 1)

            software_pipeline(pe, NB, [(1, p)], 2)


SHAPES = {
    "x_rows": ([NTOK, D], FP32), "xt_groups": ([8, P, NB // 8, DC, P], FP32), "xt_tiles": ([NB, P, DC, P], FP32),
    "ids": ([P, NB], I32), "cond_t": ([P, DC, NB], FP32), "rt_w": ([P, DC, ER], FP32), "r_w": ([P, DC, ER], FP32),
    "r_bias": ([ER], FP32), "rw": ([ER, P, DC * HR + RC * D], FP32), "sw": ([12, P, HS], FP32),
    "wp1": ([P, DC, P], FP32), "wp2": ([P, ER], FP32), "bp1": ([P, 1], FP32), "bp2": ([ER], FP32),
    "w1": ([ER, P, DC, HS], FP32), "w2": ([ER, P, DC, HS], FP32), "b1": ([ER, HS], FP32), "b2": ([ER, D], FP32),
    "wo": ([P, 2, HS], FP32), "bo": ([D], FP32), "w_recept": ([P, 2, HS], FP32), "maa_k": ([D], FP32),
    "maa_r": ([D], FP32), "cond": ([NB, D], FP32), "w1h": ([EH, P, DC, HS], FP32),
    "w2h": ([EH, P, DC, HS], FP32), "gate_w": ([14, P, HS], FP32), "gate_bias": ([3, D], FP32),
    "uo": ([P, 2 * HS], FP32), "bo_r": ([D], FP32), "in_c": ([D], FP32),
    "c_batch": ([NB, 1], FP32), "c_eight": ([NB, ER], FP32),
    "c_tri": ([P, P], FP32), "c_ident": ([P, P], FP32), "c_expert": ([P, EH, NB], FP32), "c_run": ([P, EH, NB], FP32),
    "c_tile": ([P, RT, ER], FP32), "c_token": ([P, NB], I32),
}


def constants():
    import numpy as np
    i = np.arange(NB)
    p = np.arange(P)
    return {
        "c_tri": (p[:, None] < p[None, :]).astype(np.float32),
        "c_batch": i[:, None].astype(np.float32),
        "c_eight": np.broadcast_to(np.arange(ER, dtype=np.float32), (NB, ER)),
        "c_ident": np.eye(P, dtype=np.float32),
        "c_expert": np.broadcast_to(np.arange(EH, dtype=np.float32)[None, :, None], (P, EH, NB)),
        "c_run": np.broadcast_to((i > 0).astype(np.float32), (P, EH, NB)),
        "c_tile": np.broadcast_to(np.arange(RT, dtype=np.float32)[None, :, None], (P, RT, ER)),
        "c_token": (i[None, :] * P + p[:, None]).astype(np.int32),
    }


def chunked(w, width=None):
    return w.reshape(-1, P, w.shape[-1]).swapaxes(0, 1)


def lay_out(x, cond_1024, itok_BxS_2_50255, L0_cond_router_w, L0_cond_router_t_w, L0_cond_router_bias, L0_cond_sw1,
            L0_cond_sw3, L0_cond_sw2, L0_cond_rw1, L0_cond_rw2, L0_ffn_Wp1, L0_ffn_bp1, L0_ffn_Wp2, L0_ffn_bp2,
            L0_ffn_W1, L0_ffn_b1, L0_ffn_W2, L0_ffn_b2, L0_ffn_Wo, L0_ffn_bo, L1_cond_time_maa_k,
            L1_cond_time_maa_r, L1_cond_w_recept, L1_cond_w_key, L1_cond_w_value, L1_ffn_wf, L1_ffn_uf, L1_ffn_bf,
            L1_ffn_wi, L1_ffn_ui, L1_ffn_bi, L1_ffn_wc, L1_ffn_uc, L1_ffn_bc, L1_ffn_wo, L1_ffn_uo, L1_ffn_bo,
            L1_ffn_in_c):
    import numpy as np
    xt = x.reshape(NB, P, DC, P).transpose(0, 3, 2, 1)
    a = {
        "x_rows": x.reshape(NTOK, D),
        "xt_tiles": xt,
        "xt_groups": xt.reshape(8, NB // 8, P, DC, P).swapaxes(1, 2),
        "ids": itok_BxS_2_50255.T,
        "cond_t": chunked(cond_1024.T),
        "rt_w": chunked(L0_cond_router_t_w.T),
        "r_w": chunked(L0_cond_router_w.T),
        "r_bias": L0_cond_router_bias,
        "sw": np.concatenate([L0_cond_sw1.T.reshape(DC, P, HS), L0_cond_sw3.T.reshape(DC, P, HS),
                              L0_cond_sw2.T.reshape(HC // 2, 2, P, D).swapaxes(1, 2).reshape(HC // 2, P, HS)]),
    }
    a["rw"] = np.concatenate([L0_cond_rw1.reshape(ER, HR, DC, P).transpose(0, 3, 2, 1).reshape(ER, P, DC * HR),
                              L0_cond_rw2.reshape(ER, D, RC, P).transpose(0, 3, 2, 1).reshape(ER, P, RC * D)], 2)
    def by_expert(w):
        return w.reshape(w.shape[0], -1, P, w.shape[-1]).swapaxes(1, 2).reshape(w.shape[0], P, -1, HS)

    def square(w):
        return chunked(w).reshape(P, 2, HS)

    a.update(wp1=chunked(L0_ffn_Wp1), wp2=L0_ffn_Wp2, bp1=L0_ffn_bp1[:, None], bp2=L0_ffn_bp2,
             w1=by_expert(L0_ffn_W1), w2=by_expert(L0_ffn_W2), b1=L0_ffn_b1, b2=L0_ffn_b2,
             wo=square(L0_ffn_Wo), bo=L0_ffn_bo, w_recept=square(L1_cond_w_recept.T), maa_k=L1_cond_time_maa_k,
             maa_r=L1_cond_time_maa_r, cond=cond_1024)
    gate_w = [L1_ffn_wc, L1_ffn_wi, L1_ffn_wf, L1_ffn_uc, L1_ffn_ui, L1_ffn_uf, L1_ffn_wo]
    a.update(w1h=by_expert(L1_cond_w_key), w2h=by_expert(L1_cond_w_value),
             gate_w=np.stack([square(w.T) for w in gate_w]).swapaxes(1, 2).reshape(-1, P, HS),
             gate_bias=np.stack([L1_ffn_bc, L1_ffn_bi, L1_ffn_bf]), uo=chunked(L1_ffn_uo.T).reshape(P, -1),
             bo_r=L1_ffn_bo, in_c=L1_ffn_in_c)
    a.update(constants())
    return a


def build(nc, ins, out):
    with ExitStack() as ctx:
        dram = lambda n, s, t=FP32: nc.dram_tensor("mid_" + n, s, t, kind="Internal").ap()
        d = {"shared": dram("shared", [NB, P, D]), "routed": dram("routed", [NSLOT, D]), "rec": dram("rec", [NB, P, REC], I32),
             "slot_token": dram("slot_token", [NSLOT, 1], I32), "hash_in": dram("hash_in", [NTOK, D]),
             "x1": dram("x1", [NB, P + 1, D]), "r": dram("r", [NB, P, D]),
             "hash_out": dram("hash_out", [NTOK + 1, D])}
        keep = {"ident": ctx.enter_context(nc.sbuf_tensor("ident", [P, P], FP32)),
                "route": ctx.enter_context(nc.sbuf_tensor("route", [P, 2, RT], I32)),
                "order": ctx.enter_context(nc.sbuf_tensor("order", [1, 3, NB], I32))}
        stage_shared(nc, ins, d, keep)
        stage_routed(nc, ins, d, keep)
        stage_choose(nc, ins, d, keep)
        stage_ffn(nc, ins, d, keep)
        stage_hashed(nc, ins, d, keep)
        stage_recurrent(nc, ins, d, keep, out)


def kernel(**inputs):
    import numpy as np
    import concourse.bacc as bacc
    from concourse.bass_utils import run_bass_kernel_spmd

    nc = bacc.Bacc("TRN2", target_bir_lowering=False, num_devices=1)
    arrays = {"in_" + n: np.ascontiguousarray(a)
              for n, a in lay_out(**{n: np.asarray(a) for n, a in inputs.items()}).items()}
    ins = {n: nc.dram_tensor("in_" + n, shape, dtype, kind="ExternalInput").ap() for n, (shape, dtype) in SHAPES.items()}
    out = nc.dram_tensor("out", [NB, P, D], FP32, kind="ExternalOutput").ap()
    build(nc, ins, out)
    return run_bass_kernel_spmd(nc, [arrays], core_ids=[0]).results[0]["out"]
```

```python
import concourse.bass as bass
from concourse import mybir
from contextlib import ExitStack

FP32 = mybir.dt.float32
FP32R = mybir.dt.float32r
BF16 = mybir.dt.bfloat16
I32 = mybir.dt.int32
U32 = mybir.dt.uint32
ALU = mybir.AluOpType
ACT = mybir.ActivationFunctionType
AX = mybir.AxisListType.X

P = 128
NB = 32
NTOK = NB * P
D = 512
DC = D // P
HS = 1024
HC = HS // P
HR = 256
RC = HR // P
ER = 8
EH = 16
CAP = NTOK // EH
RT = 2 * NTOK // P + ER
NSLOT = RT * P
SLOT1, SLOT2, SLOTH, GATE1, GATE2, TOKEN = range(6)
REC = 6
EPS = 1e-9
DVE_BIG = 3.0e38


def wait_for(eng, sem, n):
    if isinstance(n, int) and n <= 0:
        return
    eng.wait_ge(sem, n)


def wait_apart(eng, sem, n):
    if isinstance(n, int) and n <= 0:
        return
    eng.wait_ge(sem, n)
    eng.nop(nofuse=True)


def software_pipeline(eng, tiles, stages, unroll=1):
    depth = max(lag for lag, _ in stages)
    head = -(-(depth + unroll) // unroll) * unroll

    def step(j, par, block=None):
        for lag, stage in stages:
            i = j - lag
            n = (par - lag) % unroll
            if not isinstance(i, int):
                stage(*((i, n, block + (par - lag - n) // unroll) if unroll > 1 else (i,)))
            elif 0 <= i < tiles:
                stage(*((i, n, i // unroll) if unroll > 1 else (i,)))

    for j in range(head):
        step(j, j % unroll)
    with eng.Fori(head // unroll, tiles // unroll) as block:
        for par in range(unroll):
            step(block * unroll + par, par, block)
    for j in range(tiles, tiles + depth):
        step(j, j % unroll)


def but_first(stage):
    return lambda i: None if isinstance(i, int) and i == 0 else stage(i)


def product(pe, out, a, w, first, last):
    (a_hi, a_lo), (w_hi, w_lo) = a, w
    pe.matmul(out, a_hi, w_hi, start=first, stop=False, skip_group_check=True)
    pe.matmul(out, a_hi, w_lo, start=False, stop=False, skip_group_check=True)
    return pe.matmul(out, a_lo, w_hi, start=False, stop=last, skip_group_check=True)


def sems(nc, ctx, prefix, names):
    own = {n[1:]: nc.alloc_semaphore(prefix + n[1:]) for n in names.split() if n[0] == "~"}
    names = " ".join(n for n in names.split() if n[0] != "~")
    made = {n: ctx.enter_context(nc.semaphore(prefix + n)) for n in names.split()}

    def clear():
        numbers = sorted(sem.num for sem in made.values())
        while numbers:
            run = 1
            while run < len(numbers) and numbers[run] == numbers[0] + run:
                run += 1
            nc.sync.sem_clear(range(numbers[0], numbers[0] + run))
            numbers = numbers[run:]

    ctx.callback(clear)
    return made | own



def stage_shared(nc, ins, d, keep):
    G = 8
    TG = NB // G
    NU = 12
    with ExitStack() as ctx:
        sb = lambda n, s, t=FP32: ctx.enter_context(nc.sbuf_tensor("s1_" + n, s, t))
        ps = lambda n, s, t=FP32: ctx.enter_context(nc.psum_tensor("s1_" + n, s, t))
        S = sems(nc, ctx, "s1_", "const late_const ~x_in0 ~x_in1 logits_t logits_sum logits bias_ps bias w_in0 w_in1 w_hi w_lo ones sig dve pe_rank "
                 "~rec_out ~rec_in ~tokens_sent0 ~tokens_sent1 zeroed ~zero_out "
                 "xt_in xt_hi xt_lo gu silu hmul th h_hi h_lo mm2 o_ready o_out ~lists hash_members hash_total_read hash_rank_read "
                 "rank_read members rec_done")

        x_grp = sb("x_grp", [P, 2, TG, DC, P])
        w_raw = sb("w_raw", [P, 2, HS])
        w_hi = sb("w_hi", [P, NU, HS], FP32R)
        w_lo = sb("w_lo", [P, NU, HS], FP32R)
        sw2_hi = w_hi[:, 8:12, :].rearrange("p u (a n) -> p (u a) n", a=2)
        sw2_lo = w_lo[:, 8:12, :].rearrange("p u (a n) -> p (u a) n", a=2)
        ident = keep["ident"]
        tri_f = sb("tri_f", [P, P])
        tri = sb("tri", [P, P], BF16)
        ones = sb("ones", [P, P], BF16)
        ones_f = sb("ones_f", [P, ER])
        expert_no = sb("expert_no", [P, EH, NB])
        new_run = sb("new_run", [P, EH, NB])
        tile_no = sb("tile_no", [P, RT, ER])
        token_no = sb("token_no", [P, NB], I32)
        ids = sb("ids", [P, NB], I32)
        hash_id = sb("hash_id", [P, NB], I32)
        cond_t = sb("cond_t", [P, DC, NB])
        rt_w = sb("rt_w", [P, DC, ER])
        r_w = sb("r_w", [P, DC, ER])
        r_bias = sb("r_bias", [P, ER])
        batch_bias = sb("batch_bias", [ER, NB])
        logits_sb = sb("logits_sb", [ER, 2, TG, P])
        score = sb("score", [P, ER, NB])
        sel = sb("sel", [P, ER, NB])
        t1 = sb("t1", [P, EH, NB])
        t2 = sb("t2", [P, EH, NB])
        oh1 = sb("oh1", [P, EH, NB])
        oh2 = sb("oh2", [P, ER, NB])
        member = sb("member", [P, EH, NB], BF16)
        col = sb("col", [P, 8, NB])
        cnt_i = sb("cnt_i", [P, ER], I32)
        cnt_f = sb("cnt_f", [P, 4, ER])
        tile_ge = sb("tile_ge", [P, RT, ER])
        tile_e = sb("tile_e", [P, 3, RT])
        rec = sb("rec", [P, NB, REC], I32)
        rec_f = rec[:].bitcast(FP32)
        rec_tile = sb("rec_tile", [P, 2, REC], I32)
        zero = sb("zero", [P, D])
        izero = sb("izero", [P, RT], I32)

        xt_raw = sb("xt_raw", [P, DC, P])
        xt_hi = sb("xt_hi", [P, DC, P], FP32R)
        xt_lo = sb("xt_lo", [P, DC, P], FP32R)
        sg = sb("sg", [P, 2, D])
        h = sb("h", [P, 2, D])
        ht_hi = sb("ht_hi", [P, HC, P], FP32R)
        ht_lo = sb("ht_lo", [P, HC, P], FP32R)
        o_sb = sb("o_sb", [P, D])

        gate_ps = [ps(f"gate{n}", [P, D]) for n in range(2)]
        up_ps = [ps(f"up{n}", [P, D]) for n in range(2)]
        th_ps = [ps(f"th{n}", [P, DC, P]) for n in range(2)]
        o_ps = ps("o", [P, D])
        aux_ps = ps("aux", [P, 512])
        lg_ps = aux_ps[:, 0:ER * NB].rearrange("p (e i) -> p e i", e=ER)
        aux_h = aux_ps[:, :].rearrange("p (e i) -> p e i", e=EH)
        rank_ps = aux_ps[:, 0:256].rearrange("p (e i) -> p e i", e=ER)
        bias_ps = o_ps[0:ER, 0:NB]
        tot_ps = aux_ps[:, 256:512].rearrange("p (e i) -> p e i", e=ER)

        n_const, n_late = 8, 3

        block = ctx.enter_context(nc.Block())

        @block.sync
        def _(sp):
            for dst, src in ((rt_w[:], ins["rt_w"]), (cond_t[:], ins["cond_t"]), (r_w[:], ins["r_w"]),
                             (ids[:], ins["ids"]), (tri_f[:], ins["c_tri"]), (ident[:], ins["c_ident"]),
                             (expert_no[:], ins["c_expert"]), (new_run[:], ins["c_run"])):
                sp.dma_start(dst, src).then_inc(S["const"], 16)

            def units(u2):
                for n in range(2):
                    wait_for(sp, S["w_lo"], u2 * 2 + n - 1)
                    sp.dma_start(w_raw[:, n], ins["sw"][u2 * 2 + n]).then_inc(S[f"w_in{n}"], 16)

            units(0)
            for dst, src in ((tile_no[:], ins["c_tile"]), (token_no[:], ins["c_token"]),
                             (r_bias[:], ins["r_bias"].partition_broadcast(P))):
                sp.dma_start(dst, src).then_inc(S["late_const"], 16)
            with sp.Fori(1, NU // 2) as u2:
                units(u2)

            def load_x(i):
                wait_for(sp, S["xt_lo"], i)
                sp.dma_start(xt_raw[:], ins["xt_tiles"][i]).then_inc(S["xt_in"], 16)

            def store_o(i):
                sp.wait_ge(S["o_ready"], i + 1)
                sp.dma_start(d["shared"][i], o_sb[:]).then_inc(S["o_out"], 16)

            software_pipeline(sp, NB, [(0, load_x), (2, store_o)])
            sp.wait_ge(S["o_out"], 16 * NB)

        @block.gpsimd
        def _(pool):
            for k in range(2):
                pool.dma_start(x_grp[:, k], ins["xt_groups"][k]).then_inc(S[f"x_in{k}"], 16)
            pool.memset(zero[:], 0.0).then_inc(S["zeroed"], 1)
            pool.memset(izero[:], 0).then_inc(S["zeroed"], 1)
            pool.wait_ge(S["zeroed"], 2)
            pool.dma_start(d["slot_token"].rearrange("(p j) o -> p (j o)", j=RT), izero[:]).then_inc(S["lists"], 16)
            pool.dma_start(d["hash_out"][NTOK:NTOK + 1, :], zero[0:1, :]).then_inc(S["zero_out"], 16)
            pool.wait_ge(S["lists"], 16)
            for g in range(2, G):
                pool.wait_ge(S["logits_t"], g - 1)
                pool.dma_start(x_grp[:, g % 2], ins["xt_groups"][g]).then_inc(S[f"x_in{g % 2}"], 16)
            pool.wait_ge(S["rec_done"], 1)
            pool.dma_start(d["rec"].rearrange("i p c -> p i c"), rec[:]).then_inc(S["rec_out"], 16)
            pool.wait_ge(S["rec_out"], 16)

            def enter_tokens(i2, first):
                for k in range(2):
                    if not first:
                        pool.wait_ge(S[f"tokens_sent{k}"], i2 * 32)
                    pool.dma_start(rec_tile[:, k], d["rec"][i2 * 2 + k]).then_inc(S["rec_in"], 16)
                    wait_apart(pool, S["rec_in"], i2 * 32 + 16 * k + 16)
                    for c in (SLOT1, SLOT2):
                        pool.indirect_dma_start(
                            d["slot_token"], bass.IndirectOffsetOnAxis(rec_tile[:, k, c:c + 1].bitcast(U32), 0),
                            rec_tile[:, k, TOKEN:TOKEN + 1], None).then_inc(S[f"tokens_sent{k}"], 16)
                    pool.dma_start(d["hash_in"][bass.ds((i2 * 2 + k) * P, P)], zero[:]).then_inc(S["zero_out"], 16)

            enter_tokens(0, True)
            with pool.Fori(1, NB // 2) as i2:
                enter_tokens(i2, False)
            for k in range(2):
                pool.wait_ge(S[f"tokens_sent{k}"], 16 * NB)
            pool.wait_ge(S["zero_out"], 16 * (NB + 1))

        @block.scalar
        def _(act):
            with act.Fori(0, NU // 2) as u2:
                for n in range(2):
                    act.wait_ge(S[f"w_in{n}"], u2 * 16 + 16)
                    act.activation(w_hi[:, u2 * 2 + n, :], w_raw[:, n, :], ACT.Copy).then_inc(S["w_hi"], 1)
            def x_hi(i):
                act.wait_ge(S["xt_in"], i * 16 + 16)
                wait_for(act, S["gu"], 2 * i)
                act.activation(xt_hi[:], xt_raw[:], ACT.Copy).then_inc(S["xt_hi"], 1)

            def silu(i):
                for n in range(2):
                    act.wait_ge(S["gu"], 2 * i + n + 1)
                    wait_for(act, S["hmul"], 2 * i + n - 1)
                    act.activation(sg[:, n], gate_ps[n][:], ACT.Silu).then_inc(S["silu"], 1)

            def h_hi(i):
                for n in range(2):
                    act.wait_ge(S["th"], 2 * i + n + 1)
                    wait_for(act, S["mm2"], i)
                    act.activation(ht_hi[:, n * DC:(n + 1) * DC], th_ps[n][:], ACT.Copy).then_inc(S["h_hi"], 1)

            def o_out(i):
                act.wait_ge(S["mm2"], i + 1)
                wait_for(act, S["o_out"], i * 16)
                act.activation(o_sb[:], o_ps[:], ACT.Copy, scale=1.0 / 3.0).then_inc(S["o_ready"], 1)

            x_hi(0)
            act.wait_ge(S["logits"], G)
            act.activation(score[:], lg_ps, ACT.Sigmoid).then_inc(S["sig"], 1)
            software_pipeline(act, NB, [(1, silu), (0, but_first(x_hi)), (2, o_out), (1, h_hi)])

        @block.vector
        def _(dve):
            done = [0]

            def op(ins_):
                done[0] += 1
                ins_.then_inc(S["dve"], 1)
                dve.wait_ge(S["dve"], done[0])

            def signal(ins_, name):
                ins_.then_inc(S[name], 1)
                dve.wait_ge(S[name], 1)

            def ranks(experts, rank, off, incl, last_step):
                op(dve.tensor_tensor_scan(incl.rearrange("p e i -> p (e i)"),
                                          new_run[:, 0:experts].rearrange("p e i -> p (e i)"),
                                          off.rearrange("p e i -> p (e i)"), 0.0, ALU.mult, ALU.add))
                op(dve.tensor_tensor(off, incl, off, ALU.subtract))
                signal(dve.tensor_tensor(off, off, rank, ALU.add), last_step)

            dve.wait_ge(S["const"], 16 * n_const)
            dve.memset(ones[:], 1.0).then_inc(S["ones"], 1)
            dve.memset(ones_f[:], 1.0).then_inc(S["ones"], 1)
            dve.tensor_copy(tri[:], tri_f[:]).then_inc(S["ones"], 1)
            low = col[:, 0]
            hid = hash_id[:]
            op(dve.tensor_scalar(hid, ids[:], 15, None, ALU.bitwise_and))
            op(dve.tensor_copy(low, hid))
            op(dve.tensor_scalar(low, low, 11.0, None, ALU.mult))
            op(dve.tensor_copy(hid, low))
            op(dve.tensor_scalar(hid, hid, 15, None, ALU.bitwise_and))
            op(dve.tensor_copy(low, hid))
            op(dve.tensor_tensor(oh1[:], expert_no[:], low[:, None, :].to_broadcast([P, EH, NB]), ALU.is_equal))
            signal(dve.tensor_copy(member[:], oh1[:]), "hash_members")
            dve.wait_ge(S["pe_rank"], 1)
            signal(dve.tensor_copy(t1[:], aux_h), "hash_total_read")
            dve.wait_ge(S["pe_rank"], 2)
            ranks(EH, aux_h, t1[:], t2[:], "hash_rank_read")
            op(dve.tensor_tensor(t1[:], t1[:], oh1[:], ALU.mult))
            pos, keep_, slot = col[:, 2], col[:, 3], col[:, 4]
            op(dve.tensor_reduce(pos, t1[:].rearrange("p e i -> p i e"), AX, ALU.add))
            op(dve.tensor_scalar(keep_, pos, float(CAP), None, ALU.is_lt))
            op(dve.scalar_tensor_tensor(slot, low, float(CAP), pos, ALU.mult, ALU.add))
            op(dve.scalar_tensor_tensor(slot, slot, -float(NTOK), keep_, ALU.add, ALU.mult))
            op(dve.tensor_scalar(slot, slot, float(NTOK), None, ALU.add))
            op(dve.tensor_copy(rec[:, :, SLOTH], slot))
            dve.wait_ge(S["late_const"], 16 * n_late)
            op(dve.tensor_copy(rec[:, :, TOKEN], token_no[:]))
            dve.wait_ge(S["bias_ps"], 1)
            signal(dve.tensor_copy(batch_bias[:], bias_ps), "bias")

            def add_bias(g):
                dve.wait_ge(S["logits_t"], g + 1)
                wait_for(dve, S["logits"], g - 1)
                dve.tensor_tensor(logits_sb[:, g % 2], th_ps[g % 2][0:ER],
                                  batch_bias[:, g * TG:(g + 1) * TG, None].to_broadcast([ER, TG, P]),
                                  ALU.add).then_inc(S["logits_sum"], 1)

            add_bias(0)
            for u2, groups in enumerate(((1,), (2, 3), (4,), (5, 6), (7,), ())):
                for n in range(2):
                    u = u2 * 2 + n
                    dve.wait_ge(S["w_hi"], u + 1)
                    dve.tensor_tensor(w_lo[:, u, :], w_raw[:, n, :], w_hi[:, u, :], ALU.subtract).then_inc(S["w_lo"], 1)
                for g in groups:
                    add_bias(g)

            def x_lo(i):
                dve.wait_ge(S["xt_hi"], i + 1)
                dve.tensor_tensor(xt_lo[:], xt_raw[:], xt_hi[:], ALU.subtract).then_inc(S["xt_lo"], 1)

            def h_mul(i):
                for n in range(2):
                    dve.wait_ge(S["silu"], 2 * i + n + 1)
                    wait_for(dve, S["th"], 2 * i + n - 1)
                    dve.tensor_tensor(h[:, n], sg[:, n], up_ps[n][:], ALU.mult).then_inc(S["hmul"], 1)

            def h_lo(i):
                for n in range(2):
                    dve.wait_ge(S["h_hi"], 2 * i + n + 1)
                    dve.tensor_tensor(ht_lo[:, n * DC:(n + 1) * DC], th_ps[n][:], ht_hi[:, n * DC:(n + 1) * DC],
                                      ALU.subtract).then_inc(S["h_lo"], 1)

            x_lo(0)
            dve.wait_ge(S["sig"], 1)
            no8 = expert_no[:, 0:ER]
            op(dve.tensor_tensor(sel[:], score[:], r_bias[:, :, None].to_broadcast([P, ER, NB]), ALU.add))
            gate = []
            for c, one in ((0, oh1[:, 0:ER]), (1, oh2[:])):
                best, idx, g = col[:, c], col[:, 2 + c], col[:, 4 + c]
                op(dve.tensor_reduce(best, sel[:].rearrange("p e i -> p i e"), AX, ALU.max))
                op(dve.tensor_tensor(t1[:, 0:ER], sel[:], best[:, None, :].to_broadcast([P, ER, NB]), ALU.is_lt))
                op(dve.scalar_tensor_tensor(t1[:, 0:ER], t1[:, 0:ER], float(ER), no8, ALU.mult, ALU.add))
                op(dve.tensor_reduce(idx, t1[:, 0:ER].rearrange("p e i -> p i e"), AX, ALU.min))
                op(dve.tensor_tensor(one, no8, idx[:, None, :].to_broadcast([P, ER, NB]), ALU.is_equal))
                op(dve.tensor_tensor(t1[:, 0:ER], one, score[:], ALU.mult))
                op(dve.tensor_reduce(g, t1[:, 0:ER].rearrange("p e i -> p i e"), AX, ALU.add))
                if c == 0:
                    op(dve.scalar_tensor_tensor(sel[:], one, -DVE_BIG, sel[:], ALU.mult, ALU.add))
                gate.append(g)
            signal(dve.tensor_tensor(member[:, 0:ER], oh1[:, 0:ER], oh2[:], ALU.add), "members")

            tiles_f, end, base = cnt_f[:, 0], cnt_f[:, 1], cnt_f[:, 2]

            def after_ranks():
                den, inv, above = col[:, 0], col[:, 1], col[:, 2]
                op(dve.tensor_tensor(den, gate[0], gate[1], ALU.add))
                op(dve.tensor_scalar(above, den, EPS, None, ALU.is_gt))
                op(dve.tensor_scalar(den, den, EPS, None, ALU.add))
                op(dve.reciprocal(inv, den))
                for c, g in enumerate(gate):
                    op(dve.tensor_tensor(g, g, inv, ALU.mult))
                    op(dve.scalar_tensor_tensor(g, g, -0.5, above, ALU.add, ALU.mult))
                    op(dve.tensor_scalar(g, g, 0.5, 1.0 / 3.0, ALU.add, ALU.mult))
                    op(dve.tensor_copy(rec_f[:, :, GATE1 + c], g))
                dve.wait_ge(S["pe_rank"], 3)
                op(dve.tensor_copy(t1[:, 0:ER], tot_ps))
                ranks(ER, rank_ps, t1[:, 0:ER], t2[:, 0:ER], "rank_read")
                op(dve.tensor_scalar(tiles_f, t2[:, 0:ER, NB - 1], float(P - 1), None, ALU.add))
                op(dve.tensor_copy(cnt_i[:], tiles_f))
                op(dve.tensor_scalar(cnt_i[:], cnt_i[:], 7, None, ALU.arith_shift_right))
                op(dve.tensor_copy(tiles_f, cnt_i[:]))
                op(dve.tensor_tensor_scan(end, ones_f[:, 0:ER], tiles_f, 0.0, ALU.mult, ALU.add))
                op(dve.tensor_tensor(base, end, tiles_f, ALU.subtract))
                op(dve.tensor_scalar(base, base, float(P), None, ALU.mult))
                op(dve.tensor_tensor(t1[:, 0:ER], t1[:, 0:ER], base[:, :, None].to_broadcast([P, ER, NB]), ALU.add))
                for c, one in ((0, oh1[:, 0:ER]), (1, oh2[:])):
                    op(dve.tensor_tensor(t2[:, 0:ER], t1[:, 0:ER], one, ALU.mult))
                    op(dve.tensor_reduce(col[:, c], t2[:, 0:ER].rearrange("p e i -> p i e"), AX, ALU.add))
                    (op, lambda x: signal(x, "rec_done"))[c](dve.tensor_copy(rec[:, :, SLOT1 + c], col[:, c]))
            after_ranks()
            software_pipeline(dve, NB, [(1, h_mul), (0, but_first(x_lo)), (1, h_lo)])
            op(dve.tensor_tensor(tile_ge[:], tile_no[:], end[:, None, :].to_broadcast([P, RT, ER]), ALU.is_ge))
            te, new = tile_e[:, 0], tile_e[:, 1]
            op(dve.tensor_reduce(te, tile_ge[:], AX, ALU.add))
            op(dve.tensor_scalar(te, te, float(ER - 1), None, ALU.min))
            op(dve.memset(new, 1.0))
            op(dve.tensor_tensor(new[:, 2:RT], te[:, 2:RT], te[:, 0:RT - 2], ALU.not_equal))
            op(dve.tensor_copy(keep["route"][:, 0], te))
            op(dve.tensor_copy(keep["route"][:, 1], new))

        @block.tensor
        def _(pe):
            pe.wait_ge(S["const"], 16 * n_const)
            for k in range(DC):
                mm = pe.matmul(bias_ps, rt_w[:, k], cond_t[:, k], start=(k == 0), stop=(k == DC - 1))
            mm.then_inc(S["bias_ps"], 1)
            pe.wait_ge(S["ones"], 3)
            pe.wait_ge(S["hash_members"], 1)
            flat = member[:].rearrange("p e i -> p (e i)")
            pe.matmul(aux_ps[:, :], ones[:], flat, start=True, stop=True).then_inc(S["pe_rank"], 1)
            pe.wait_ge(S["hash_total_read"], 1)
            pe.matmul(aux_ps[:, :], tri[:], flat, start=True, stop=True).then_inc(S["pe_rank"], 1)

            def score_t(g):
                pe.wait_ge(S[f"x_in{g % 2}"], g // 2 * 16 + 16)
                wait_for(pe, S["logits_sum"], g - 1)
                for k in range(DC):
                    mm = pe.matmul(th_ps[g % 2][0:ER], r_w[:, k], x_grp[:, g % 2, :, k], start=(k == 0),
                                   stop=(k == DC - 1))
                mm.then_inc(S["logits_t"], 1)

            def turn_scores(g):
                pe.wait_ge(S["logits_sum"], g + 1)
                for tt in range(TG):
                    mm = pe.transpose(lg_ps[:, :, g * TG + tt], logits_sb[:, g % 2, tt], ident[0:ER, 0:ER])
                mm.then_inc(S["logits"], 1)

            score_t(0)
            pe.wait_ge(S["hash_rank_read"], 1)
            for g in range(1, G):
                score_t(g)
                turn_scores(g - 1)
            turn_scores(G - 1)

            def gate_up(i):
                pe.wait_ge(S["xt_lo"], i + 1)
                for n in range(2):
                    wait_for(pe, S["hmul"], 2 * i + n - 1)
                    for out, u0 in ((gate_ps[n], 0), (up_ps[n], 4)):
                        for k in range(DC):
                            mm = product(pe, out[:], (xt_hi[:, k], xt_lo[:, k]),
                                         (w_hi[:, u0 + k, n * D:(n + 1) * D], w_lo[:, u0 + k, n * D:(n + 1) * D]),
                                         k == 0, k == DC - 1)
                    mm.then_inc(S["gu"], 1)

            def turn_h(i):
                for n in range(2):
                    pe.wait_ge(S["hmul"], 2 * i + n + 1)
                    wait_for(pe, S["h_lo"], 2 * i + n - 1)
                    for k in range(DC):
                        mm = pe.transpose(th_ps[n][:, k], h[:, n, k * P:(k + 1) * P], ident[:])
                    mm.then_inc(S["th"], 1)

            def down(i):
                pe.wait_ge(S["h_lo"], 2 * i + 2)
                wait_for(pe, S["o_ready"], i)
                for k in range(HC):
                    mm = product(pe, o_ps[:], (ht_hi[:, k], ht_lo[:, k]), (sw2_hi[:, k], sw2_lo[:, k]),
                                 k == 0, k == HC - 1)
                mm.then_inc(S["mm2"], 1)

            pe.wait_ge(S["w_lo"], NU)
            gate_up(0)
            pe.wait_ge(S["members"], 1)
            flat8 = member[:, 0:ER].rearrange("p e i -> p (e i)")
            pe.matmul(aux_ps[:, 0:256], tri[:], flat8, start=True, stop=True)
            pe.matmul(aux_ps[:, 256:512], ones[:], flat8, start=True, stop=True,
                      skip_group_check=True).then_inc(S["pe_rank"], 1)
            software_pipeline(pe, NB, [(1, but_first(gate_up)), (2, down), (1, turn_h)])




def stage_routed(nc, ins, d, keep):
    with ExitStack() as ctx:
        sb = lambda n, s, t=FP32: ctx.enter_context(nc.sbuf_tensor("s2_" + n, s, t))
        ps = lambda n, s, t=FP32: ctx.enter_context(nc.psum_tensor("s2_" + n, s, t))
        S = sems(nc, ctx, "s2_", "idx_in0 idx_in1 idx_in2 idx_in3 ~x_in0 ~x_in1 ~x_in2 ~x_in3 w1_in0 w1_in1 w2_in0 w2_in1 wo_in wo_hi wo_lo w1_hi w1_lo w2_hi w2_lo tx x_hi x_lo mm1 "
                 "gelu th h_hi h_lo mm2 o_ready o_out0 o_out1 o_out2 o_out3")
        W1, W2 = DC * HR, RC * D
        route = keep["route"]
        ident = keep["ident"]
        NI = 4
        idx = sb("idx", [P, NI, 1], I32)
        x = sb("x", [P, NI, D])
        w_raw = sb("w_raw", [P, 2, W1 + W2])
        w_hi = sb("w_hi", [P, 2, W1 + W2], FP32R)
        w_lo = sb("w_lo", [P, 2, W1 + W2], FP32R)
        x_hi = sb("x_hi", [P, 2, DC, P], FP32R)
        x_lo = sb("x_lo", [P, 2, DC, P], FP32R)
        h = sb("h", [P, 2, HR])
        ht_hi = sb("ht_hi", [P, 2, RC, P], FP32R)
        ht_lo = sb("ht_lo", [P, 2, RC, P], FP32R)
        o_sb = sb("o_sb", [P, NI, D])
        wo_raw = sb("wo_raw", [P, 2, DC * D])
        flat = lambda w, n: w[:, n].rearrange("p k n -> p (k n)")
        tx_ps = [ps(f"tx{n}", [P, DC, P]) for n in range(2)]
        h_ps = [ps(f"h{n}", [P, HR]) for n in range(2)]
        th_ps = [ps(f"th{n}", [P, RC, P]) for n in range(2)]
        o_ps = [ps(f"o{n}", [P, D]) for n in range(2)]

        block = ctx.enter_context(nc.Block())

        @block.sync
        def _(sp):
            def load_idx(i, n, turn):
                wait_for(sp, S[f"x_in{n}"], turn * 16)
                sp.dma_start(idx[:, n], d["slot_token"][bass.ds(i * P, P)]).then_inc(S[f"idx_in{n}"], 16)

            def load_w(name, c):
                def stage(i, n, turn):
                    expert = sp.value_load(route[0:1, 0, bass.ds(i, 1)], min_val=0, max_val=ER - 1)
                    new = sp.value_load(route[0:1, 1, bass.ds(i, 1)], min_val=0, max_val=1)
                    wait_apart(sp, S[name + "_lo"], i - 1)
                    sp.dma_start(w_raw[:, n % 2, c], ins["rw"][expert, :, c],
                                 cond=new > 0).then_inc(S[f"{name}_in{n % 2}"], 16)
                return stage

            def store(i, n, turn):
                sp.wait_ge(S["o_ready"], i + 1)
                sp.dma_start(d["routed"][bass.ds(i * P, P)], o_sb[:, n]).then_inc(S[f"o_out{n}"], 16)

            def load_wo(i, n, turn):
                if isinstance(i, int) and i < 2:
                    sp.dma_start(wo_raw[:, i], ins["square"][i]).then_inc(S["wo_in"], 16)

            software_pipeline(sp, RT, [(0, load_idx), (2, load_w("w1", slice(0, W1))),
                                       (3, load_w("w2", slice(W1, W1 + W2))), (4, load_wo), (7, store)], NI)
            for n in range(NI):
                sp.wait_ge(S[f"o_out{n}"], 16 * RT // NI)

        @block.gpsimd
        def _(pool):
            def gather(i, n, turn):
                pool.wait_ge(S[f"idx_in{n}"], turn * 16 + 16)
                wait_apart(pool, S["tx"], i - NI + 1)
                pool.indirect_dma_start(x[:, n], None, ins["x_rows"],
                                        bass.IndirectOffsetOnAxis(idx[:, n].bitcast(U32), 0)
                                        ).then_inc(S[f"x_in{n}"], 16)

            software_pipeline(pool, RT, [(0, gather)], NI)

        @block.scalar
        def _(act):
            def w1_hi(i, n, turn):
                act.wait_ge(S[f"w1_in{n % 2}"], (turn * 2 + n // 2) * 16 + 16)
                wait_for(act, S["mm1"], i - 1)
                act.activation(w_hi[:, n % 2, 0:W1], w_raw[:, n % 2, 0:W1], ACT.Copy).then_inc(S["w1_hi"], 1)

            def w2_hi(i, n, turn):
                act.wait_ge(S[f"w2_in{n % 2}"], (turn * 2 + n // 2) * 16 + 16)
                wait_for(act, S["mm2"], i - 1)
                act.activation(w_hi[:, n % 2, W1:], w_raw[:, n % 2, W1:], ACT.Copy).then_inc(S["w2_hi"], 1)

            def x_hi_(i, n, turn):
                act.wait_ge(S["tx"], i + 1)
                wait_for(act, S["mm1"], i - 1)
                act.activation(x_hi[:, n % 2], tx_ps[n % 2][:], ACT.Copy).then_inc(S["x_hi"], 1)

            def gelu(i, n, turn):
                act.wait_ge(S["mm1"], i + 1)
                wait_for(act, S["th"], i - 1)
                act.activation(h[:, n % 2], h_ps[n % 2][:], ACT.Gelu).then_inc(S["gelu"], 1)

            def h_hi(i, n, turn):
                act.wait_ge(S["th"], i + 1)
                wait_for(act, S["mm2"], i - 1)
                act.activation(ht_hi[:, n % 2], th_ps[n % 2][:], ACT.Copy).then_inc(S["h_hi"], 1)

            def o_copy(i, n, turn):
                act.wait_ge(S["mm2"], i + 1)
                wait_for(act, S[f"o_out{n}"], turn * 16)
                act.activation(o_sb[:, n], o_ps[n % 2][:], ACT.Copy).then_inc(S["o_ready"], 1)

            def wo_hi(i, n, turn):
                if isinstance(i, int) and i < 2:
                    act.wait_ge(S["wo_in"], 32)
                    act.activation(flat(keep["wo_hi"], i), wo_raw[:, i], ACT.Copy).then_inc(S["wo_hi"], 1)

            software_pipeline(act, RT, [(2, gelu), (1, x_hi_), (0, w1_hi), (3, o_copy), (2, h_hi), (1, w2_hi),
                                        (3, wo_hi)], NI)

        @block.vector
        def _(dve):
            def w1_lo(i, n, turn):
                dve.wait_ge(S["w1_hi"], i + 1)
                dve.tensor_tensor(w_lo[:, n, 0:W1], w_raw[:, n, 0:W1], w_hi[:, n, 0:W1],
                                  ALU.subtract).then_inc(S["w1_lo"], 1)

            def w2_lo(i, n, turn):
                dve.wait_ge(S["w2_hi"], i + 1)
                dve.tensor_tensor(w_lo[:, n, W1:], w_raw[:, n, W1:], w_hi[:, n, W1:],
                                  ALU.subtract).then_inc(S["w2_lo"], 1)

            def x_lo_(i, n, turn):
                dve.wait_ge(S["x_hi"], i + 1)
                dve.tensor_tensor(x_lo[:, n], tx_ps[n][:], x_hi[:, n], ALU.subtract).then_inc(S["x_lo"], 1)

            def h_lo(i, n, turn):
                dve.wait_ge(S["h_hi"], i + 1)
                dve.tensor_tensor(ht_lo[:, n], th_ps[n][:], ht_hi[:, n], ALU.subtract).then_inc(S["h_lo"], 1)

            def wo_lo(i, n, turn):
                if isinstance(i, int) and i < 2:
                    dve.wait_ge(S["wo_hi"], i + 1)
                    dve.tensor_tensor(flat(keep["wo_lo"], i), wo_raw[:, i], flat(keep["wo_hi"], i),
                                      ALU.subtract).then_inc(S["wo_lo"], 1)

            software_pipeline(dve, RT, [(1, x_lo_), (0, w1_lo), (2, h_lo), (1, w2_lo), (3, wo_lo)], 2)

        @block.tensor
        def _(pe):
            def turn_x(i, n, turn):
                pe.wait_ge(S[f"x_in{n}"], turn * 16 + 16)
                wait_for(pe, S["x_lo"], i - 1)
                for k in range(DC):
                    mm = pe.transpose(tx_ps[n % 2][:, k], x[:, n, k * P:(k + 1) * P], ident[:])
                mm.then_inc(S["tx"], 1)

            def up(i, n, turn):
                pe.wait_ge(S["x_lo"], i + 1)
                pe.wait_ge(S["w1_lo"], i + 1)
                wait_for(pe, S["gelu"], i - 1)
                for k in range(DC):
                    c = slice(k * HR, (k + 1) * HR)
                    mm = product(pe, h_ps[n % 2][:], (x_hi[:, n % 2, k], x_lo[:, n % 2, k]), (w_hi[:, n % 2, c], w_lo[:, n % 2, c]),
                                 k == 0, k == DC - 1)
                mm.then_inc(S["mm1"], 1)

            def turn_h(i, n, turn):
                pe.wait_ge(S["gelu"], i + 1)
                wait_for(pe, S["h_lo"], i - 1)
                for k in range(RC):
                    mm = pe.transpose(th_ps[n % 2][:, k], h[:, n % 2, k * P:(k + 1) * P], ident[:])
                mm.then_inc(S["th"], 1)

            def down(i, n, turn):
                pe.wait_ge(S["h_lo"], i + 1)
                pe.wait_ge(S["w2_lo"], i + 1)
                wait_for(pe, S["o_ready"], i - 1)
                for k in range(RC):
                    c = slice(W1 + k * D, W1 + (k + 1) * D)
                    mm = product(pe, o_ps[n % 2][:], (ht_hi[:, n % 2, k], ht_lo[:, n % 2, k]), (w_hi[:, n % 2, c], w_lo[:, n % 2, c]),
                                 k == 0, k == RC - 1)
                mm.then_inc(S["mm2"], 1)

            software_pipeline(pe, RT, [(2, up), (1, turn_x), (3, down), (2, turn_h)], NI)



def stage_choose(nc, ins, d, keep):
    with ExitStack() as ctx:
        sb = lambda n, s, t=FP32: ctx.enter_context(nc.sbuf_tensor("s3_" + n, s, t))
        ps = lambda n, s, t=FP32: ctx.enter_context(nc.psum_tensor("s3_" + n, s, t))
        S = sems(nc, ctx, "s3_", "y_ready rec_in params_in ~rows_in dve turned turned_read nav nav_gelu logits shifted prob_e "
                 "key key_turned")
        ident = keep["ident"]
        order = keep["order"]
        rec = sb("rec", [NB, REC], I32)
        rec_f = rec[:].bitcast(FP32)
        shared = sb("shared", [NB, D])
        routed = [sb(f"routed{n}", [NB, D]) for n in range(2)]
        y = sb("y", [NB, D])
        y_t = sb("y_t", [P, DC, NB])
        wp1 = sb("wp1", [P, DC, P])
        wp2 = sb("wp2", [P, ER])
        bp1 = sb("bp1", [P, 1])
        bp2 = sb("bp2", [NB, ER])
        nav = sb("nav", [P, NB])
        number = sb("number", [NB, ER])
        batch_no = sb("batch_no", [NB, 1])
        v = sb("v", [NB, 4, ER])
        c = sb("c", [NB, 6])
        keys = sb("keys", [1, 2, NB])
        best = sb("best", [1, NB])
        key_i = sb("key_i", [1, 3, NB], I32)
        turned_ps = ps("turned", [P, DC, NB])
        nav_ps = ps("nav_ps", [P, NB])
        logit_ps = ps("logits_ps", [NB, ER])
        key_ps = ps("key_ps", [1, NB])

        block = ctx.enter_context(nc.Block())

        @block.sync
        def _(sp):
            sp.dma_start(rec[:], d["rec"][:, P - 1, :]).then_inc(S["rec_in"], 16)
            sp.dma_start(shared[:], d["shared"][:, P - 1, :]).then_inc(S["params_in"], 16)
            for dst, src in ((wp1[:], ins["wp1"]), (wp2[:], ins["wp2"]), (bp1[:], ins["bp1"]),
                             (bp2[:], ins["bp2"].partition_broadcast(NB)), (number[:], ins["c_eight"]),
                             (batch_no[:], ins["c_batch"])):
                sp.dma_start(dst, src).then_inc(S["params_in"], 16)

        @block.gpsimd
        def _(pool):
            pool.wait_ge(S["rec_in"], 16)
            for n, slot in enumerate((SLOT1, SLOT2)):
                pool.indirect_dma_start(routed[n][:], None, d["routed"],
                                        bass.IndirectOffsetOnAxis(rec[:, slot:slot + 1].bitcast(U32), 0)
                                        ).then_inc(S["rows_in"], 16)

        @block.scalar
        def _(act):
            act.wait_ge(S["nav"], 1)
            act.activation(nav[:], nav_ps[:], ACT.Gelu, bias=bp1[:]).then_inc(S["nav_gelu"], 1)
            act.wait_ge(S["shifted"], 1)
            act.activation(v[:, 1], v[:, 0], ACT.Exp, accum_out=c[:, 1:2]).then_inc(S["prob_e"], 1)

        @block.vector
        def _(dve):
            done = [0]

            def op(ins_):
                done[0] += 1
                ins_.then_inc(S["dve"], 1)
                dve.wait_ge(S["dve"], done[0])

            def signal(ins_, name):
                ins_.then_inc(S[name], 1)
                dve.wait_ge(S[name], 1)

            dve.wait_ge(S["params_in"], 16 * 7)
            dve.wait_ge(S["rows_in"], 32)
            op(dve.scalar_tensor_tensor(y[:], routed[0][:], rec_f[:, GATE1:GATE1 + 1], shared[:], ALU.mult, ALU.add))
            signal(dve.scalar_tensor_tensor(y[:], routed[1][:], rec_f[:, GATE2:GATE2 + 1], y[:], ALU.mult, ALU.add),
                   "y_ready")
            dve.wait_ge(S["turned"], 1)
            signal(dve.tensor_copy(y_t[:], turned_ps[:]), "turned_read")
            dve.wait_ge(S["logits"], 1)
            op(dve.tensor_tensor(v[:, 2], logit_ps[:], bp2[:], ALU.add))
            op(dve.tensor_reduce(c[:, 0:1], v[:, 2], AX, ALU.max))
            signal(dve.tensor_scalar(v[:, 0], v[:, 2], c[:, 0:1], None, ALU.subtract), "shifted")
            dve.wait_ge(S["prob_e"], 1)
            op(dve.reciprocal(c[:, 2:3], c[:, 1:2]))
            op(dve.tensor_scalar(v[:, 3], v[:, 1], c[:, 2:3], None, ALU.mult))
            op(dve.tensor_reduce(c[:, 3:4], v[:, 3], AX, ALU.max))
            op(dve.tensor_scalar(v[:, 2], v[:, 3], c[:, 3:4], float(ER), ALU.is_lt, ALU.mult))
            op(dve.tensor_tensor(v[:, 2], v[:, 2], number[:], ALU.add))
            op(dve.tensor_reduce(c[:, 4:5], v[:, 2], AX, ALU.min))
            signal(dve.scalar_tensor_tensor(c[:, 5:6], c[:, 4:5], float(NB), batch_no[:], ALU.mult, ALU.add), "key")
            dve.wait_ge(S["key_turned"], 1)
            op(dve.tensor_copy(keys[:, 0], key_ps[:]))
            for r in range(NB // 8):
                eight = best[:, 8 * r:8 * r + 8]
                op(dve.max(eight, keys[:, r % 2]))
                if r < NB // 8 - 1:
                    op(dve.match_replace(keys[:, 1 - r % 2], eight, keys[:, r % 2], -1.0))
            op(dve.tensor_copy(key_i[:, 0], best[:]))
            op(dve.tensor_scalar(order[:, 0], key_i[:, 0], 5, None, ALU.arith_shift_right))
            op(dve.tensor_scalar(order[:, 1], key_i[:, 0], NB - 1, None, ALU.bitwise_and))
            op(dve.memset(order[:, 2], 1))
            op(dve.tensor_tensor(order[:, 2, 1:NB], order[:, 0, 1:NB], order[:, 0, 0:NB - 1], ALU.not_equal))

        @block.tensor
        def _(pe):
            pe.wait_ge(S["y_ready"], 1)
            for k in range(DC):
                mm = pe.transpose(turned_ps[:, k], y[:, k * P:(k + 1) * P], ident[0:NB, 0:NB])
            mm.then_inc(S["turned"], 1)
            pe.wait_ge(S["turned_read"], 1)
            for k in range(DC):
                mm = pe.matmul(nav_ps[:], wp1[:, k], y_t[:, k], start=(k == 0), stop=(k == DC - 1))
            mm.then_inc(S["nav"], 1)
            pe.wait_ge(S["nav_gelu"], 1)
            pe.matmul(logit_ps[:], nav[:], wp2[:], start=True, stop=True).then_inc(S["logits"], 1)
            pe.wait_ge(S["key"], 1)
            pe.transpose(key_ps[:], c[:, 5:6], ident[0:NB, 0:NB]).then_inc(S["key_turned"], 1)



def stage_ffn(nc, ins, d, keep):
    with ExitStack() as ctx:
        sb = lambda n, s, t=FP32: ctx.enter_context(nc.sbuf_tensor("s4_" + n, s, t))
        ps = lambda n, s, t=FP32: ctx.enter_context(nc.psum_tensor("s4_" + n, s, t))
        S = sems(nc, ctx, "s4_", "params_in rec_in hrec_in shared_in x_in ~routed1_in ~routed2_in b1_in b2_in w1_in "
                 "w2_in0 w2_in1 w1_hi w1_lo w2_hi w2_lo part_y y base x_plus_y bo_scaled ty y_hi y_lo h_ps h_add gelu th h_hi "
                 "h_lo mm2 z_add tz z_hi z_lo mmo x1_part x1 x1_out prev_in dx k_part xk r_part xr ~xk_sent txr xr_hi "
                 "xr_lo mmr r_ready r_out")
        ident = keep["ident"]
        order = keep["order"]
        rec = sb("rec", [P, REC], I32)
        rec_f = rec[:].bitcast(FP32)
        hrec = sb("hrec", [P, REC], I32)
        shared = sb("shared", [P, D])
        x = sb("x", [P, D])
        routed = [sb(f"routed{n}", [P, D]) for n in range(2)]
        y_part = sb("y_part", [P, D])
        y = sb("y", [P, D])
        base_part = sb("base_part", [P, D])
        base = sb("base", [P, 2, D])
        b1 = sb("b1", [P, HS])
        b2 = sb("b2", [P, D])
        bo = sb("bo", [P, D])
        maa_k = sb("maa_k", [P, D])
        maa_r = sb("maa_r", [P, D])
        w1_raw = sb("w1_raw", [P, DC, HS])
        w2_raw = sb("w2_raw", [P, DC, HS])
        w1_hi = sb("w1_hi", [P, DC, HS], FP32R)
        w1_lo = sb("w1_lo", [P, DC, HS], FP32R)
        w2_hi = sb("w2_hi", [P, DC, HS], FP32R)
        w2_lo = sb("w2_lo", [P, DC, HS], FP32R)
        wo_hi, wo_lo = keep["wo_hi"], keep["wo_lo"]
        y_hi = sb("y_hi", [P, DC, P], FP32R)
        y_lo = sb("y_lo", [P, DC, P], FP32R)
        h_pre = sb("h_pre", [P, 2, D])
        h = sb("h", [P, 2, D])
        ht_hi = sb("ht_hi", [P, HC, P], FP32R)
        ht_lo = sb("ht_lo", [P, HC, P], FP32R)
        z = sb("z", [P, D])
        z_hi = sb("z_hi", [P, DC, P], FP32R)
        z_lo = sb("z_lo", [P, DC, P], FP32R)
        x1 = sb("x1", [P, D])
        prev = sb("prev", [P, D])
        dx = sb("dx", [P, D])
        k_part = sb("k_part", [P, D])
        xk = sb("xk", [P, D])
        xr = sb("xr", [P, D])
        xr_hi = sb("xr_hi", [P, DC, P], FP32R)
        xr_lo = sb("xr_lo", [P, DC, P], FP32R)
        r = sb("r", [P, D])
        h_ps = [ps(f"h_ps{n}", [P, D]) for n in range(2)]
        th_ps = [ps(f"th_ps{n}", [P, DC, P]) for n in range(2)]
        ty_ps = ps("ty_ps", [P, DC, P])
        tz_ps = ps("tz_ps", [P, DC, P])
        z_ps = ps("z_ps", [P, D])
        square_ps = ps("square_ps", [P, D])

        block = ctx.enter_context(nc.Block())
        w2_chunk = lambda w, k: w[:, k // 2, (k % 2) * D:(k % 2 + 1) * D]

        @block.sync
        def _(sp):
            for dst, src in ((bo, "bo"), (maa_k, "maa_k"), (maa_r, "maa_r")):
                sp.dma_start(dst[:], ins[src].partition_broadcast(P)).then_inc(S["params_in"], 16)

            def batch(i):
                return sp.value_load(order[0:1, 1, bass.ds(i, 1)], min_val=0, max_val=NB - 1)

            def expert(i):
                return sp.value_load(order[0:1, 0, bass.ds(i, 1)], min_val=0, max_val=ER - 1)

            def is_new(i):
                return sp.value_load(order[0:1, 2, bass.ds(i, 1)], min_val=0, max_val=1) > 0

            def load_rec(i):
                b = batch(i)
                wait_for(sp, S["y"], i)
                sp.dma_start(rec[:], d["rec"][b]).then_inc(S["rec_in"], 16)
                sp.dma_start(shared[:], d["shared"][b]).then_inc(S["shared_in"], 16)

            def load_x(i):
                b = batch(i)
                wait_apart(sp, S["base"], i)
                sp.dma_start(x[:], ins["x_rows"].rearrange("(b p) n -> b p n", p=P)[b]).then_inc(S["x_in"], 16)

            def load_w1(i):
                e, new = expert(i), is_new(i)
                wait_apart(sp, S["w1_lo"], i * DC)
                sp.dma_start(w1_raw[:], ins["w1"][e], cond=new).then_inc(S["w1_in"], 16)

            def load_w2(half):
                def stage(i):
                    e, new = expert(i), is_new(i)
                    c = slice(half * DC // 2, (half + 1) * DC // 2)
                    wait_apart(sp, S["w2_lo"], i * DC - (1 - half) * DC // 2)
                    sp.dma_start(w2_raw[:, c], ins["w2"][e, :, c], cond=new).then_inc(S[f"w2_in{half}"], 16)
                return stage

            def load_b1(i):
                e = expert(i)
                wait_for(sp, S["h_add"], 2 * i)
                sp.dma_start(b1[:], ins["b1"][e].partition_broadcast(P)).then_inc(S["b1_in"], 16)

            def load_b2(i):
                e = expert(i)
                wait_for(sp, S["z_add"], i)
                sp.dma_start(b2[:], ins["b2"][e].partition_broadcast(P)).then_inc(S["b2_in"], 16)

            def store_x1(i):
                b = batch(i)
                wait_apart(sp, S["x1"], i + 1)
                wait_apart(sp, S["dx"], i)
                sp.dma_start(prev[1:P], x1[0:P - 1]).then_inc(S["prev_in"], 16)
                sp.dma_start(prev[0:1], ins["cond"][bass.ds(b, 1)]).then_inc(S["prev_in"], 16)
                sp.dma_start(d["x1"][b], x1[:]).then_inc(S["x1_out"], 16)
                wait_apart(sp, S["xk_sent"], i * 16)
                sp.dma_start(hrec[:], d["rec"][b]).then_inc(S["hrec_in"], 16)

            def store_r(i):
                b = batch(i)
                sp.wait_ge(S["r_ready"], i + 1)
                sp.dma_start(d["r"][b], r[:]).then_inc(S["r_out"], 16)

            software_pipeline(sp, NB, [(2, load_b2), (1, load_w1), (5, store_r), (0, load_rec), (1, load_w2(0)),
                                       (1, load_b1), (3, store_x1), (0, load_x), (1, load_w2(1))])
            sp.wait_ge(S["r_out"], 16 * NB)

        @block.gpsimd
        def _(pool):
            def gather(i):
                pool.wait_ge(S["rec_in"], i * 16 + 16)
                for n, slot in enumerate((SLOT1, SLOT2)):
                    wait_apart(pool, S[("part_y", "y")[n]], i)
                    pool.indirect_dma_start(routed[n][:], None, d["routed"],
                                            bass.IndirectOffsetOnAxis(rec[:, slot:slot + 1].bitcast(U32), 0)
                                            ).then_inc(S[f"routed{n + 1}_in"], 16)

            def add_base(i):
                pool.wait_ge(S["x_in"], i * 16 + 16)
                pool.wait_ge(S["y"], i + 1)
                pool.tensor_tensor(base_part[:], x[:], y[:], ALU.add).then_inc(S["x_plus_y"], 1)
                pool.wait_ge(S["x_plus_y"], i + 1)
                wait_for(pool, S["x1"], i - 1)
                pool.tensor_tensor(base[:, i % 2], base_part[:], bo[:], ALU.add).then_inc(S["base"], 1)

            def mix(i):
                pool.wait_ge(S["prev_in"], i * 32 + 32)
                pool.tensor_tensor(dx[:], prev[:], x1[:], ALU.subtract).then_inc(S["dx"], 1)
                pool.wait_ge(S["dx"], i + 1)
                pool.tensor_tensor(k_part[:], dx[:], maa_r[:], ALU.mult).then_inc(S["r_part"], 1)
                pool.wait_ge(S["r_part"], i + 1)
                wait_for(pool, S["txr"], i)
                pool.tensor_tensor(xr[:], k_part[:], x1[:], ALU.add).then_inc(S["xr"], 1)
                pool.wait_ge(S["xr"], i + 1)
                pool.tensor_tensor(k_part[:], dx[:], maa_k[:], ALU.mult).then_inc(S["k_part"], 1)
                pool.wait_ge(S["k_part"], i + 1)
                wait_for(pool, S["xk_sent"], i * 16)
                pool.tensor_tensor(xk[:], k_part[:], x1[:], ALU.add).then_inc(S["xk"], 1)
                pool.wait_ge(S["hrec_in"], i * 16 + 16)
                wait_apart(pool, S["xk"], i + 1)
                pool.indirect_dma_start(d["hash_in"], bass.IndirectOffsetOnAxis(hrec[:, SLOTH:SLOTH + 1].bitcast(U32), 0),
                                        xk[:], None, bounds_check=NTOK - 1, oob_is_err=False).then_inc(S["xk_sent"], 16)

            pool.wait_ge(S["params_in"], 48)
            pool.tensor_scalar(bo[:], bo[:], 0.3, None, ALU.mult).then_inc(S["bo_scaled"], 1)
            pool.wait_ge(S["bo_scaled"], 1)
            software_pipeline(pool, NB, [(0, gather), (1, add_base), (3, mix)])
            pool.wait_ge(S["xk_sent"], 16 * NB)

        @block.scalar
        def _(act):
            def split_w(name, raw, hi, mm, per, c0, c1):
                def stage(i):
                    if name == "w2":
                        act.wait_ge(S[f"w2_in{c0 // 2}"], i * 16 + 16)
                    elif c0 == 0:
                        act.wait_ge(S["w1_in"], i * 16 + 16)
                    if c0 == 0:
                        wait_for(act, S[mm], i * per)
                    for c in range(c0, c1):
                        act.activation(hi[:, c], raw[:, c], ACT.Copy).then_inc(S[name + "_hi"], 1)
                return stage

            def gelu(n):
                def stage(i):
                    act.wait_ge(S["h_add"], 2 * i + n + 1)
                    wait_for(act, S["th"], 2 * i + n - 1)
                    act.activation(h[:, n], h_pre[:, n], ACT.Gelu).then_inc(S["gelu"], 1)
                return stage

            def h_hi(n):
                def stage(i):
                    act.wait_ge(S["th"], 2 * i + n + 1)
                    wait_for(act, S["mm2"], i)
                    act.activation(ht_hi[:, n * DC:(n + 1) * DC], th_ps[n][:], ACT.Copy).then_inc(S["h_hi"], 1)
                return stage

            def part_hi(dst, src, turned, used, name):
                def stage(i):
                    act.wait_ge(S[turned], i + 1)
                    wait_for(act, S[used], i if used != "h_ps" else 2 * i)
                    act.activation(dst[:], src[:], ACT.Copy).then_inc(S[name], 1)
                return stage

            def copy_r(i):
                act.wait_ge(S["mmr"], i + 1)
                wait_for(act, S["r_out"], i * 16)
                act.activation(r[:], square_ps[:], ACT.Copy).then_inc(S["r_ready"], 1)

            w1 = lambda c0, c1: split_w("w1", w1_raw, w1_hi, "h_ps", 2, c0, c1)
            w2 = lambda c0, c1: split_w("w2", w2_raw, w2_hi, "mm2", 1, c0, c1)
            software_pipeline(act, NB, [
                (1, w2(0, 2)), (4, copy_r), (1, gelu(0)), (2, part_hi(z_hi, tz_ps, "tz", "mmo", "z_hi")), (1, gelu(1)),
                (1, h_hi(0)), (1, w2(2, 3)), (1, h_hi(1)), (3, part_hi(xr_hi, tz_ps, "txr", "mmr", "xr_hi")),
                (1, w2(3, 4)), (0, w1(0, 2)), (0, part_hi(y_hi, ty_ps, "ty", "h_ps", "y_hi")), (0, w1(2, 4))])

        @block.vector
        def _(dve):
            def split_w(name, raw, hi, lo, c0, c1):
                def stage(i):
                    for c in range(c0, c1):
                        dve.wait_ge(S[name + "_hi"], i * DC + c + 1)
                        dve.tensor_tensor(lo[:, c], raw[:, c], hi[:, c], ALU.subtract).then_inc(S[name + "_lo"], 1)
                return stage

            def h_add(n):
                def stage(i):
                    dve.wait_ge(S["h_ps"], 2 * i + n + 1)
                    if n == 0:
                        dve.wait_ge(S["b1_in"], i * 16 + 16)
                    wait_for(dve, S["gelu"], 2 * i + n - 1)
                    dve.tensor_tensor(h_pre[:, n], h_ps[n][:], b1[:, n * D:(n + 1) * D],
                                      ALU.add).then_inc(S["h_add"], 1)
                return stage

            def h_lo(n):
                def stage(i):
                    dve.wait_ge(S["h_hi"], 2 * i + n + 1)
                    dve.tensor_tensor(ht_lo[:, n * DC:(n + 1) * DC], th_ps[n][:], ht_hi[:, n * DC:(n + 1) * DC],
                                      ALU.subtract).then_inc(S["h_lo"], 1)
                return stage

            def part_lo(dst, src, hi, hi_done, name):
                def stage(i):
                    dve.wait_ge(S[hi_done], i + 1)
                    dve.tensor_tensor(dst[:], src[:], hi[:], ALU.subtract).then_inc(S[name], 1)
                return stage

            def z_add(i):
                dve.wait_ge(S["mm2"], i + 1)
                dve.wait_ge(S["b2_in"], i * 16 + 16)
                wait_for(dve, S["tz"], i)
                dve.tensor_tensor(z[:], z_ps[:], b2[:], ALU.add).then_inc(S["z_add"], 1)

            def x1_(i):
                dve.wait_ge(S["mmo"], i + 1)
                dve.wait_ge(S["base"], i + 1)
                wait_for(dve, S["xk"], i)
                wait_for(dve, S["x1_out"], i * 16)
                dve.scalar_tensor_tensor(x1[:], square_ps[:], 0.3, base[:, i % 2], ALU.mult, ALU.add).then_inc(S["x1"], 1)

            def combine(i):
                dve.wait_ge(S["rec_in"], i * 16 + 16)
                dve.wait_ge(S["shared_in"], i * 16 + 16)
                dve.wait_ge(S["routed1_in"], i * 16 + 16)
                dve.scalar_tensor_tensor(y_part[:], routed[0][:], rec_f[:, GATE1:GATE1 + 1], shared[:],
                                         ALU.mult, ALU.add).then_inc(S["part_y"], 1)
                dve.wait_ge(S["part_y"], i + 1)
                dve.wait_ge(S["routed2_in"], i * 16 + 16)
                wait_for(dve, S["ty"], i)
                wait_for(dve, S["x_plus_y"], i)
                dve.scalar_tensor_tensor(y[:], routed[1][:], rec_f[:, GATE2:GATE2 + 1], y_part[:],
                                         ALU.mult, ALU.add).then_inc(S["y"], 1)

            w1 = lambda c0, c1: split_w("w1", w1_raw, w1_hi, w1_lo, c0, c1)
            w2 = lambda c0, c1: split_w("w2", w2_raw, w2_hi, w2_lo, c0, c1)
            software_pipeline(dve, NB, [
                (2, w2(0, 2)), (2, h_add(0)), (1, combine), (3, part_lo(z_lo, tz_ps, z_hi, "z_hi", "z_lo")), (2, h_add(1)),
                (2, h_lo(0)), (3, x1_), (2, w2(2, 3)), (2, h_lo(1)),
                (4, part_lo(xr_lo, tz_ps, xr_hi, "xr_hi", "xr_lo")), (2, w2(3, 4)), (1, w1(0, 2)), (1, part_lo(y_lo, ty_ps, y_hi, "y_hi", "y_lo")),
                (1, w1(2, 4)), (2, z_add)])

        @block.tensor
        def _(pe):
            def up(n):
                def stage(i):
                    if n == 0:
                        pe.wait_ge(S["y_lo"], i + 1)
                    wait_for(pe, S["h_add"], 2 * i + n - 1)
                    for k in range(DC):
                        if n == 0:
                            pe.wait_ge(S["w1_lo"], i * DC + k + 1)
                        mm = product(pe, h_ps[n][:], (y_hi[:, k], y_lo[:, k]),
                                     (w1_hi[:, k, n * D:(n + 1) * D], w1_lo[:, k, n * D:(n + 1) * D]),
                                     k == 0, k == DC - 1)
                    mm.then_inc(S["h_ps"], 1)
                return stage

            def turn_h(n):
                def stage(i):
                    pe.wait_ge(S["gelu"], 2 * i + n + 1)
                    wait_for(pe, S["h_lo"], 2 * i + n - 1)
                    for k in range(DC):
                        mm = pe.transpose(th_ps[n][:, k], h[:, n, k * P:(k + 1) * P], ident[:])
                    mm.then_inc(S["th"], 1)
                return stage

            def turn(src, ready, dst, free, free_lag, name):
                def stage(i):
                    pe.wait_ge(S[ready], i + 1)
                    wait_for(pe, S[free], min(i - free_lag, NB) if isinstance(i, int) else i - free_lag)
                    for k in range(DC):
                        mm = pe.transpose(dst[:, k], src[:, k * P:(k + 1) * P], ident[:])
                    mm.then_inc(S[name], 1)
                return stage

            def down(i):
                wait_for(pe, S["z_add"], i)
                for k in range(HC):
                    if k % DC == 0:
                        pe.wait_ge(S["h_lo"], 2 * i + k // DC + 1)
                    if k % 2 == 0:
                        pe.wait_ge(S["w2_lo"], i * DC + k // 2 + 1)
                    mm = product(pe, z_ps[:], (ht_hi[:, k], ht_lo[:, k]), (w2_chunk(w2_hi, k), w2_chunk(w2_lo, k)),
                                 k == 0, k == HC - 1)
                mm.then_inc(S["mm2"], 1)

            def square(n, parts, name):
                for k in range(DC):
                    mm = product(pe, square_ps[:], (parts[0][:, k], parts[1][:, k]), (wo_hi[:, n, k], wo_lo[:, n, k]),
                                 k == 0, k == DC - 1)
                mm.then_inc(S[name], 1)

            def times_wo(i):
                pe.wait_ge(S["z_lo"], i + 1)
                wait_for(pe, S["r_ready"], i - 1)
                square(0, (z_hi, z_lo), "mmo")

            def receptance(i):
                pe.wait_ge(S["xr_lo"], i + 1)
                pe.wait_ge(S["x1"], min(i + 2, NB) if isinstance(i, int) else i + 2)
                square(1, (xr_hi, xr_lo), "mmr")

            software_pipeline(pe, NB, [
                (1, up(0)), (2, turn(z, "z_add", tz_ps, "xr_lo", 1, "tz")), (1, up(1)), (1, turn_h(0)),
                (2, times_wo), (1, turn_h(1)),
                (3, turn(xr, "xr", tz_ps, "z_lo", -2, "txr")), (0, turn(y, "y", ty_ps, "y_lo", 0, "ty")),
                (1, down), (3, receptance)])



def stage_hashed(nc, ins, d, keep):
    with ExitStack() as ctx:
        sb = lambda n, s, t=FP32: ctx.enter_context(nc.sbuf_tensor("s5_" + n, s, t))
        ps = lambda n, s, t=FP32: ctx.enter_context(nc.psum_tensor("s5_" + n, s, t))
        S = sems(nc, ctx, "s5_", "x_in0 x_in1 w1_in w2_in w1_hi w1_lo w2_hi w2_lo tx0 tx1 x_hi0 x_hi1 x_lo0 x_lo1 "
                 "g_in g_hi g_lo h_ps pos relu th h_hi h_lo mm2 o_ready0 o_ready1 o_out0 o_out1")
        ident = keep["ident"]
        GP = 3 * DC * D // EH
        g_raw = sb("g_raw", [P, GP])
        part = lambda w, e: w[:].rearrange("p g k n -> p (g k n)")[:, bass.ds(e * GP, GP)]
        w1_raw = sb("w1_raw", [P, DC, HS])
        w2_raw = sb("w2_raw", [P, DC, HS])
        w1_hi = sb("w1_hi", [P, DC, HS], FP32R)
        w1_lo = sb("w1_lo", [P, DC, HS], FP32R)
        w2_hi = sb("w2_hi", [P, DC, HS], FP32R)
        w2_lo = sb("w2_lo", [P, DC, HS], FP32R)
        x = sb("x", [P, 2, D])
        x_hi = sb("x_hi", [P, 2, DC, P], FP32R)
        x_lo = sb("x_lo", [P, 2, DC, P], FP32R)
        pos = sb("pos", [P, 2, D])
        h = sb("h", [P, 2, 2, D])
        ht_hi = sb("ht_hi", [P, 2, HC, P], FP32R)
        ht_lo = sb("ht_lo", [P, 2, HC, P], FP32R)
        o_sb = sb("o_sb", [P, 2, D])
        h_ps = [ps(f"h_ps{n}", [P, D]) for n in range(2)]
        th_ps = [ps(f"th_ps{n}", [P, DC, P]) for n in range(2)]
        tx_ps = [ps(f"tx_ps{n}", [P, DC, P]) for n in range(2)]
        o_ps = [ps(f"o_ps{n}", [P, D]) for n in range(2)]
        w2_chunk = lambda w, k: w[:, k // 2, (k % 2) * D:(k % 2 + 1) * D]

        block = ctx.enter_context(nc.Block())

        @block.sync
        def _(sp):
            def load_x(m):
                def stage(e):
                    wait_for(sp, S[f"tx{m}"], e)
                    sp.dma_start(x[:, m], d["hash_in"][bass.ds(e * CAP + m * P, P)]).then_inc(S[f"x_in{m}"], 16)
                return stage

            def load_w(name, raw):
                def stage(e):
                    wait_for(sp, S[name + "_lo"], e * DC)
                    sp.dma_start(raw[:], ins[name + "h"][e]).then_inc(S[name + "_in"], 16)
                return stage

            def store(m):
                def stage(e):
                    sp.wait_ge(S[f"o_ready{m}"], e + 1)
                    sp.dma_start(d["hash_out"][bass.ds(e * CAP + m * P, P)], o_sb[:, m]).then_inc(S[f"o_out{m}"], 16)
                return stage

            def load_g(e):
                wait_for(sp, S["g_lo"], e)
                sp.dma_start(g_raw[:], ins["gate_x"][e]).then_inc(S["g_in"], 16)

            software_pipeline(sp, EH, [(0, load_w("w1", w1_raw)), (0, load_x(0)), (0, load_x(1)), (2, store(1)),
                                       (0, load_w("w2", w2_raw)), (1, store(0)), (1, load_g)])
            for m in range(2):
                sp.wait_ge(S[f"o_out{m}"], 16 * EH)

        @block.scalar
        def _(act):
            def split_w(name, raw, hi, used, per, c0, c1):
                def stage(e):
                    if c0 == 0:
                        act.wait_ge(S[name + "_in"], e * 16 + 16)
                        wait_for(act, S[used], e * per)
                    for c in range(c0, c1):
                        act.activation(hi[:, c], raw[:, c], ACT.Copy).then_inc(S[name + "_hi"], 1)
                return stage

            def g_hi(e):
                wait_apart(act, S["g_in"], e * 16 + 16)
                act.activation(part(keep["wx_hi"], e), g_raw[:], ACT.Copy).then_inc(S["g_hi"], 1)

            def x_hi_(m):
                def stage(e):
                    act.wait_ge(S[f"tx{m}"], e + 1)
                    wait_for(act, S["h_ps"], 4 * e - 2 + 2 * m)
                    act.activation(x_hi[:, m], tx_ps[m][:], ACT.Copy).then_inc(S[f"x_hi{m}"], 1)
                return stage

            def h_hi(m, n):
                def stage(e):
                    act.wait_ge(S["th"], 4 * e + 2 * m + n + 1)
                    wait_for(act, S["mm2"], 2 * e + m - 1)
                    act.activation(ht_hi[:, m, n * DC:(n + 1) * DC], th_ps[n][:], ACT.Copy).then_inc(S["h_hi"], 1)
                return stage

            def relu(m, n):
                def stage(e):
                    t = 4 * e + 2 * m + n
                    act.wait_ge(S["h_ps"], t + 1)
                    wait_for(act, S["relu"], t - 1)
                    act.activation(pos[:, n], h_ps[n][:], ACT.Relu).then_inc(S["pos"], 1)
                return stage

            def out(m):
                def stage(e):
                    act.wait_ge(S["mm2"], 2 * e + m + 1)
                    wait_for(act, S[f"o_out{m}"], e * 16)
                    act.activation(o_sb[:, m], o_ps[m][:], ACT.Copy).then_inc(S[f"o_ready{m}"], 1)
                return stage

            w1 = lambda c0, c1: split_w("w1", w1_raw, w1_hi, "h_ps", 4, c0, c1)
            w2 = lambda c0, c1: split_w("w2", w2_raw, w2_hi, "mm2", 2, c0, c1)
            software_pipeline(act, EH, [
                (2, out(1)), (1, w2(0, 2)), (1, relu(0, 0)), (1, w2(2, 3)), (1, relu(0, 1)), (1, w2(3, 4)),
                (1, relu(1, 0)), (1, h_hi(0, 0)), (1, h_hi(0, 1)), (1, relu(1, 1)), (0, x_hi_(0)), (1, h_hi(1, 0)),
                (0, w1(0, 4)), (2, g_hi), (1, out(0)), (1, h_hi(1, 1)), (0, x_hi_(1))])

        @block.vector
        def _(dve):
            def split_w(name, raw, hi, lo, c0, c1):
                def stage(e):
                    for c in range(c0, c1):
                        dve.wait_ge(S[name + "_hi"], e * DC + c + 1)
                        dve.tensor_tensor(lo[:, c], raw[:, c], hi[:, c], ALU.subtract).then_inc(S[name + "_lo"], 1)
                return stage

            def g_lo(e):
                dve.wait_ge(S["g_hi"], e + 1)
                dve.tensor_tensor(part(keep["wx_lo"], e), g_raw[:], part(keep["wx_hi"], e),
                                  ALU.subtract).then_inc(S["g_lo"], 1)

            def relu2(m, n):
                def stage(e):
                    t = 4 * e + 2 * m + n
                    dve.wait_ge(S["pos"], t + 1)
                    wait_for(dve, S["th"], t - 3)
                    dve.tensor_tensor(h[:, m, n], pos[:, n], h_ps[n][:], ALU.mult).then_inc(S["relu"], 1)
                return stage

            def h_lo(m, n):
                def stage(e):
                    dve.wait_ge(S["h_hi"], 4 * e + 2 * m + n + 1)
                    dve.tensor_tensor(ht_lo[:, m, n * DC:(n + 1) * DC], th_ps[n][:], ht_hi[:, m, n * DC:(n + 1) * DC],
                                      ALU.subtract).then_inc(S["h_lo"], 1)
                return stage

            def x_lo_(m):
                def stage(e):
                    dve.wait_ge(S[f"x_hi{m}"], e + 1)
                    dve.tensor_tensor(x_lo[:, m], tx_ps[m][:], x_hi[:, m], ALU.subtract).then_inc(S[f"x_lo{m}"], 1)
                return stage

            w1 = lambda c0, c1: split_w("w1", w1_raw, w1_hi, w1_lo, c0, c1)
            w2 = lambda c0, c1: split_w("w2", w2_raw, w2_hi, w2_lo, c0, c1)
            software_pipeline(dve, EH, [
                (1, w2(0, 2)), (1, relu2(0, 0)), (1, w2(2, 3)), (1, relu2(0, 1)), (1, w2(3, 4)), (1, relu2(1, 0)),
                (1, h_lo(0, 0)), (1, h_lo(0, 1)), (1, relu2(1, 1)), (0, x_lo_(0)), (1, h_lo(1, 0)), (0, w1(0, 4)),
                (2, g_lo), (1, h_lo(1, 1)), (0, x_lo_(1))])

        @block.tensor
        def _(pe):
            def turn_x(m):
                def stage(e):
                    pe.wait_ge(S[f"x_in{m}"], e * 16 + 16)
                    wait_for(pe, S[f"x_lo{m}"], e)
                    for k in range(DC):
                        mm = pe.transpose(tx_ps[m][:, k], x[:, m, k * P:(k + 1) * P], ident[:])
                    mm.then_inc(S[f"tx{m}"], 1)
                return stage

            def up(m, n):
                def stage(e):
                    if n == 0:
                        pe.wait_ge(S[f"x_lo{m}"], e + 1)
                        pe.wait_ge(S["w1_lo"], e * DC + DC)
                    wait_for(pe, S["relu"], 4 * e + 2 * m + n - 1)
                    for k in range(DC):
                        mm = product(pe, h_ps[n][:], (x_hi[:, m, k], x_lo[:, m, k]),
                                     (w1_hi[:, k, n * D:(n + 1) * D], w1_lo[:, k, n * D:(n + 1) * D]),
                                     k == 0, k == DC - 1)
                    mm.then_inc(S["h_ps"], 1)
                return stage

            def turn_h(m, n):
                def stage(e):
                    t = 4 * e + 2 * m + n
                    pe.wait_ge(S["relu"], t + 1)
                    wait_for(pe, S["h_lo"], t - 1)
                    for k in range(DC):
                        mm = pe.transpose(th_ps[n][:, k], h[:, m, n, k * P:(k + 1) * P], ident[:])
                    mm.then_inc(S["th"], 1)
                return stage

            def down(m):
                def stage(e):
                    pe.wait_ge(S["w2_lo"], e * DC + DC)
                    wait_for(pe, S[f"o_ready{m}"], e)
                    for k in range(HC):
                        if k % DC == 0:
                            pe.wait_ge(S["h_lo"], 4 * e + 2 * m + k // DC + 1)
                        mm = product(pe, o_ps[m][:], (ht_hi[:, m, k], ht_lo[:, m, k]),
                                     (w2_chunk(w2_hi, k), w2_chunk(w2_lo, k)), k == 0, k == HC - 1)
                    mm.then_inc(S["mm2"], 1)
                return stage

            software_pipeline(pe, EH, [
                (1, up(0, 0)), (1, up(0, 1)), (1, up(1, 0)), (1, turn_h(0, 0)), (1, turn_h(0, 1)), (1, up(1, 1)),
                (0, turn_x(0)), (1, turn_h(1, 0)), (1, down(0)), (1, turn_h(1, 1)), (0, turn_x(1)), (1, down(1))])



def stage_recurrent(nc, ins, d, keep, out):
    with ExitStack() as ctx:
        sb = lambda n, s, t=FP32: ctx.enter_context(nc.sbuf_tensor("s6_" + n, s, t))
        ps = lambda n, s, t=FP32: ctx.enter_context(nc.psum_tensor("s6_" + n, s, t))
        S = sems(nc, ctx, "s6_", "params_in w_in wo_in wo_hi wo_lo w_hi w_lo rec_in ~y_in r_in r_sig x2 tx x_raw x_hi x_lo xpart "
                 "gates added acted ig fc c tc c_hi c_lo uo_in ct_ready const_ps const "
                 "p_hi p_lo p_ps p_add p_tanh x1_in0 x1_in1 x1_in2 x1_in3 p_out out0 out1 out2 out3")
        NG = 3
        G_G, G_I, G_F = range(NG)
        ident = keep["ident"]
        NU = 2 * NG
        wx_hi, wx_lo = keep["wx_hi"], keep["wx_lo"]
        w_hi = sb("w_hi", [P, NG, DC, D], FP32R)
        w_lo = sb("w_lo", [P, NG, DC, D], FP32R)
        unit = lambda w, u: w[:].rearrange("p m k n -> p (m k n)")[:, u * HS:(u + 1) * HS]
        raw = sb("raw", [P, 2, HS])
        uo = raw[:].rearrange("p u (k n) -> p (u k) n", n=D)
        wo_hi, wo_lo = wx_hi[:, 0], wx_lo[:, 0]
        x2t = sb("x2t", [P, NB, DC, P])
        staged = x2t[:, NB - 2 * NU:NB].rearrange("p (u i) k n -> p u (i k n)", u=NU)
        bias = sb("bias", [P, NG, D])
        bo = sb("bo", [P, D])
        gate = sb("gate", [P, NG, D])
        c = sb("c", [P, D])
        c_hi = sb("c_hi", [P, DC, P], FP32R)
        c_lo = sb("c_lo", [P, DC, P], FP32R)
        x_hi = sb("x_hi", [P, 2, DC, P], FP32R)
        x_lo = sb("x_lo", [P, 2, DC, P], FP32R)
        rec = sb("rec", [P, REC], I32)
        y = sb("y", [P, D])
        r = sb("r", [P, D])
        x2 = sb("x2", [P, D])
        ct = x2
        g_ps = [[ps(f"g{n}_{g}", [P, D]) for g in range(NG)] for n in range(2)]
        tx_ps = ps("tx_ps", [P, DC, P])
        tc_ps = ps("tc_ps", [P, DC, P])

        NO = 4
        c_x1 = [bias[:, 0], bias[:, 1], bias[:, 2], gate[:, 0]]
        p_out = [r[:], y[:], gate[:, 1], c[:]]
        p_sum = [x2[:], gate[:, 2]]

        block = ctx.enter_context(nc.Block())

        @block.sync
        def _(sp):
            def load(i):
                wait_for(sp, S["x2"], i)
                sp.dma_start(rec[:], d["rec"][i]).then_inc(S["rec_in"], 16)
                sp.dma_start(r[:], d["r"][i]).then_inc(S["r_in"], 16)

            load(0)
            sp.dma_start(c[:], ins["in_c"].partition_broadcast(P)).then_inc(S["params_in"], 16)
            for g in range(NG):
                sp.dma_start(bias[:, g], ins["gate_bias"][g].partition_broadcast(P)).then_inc(S["params_in"], 16)
            sp.dma_start(bo[:], ins["bo_r"].partition_broadcast(P)).then_inc(S["params_in"], 16)

            sp.dma_start(staged, ins["gate_w"][0:NU].rearrange("u p n -> p u n")).then_inc(S["w_in"], 16)
            sp.dma_start(raw[:], ins["gate_w"][NU:NU + 2].rearrange("u p n -> p u n")).then_inc(S["wo_in"], 16)
            with sp.Fori(1, NB) as i:
                load(i)
            sp.wait_ge(S["wo_lo"], 1)
            sp.dma_start(raw[:].rearrange("p u n -> p (u n)"), ins["uo"]).then_inc(S["uo_in"], 16)

            def load_x1(i, n, turn):
                wait_for(sp, S["p_out"], i - NO + 1)
                sp.dma_start(c_x1[n], d["x1"][i]).then_inc(S[f"x1_in{n}"], 16)

            def store(i, n, turn):
                sp.wait_ge(S["p_out"], i + 1)
                sp.dma_start(out[i], p_out[n]).then_inc(S[f"out{n}"], 16)

            sp.wait_ge(S["c"], NB + 1)
            software_pipeline(sp, NB, [(0, load_x1), (3, store)], NO)
            for n in range(NO):
                sp.wait_ge(S[f"out{n}"], 16 * NB // NO)

        @block.gpsimd
        def _(pool):
            def fetch(i):
                pool.wait_ge(S["rec_in"], i * 16 + 16)
                wait_apart(pool, S["x2"], i)
                pool.indirect_dma_start(y[:], None, d["hash_out"],
                                        bass.IndirectOffsetOnAxis(rec[:, SLOTH:SLOTH + 1].bitcast(U32), 0)
                                        ).then_inc(S["y_in"], 16)
                pool.wait_ge(S["y_in"], i * 16 + 16)
                pool.wait_ge(S["r_sig"], i + 1)
                wait_for(pool, S["tx"], i)
                pool.tensor_tensor(x2[:], y[:], r[:], ALU.mult).then_inc(S["x2"], 1)

            fetch(0)
            with pool.Fori(1, NB) as i:
                fetch(i)

        @block.scalar
        def _(act):
            def r_sigmoid(i):
                act.wait_ge(S["r_in"], i * 16 + 16)
                act.activation(r[:], r[:], ACT.Sigmoid).then_inc(S["r_sig"], 1)

            def x_parts(i):
                act.wait_ge(S["tx"], i + 1)
                act.activation(x2t[:, i], tx_ps[:], ACT.Copy).then_inc(S["x_raw"], 1)
                act.wait_ge(S["x_raw"], i + 1)
                wait_apart(act, S["xpart"], i * NG)
                act.activation(x_hi[:, 0], x2t[:, i], ACT.Copy).then_inc(S["x_hi"], 1)

            def gates(i, n, turn):
                for g, f in ((G_G, ACT.Tanh), (G_I, ACT.Sigmoid), (G_F, ACT.Sigmoid)):
                    act.wait_ge(S["added"], i * NG + g + 1)
                    act.activation(gate[:, g], gate[:, g], f).then_inc(S["acted"], 1)

            def p_hi(i, n, turn, early=False):
                if isinstance(i, int) and i < 2 and not early:
                    return
                wait_apart(act, S["p_ps"], i - 1)
                act.activation(x_hi[:, n], x2t[:, i], ACT.Copy).then_inc(S["p_hi"], 1)

            def before_output(i, n, turn):
                if isinstance(i, int) and i == NB - 1:
                    act.wait_ge(S["wo_in"], 16)
                    act.wait_ge(S["xpart"], NB * NG)
                    act.activation(wo_hi.rearrange("p k n -> p (k n)"), raw[:].rearrange("p u n -> p (u n)"),
                                   ACT.Copy).then_inc(S["wo_hi"], 1)
                    act.wait_ge(S["x_raw"], NB)
                    for t in range(2):
                        p_hi(t, t, 0, early=True)

            def c_part(s):
                if isinstance(s, int) and s == NB:
                    return
                act.wait_ge(S["tc"], s + 1)
                act.activation(c_hi[:], tc_ps[:], ACT.Copy).then_inc(S["c_hi"], 1)

            def state_units(i, n, turn):
                if isinstance(i, int) and i == 0:
                    act.wait_ge(S["w_in"], 16)
                    for u in range(NU):
                        act.activation(unit(w_hi, u), staged[:, u], ACT.Copy).then_inc(S["w_hi"], 1)

            c_part(0)
            software_pipeline(act, NB, [
                (0, lambda i, n, turn: r_sigmoid(i)), (2, before_output), (2, gates),
                (2, lambda i, n, turn: c_part(i + 1)), (0, lambda i, n, turn: x_parts(i)), (0, state_units)], 2)
            act.wait_ge(S["tc"], NB + 1)
            act.activation(ct[:], tc_ps[:].rearrange("p k n -> p (k n)"), ACT.Copy).then_inc(S["ct_ready"], 1)
            def p_tanh(i, n, turn):
                act.wait_ge(S["p_add"], i + 1)
                act.activation(p_sum[n], p_sum[n], ACT.Tanh).then_inc(S["p_tanh"], 1)

            software_pipeline(act, NB, [(0, p_hi), (1, p_tanh)], 2)

        @block.vector
        def _(dve):
            def x_lo_(i, n, turn):
                dve.wait_ge(S["x_hi"], i + 1)
                dve.tensor_tensor(x_lo[:, 0], x2t[:, i], x_hi[:, 0], ALU.subtract).then_inc(S["x_lo"], 1)

            def gates(i, n, turn):
                for g in (G_G, G_I, G_F):
                    dve.wait_ge(S["gates"], i * NG + g + 1)
                    dve.wait_ge(S["c"], i + 1)
                    dve.tensor_tensor(gate[:, g], g_ps[n][g][:], bias[:, g], ALU.add).then_inc(S["added"], 1)
                dve.wait_ge(S["acted"], i * NG + 2)
                dve.tensor_tensor(gate[:, G_I], gate[:, G_I], gate[:, G_G], ALU.mult).then_inc(S["ig"], 1)
                dve.wait_ge(S["acted"], i * NG + 3)
                dve.tensor_tensor(gate[:, G_F], gate[:, G_F], c[:], ALU.mult).then_inc(S["fc"], 1)
                dve.wait_ge(S["ig"], i + 1)
                dve.wait_ge(S["fc"], i + 1)
                dve.wait_ge(S["tc"], i + 1)
                dve.tensor_tensor(c[:], gate[:, G_F], gate[:, G_I], ALU.add).then_inc(S["c"], 1)

            def p_lo(i, n, turn, early=False):
                if isinstance(i, int) and i < 2 and not early:
                    return
                n = n % 2
                dve.wait_ge(S["p_hi"], i + 1)
                dve.tensor_tensor(x_lo[:, n], x2t[:, i], x_hi[:, n], ALU.subtract).then_inc(S["p_lo"], 1)

            def before_output(i, n, turn):
                if isinstance(i, int) and i == NB - 1:
                    dve.wait_ge(S["wo_hi"], 1)
                    dve.tensor_tensor(wo_lo.rearrange("p k n -> p (k n)"), raw[:].rearrange("p u n -> p (u n)"),
                                      wo_hi.rearrange("p k n -> p (k n)"), ALU.subtract).then_inc(S["wo_lo"], 1)
                    for t in range(2):
                        p_lo(t, t, 0, early=True)

            def c_part(s):
                if isinstance(s, int) and s == NB:
                    return
                dve.wait_ge(S["c_hi"], s + 1)
                dve.tensor_tensor(c_lo[:], tc_ps[:], c_hi[:], ALU.subtract).then_inc(S["c_lo"], 1)

            dve.wait_ge(S["params_in"], 80)
            dve.tensor_copy(c[:], c[:]).then_inc(S["c"], 1)
            def state_units(i, n, turn):
                if isinstance(i, int) and i == 0:
                    for u in range(NU):
                        dve.wait_ge(S["w_hi"], u + 1)
                        dve.tensor_tensor(unit(w_lo, u), staged[:, u], unit(w_hi, u),
                                          ALU.subtract).then_inc(S["w_lo"], 1)

            c_part(0)
            software_pipeline(dve, NB, [(2, before_output), (2, gates), (2, lambda i, n, turn: c_part(i + 1)), (0, x_lo_),
                                        (0, state_units)], 2)
            dve.wait_ge(S["const_ps"], 1)
            dve.tensor_tensor(bo[:], g_ps[0][2][:], bo[:], ALU.add).then_inc(S["const"], 1)
            dve.wait_ge(S["const"], 1)

            def p_add(i, n, turn):
                dve.wait_ge(S["p_ps"], i + 1)
                wait_for(dve, S["p_out"], i - 1)
                dve.tensor_tensor(p_sum[n % 2], g_ps[n % 2][0][:], bo[:], ALU.add).then_inc(S["p_add"], 1)

            def p_out_(i, n, turn):
                dve.wait_ge(S["p_tanh"], i + 1)
                dve.wait_ge(S[f"x1_in{n}"], turn * 16 + 16)
                wait_for(dve, S[f"out{n}"], turn * 16)
                dve.tensor_tensor(p_out[n], p_sum[n % 2], c_x1[n], ALU.add).then_inc(S["p_out"], 1)

            software_pipeline(dve, NB, [(0, p_lo), (1, p_add), (2, p_out_)], NO)

        @block.tensor
        def _(pe):
            def turn_x(i, n, turn):
                pe.wait_ge(S["x2"], i + 1)
                wait_for(pe, S["x_raw"], i)
                for k in range(DC):
                    mm = pe.transpose(tx_ps[:, k], x2[:, k * P:(k + 1) * P], ident[:])
                mm.then_inc(S["tx"], 1)

            def x_part(gs):
                def stage(i, n, turn):
                    pe.wait_ge(S["x_lo"], i + 1)
                    for g in gs:
                        wait_for(pe, S["added"], (i - 2) * NG + g + 1)
                        for k in range(DC):
                            mm = product(pe, g_ps[n][g][:], (x_hi[:, 0, k], x_lo[:, 0, k]),
                                         (wx_hi[:, g, k], wx_lo[:, g, k]), k == 0, False)
                        mm.then_inc(S["xpart"], 1)
                return stage

            def c_part(i, n, turn):
                pe.wait_ge(S["c_lo"], i + 1)
                for g in range(NG):
                    if isinstance(i, int) and i == 0:
                        pe.wait_ge(S["w_lo"], 2 * g + 2)
                    for k in range(DC):
                        mm = product(pe, g_ps[n][g][:], (c_hi[:, k], c_lo[:, k]),
                                     (w_hi[:, g, k], w_lo[:, g, k]), False, k == DC - 1)
                    mm.then_inc(S["gates"], 1)

            def turn_c(s):
                pe.wait_ge(S["c"], s + 1)
                wait_for(pe, S["c_lo"], s)
                for k in range(DC):
                    mm = pe.transpose(tc_ps[:, k], c[:, k * P:(k + 1) * P], ident[:])
                mm.then_inc(S["tc"], 1)

            def p(i, n, turn, early=False):
                if isinstance(i, int) and i < 2 and not early:
                    return
                pe.wait_ge(S["p_lo"], i + 1)
                wait_for(pe, S["p_add"], i - 1)
                for k in range(DC):
                    mm = product(pe, g_ps[n][0][:], (x_hi[:, n, k], x_lo[:, n, k]), (wo_hi[:, k], wo_lo[:, k]),
                                 k == 0, k == DC - 1)
                mm.then_inc(S["p_ps"], 1)

            def first_outputs(i, n, turn):
                if isinstance(i, int) and i == NB - 1:
                    pe.wait_ge(S["wo_lo"], 1)
                    pe.wait_ge(S["added"], i * NG + 1)
                    for t in range(2):
                        p(t, t, 0, early=True)

            turn_c(0)
            software_pipeline(pe, NB, [
                (2, c_part), (1, x_part((0, 1))), (2, first_outputs), (2, lambda i, n, turn: turn_c(i + 1)),
                (1, x_part((2,))),
                (0, turn_x)], 2)
            pe.wait_ge(S["ct_ready"], 1)
            pe.wait_ge(S["uo_in"], 16)
            for k in range(DC):
                mm = pe.matmul(g_ps[0][2][:], ct[:, k * P:(k + 1) * P], uo[:, k],
                               start=(k == 0), stop=(k == DC - 1))
            mm.then_inc(S["const_ps"], 1)

            software_pipeline(pe, NB, [(1, p)], 2)


SHAPES = {
    "x_rows": ([NTOK, D], FP32), "xt_groups": ([8, P, NB // 8, DC, P], FP32), "xt_tiles": ([NB, P, DC, P], FP32),
    "ids": ([P, NB], I32), "cond_t": ([P, DC, NB], FP32), "rt_w": ([P, DC, ER], FP32), "r_w": ([P, DC, ER], FP32),
    "r_bias": ([ER], FP32), "rw": ([ER, P, DC * HR + RC * D], FP32), "sw": ([12, P, HS], FP32),
    "wp1": ([P, DC, P], FP32), "wp2": ([P, ER], FP32), "bp1": ([P, 1], FP32), "bp2": ([ER], FP32),
    "w1": ([ER, P, DC, HS], FP32), "w2": ([ER, P, DC, HS], FP32), "b1": ([ER, HS], FP32), "b2": ([ER, D], FP32),
    "square": ([2, P, DC * D], FP32), "bo": ([D], FP32), "maa_k": ([D], FP32),
    "maa_r": ([D], FP32), "cond": ([NB, D], FP32), "w1h": ([EH, P, DC, HS], FP32),
    "w2h": ([EH, P, DC, HS], FP32), "gate_x": ([EH, P, 3 * DC * D // EH], FP32), "gate_w": ([8, P, HS], FP32), "gate_bias": ([3, D], FP32),
    "uo": ([P, 2 * HS], FP32), "bo_r": ([D], FP32), "in_c": ([D], FP32),
    "c_batch": ([NB, 1], FP32), "c_eight": ([NB, ER], FP32),
    "c_tri": ([P, P], FP32), "c_ident": ([P, P], FP32), "c_expert": ([P, EH, NB], FP32), "c_run": ([P, EH, NB], FP32),
    "c_tile": ([P, RT, ER], FP32), "c_token": ([P, NB], I32),
}


def constants():
    import numpy as np
    i = np.arange(NB)
    p = np.arange(P)
    return {
        "c_tri": (p[:, None] < p[None, :]).astype(np.float32),
        "c_batch": i[:, None].astype(np.float32),
        "c_eight": np.broadcast_to(np.arange(ER, dtype=np.float32), (NB, ER)),
        "c_ident": np.eye(P, dtype=np.float32),
        "c_expert": np.broadcast_to(np.arange(EH, dtype=np.float32)[None, :, None], (P, EH, NB)),
        "c_run": np.broadcast_to((i > 0).astype(np.float32), (P, EH, NB)),
        "c_tile": np.broadcast_to(np.arange(RT, dtype=np.float32)[None, :, None], (P, RT, ER)),
        "c_token": (i[None, :] * P + p[:, None]).astype(np.int32),
    }


def chunked(w, width=None):
    return w.reshape(-1, P, w.shape[-1]).swapaxes(0, 1)


def lay_out(x, cond_1024, itok_BxS_2_50255, L0_cond_router_w, L0_cond_router_t_w, L0_cond_router_bias, L0_cond_sw1,
            L0_cond_sw3, L0_cond_sw2, L0_cond_rw1, L0_cond_rw2, L0_ffn_Wp1, L0_ffn_bp1, L0_ffn_Wp2, L0_ffn_bp2,
            L0_ffn_W1, L0_ffn_b1, L0_ffn_W2, L0_ffn_b2, L0_ffn_Wo, L0_ffn_bo, L1_cond_time_maa_k,
            L1_cond_time_maa_r, L1_cond_w_recept, L1_cond_w_key, L1_cond_w_value, L1_ffn_wf, L1_ffn_uf, L1_ffn_bf,
            L1_ffn_wi, L1_ffn_ui, L1_ffn_bi, L1_ffn_wc, L1_ffn_uc, L1_ffn_bc, L1_ffn_wo, L1_ffn_uo, L1_ffn_bo,
            L1_ffn_in_c):
    import numpy as np
    xt = x.reshape(NB, P, DC, P).transpose(0, 3, 2, 1)
    a = {
        "x_rows": x.reshape(NTOK, D),
        "xt_tiles": xt,
        "xt_groups": xt.reshape(8, NB // 8, P, DC, P).swapaxes(1, 2),
        "ids": itok_BxS_2_50255.T,
        "cond_t": chunked(cond_1024.T),
        "rt_w": chunked(L0_cond_router_t_w.T),
        "r_w": chunked(L0_cond_router_w.T),
        "r_bias": L0_cond_router_bias,
        "sw": np.concatenate([L0_cond_sw1.T.reshape(DC, P, HS), L0_cond_sw3.T.reshape(DC, P, HS),
                              L0_cond_sw2.T.reshape(HC // 2, 2, P, D).swapaxes(1, 2).reshape(HC // 2, P, HS)]),
    }
    a["rw"] = np.concatenate([L0_cond_rw1.reshape(ER, HR, DC, P).transpose(0, 3, 2, 1).reshape(ER, P, DC * HR),
                              L0_cond_rw2.reshape(ER, D, RC, P).transpose(0, 3, 2, 1).reshape(ER, P, RC * D)], 2)
    def by_expert(w):
        return w.reshape(w.shape[0], -1, P, w.shape[-1]).swapaxes(1, 2).reshape(w.shape[0], P, -1, HS)

    def square(w):
        return chunked(w).reshape(P, DC * D)

    a.update(wp1=chunked(L0_ffn_Wp1), wp2=L0_ffn_Wp2, bp1=L0_ffn_bp1[:, None], bp2=L0_ffn_bp2,
             w1=by_expert(L0_ffn_W1), w2=by_expert(L0_ffn_W2), b1=L0_ffn_b1, b2=L0_ffn_b2,
             square=np.stack([square(L0_ffn_Wo), square(L1_cond_w_recept.T)]), bo=L0_ffn_bo, maa_k=L1_cond_time_maa_k,
             maa_r=L1_cond_time_maa_r, cond=cond_1024)
    gate_x = np.concatenate([square(w.T) for w in (L1_ffn_wc, L1_ffn_wi, L1_ffn_wf)], 1)
    gate_w = [L1_ffn_uc, L1_ffn_ui, L1_ffn_uf, L1_ffn_wo]
    a.update(w1h=by_expert(L1_cond_w_key), w2h=by_expert(L1_cond_w_value),
             gate_x=gate_x.reshape(P, EH, -1).swapaxes(0, 1),
             gate_w=np.stack([square(w.T).reshape(P, 2, HS) for w in gate_w]).swapaxes(1, 2).reshape(-1, P, HS),
             gate_bias=np.stack([L1_ffn_bc, L1_ffn_bi, L1_ffn_bf]), uo=chunked(L1_ffn_uo.T).reshape(P, -1),
             bo_r=L1_ffn_bo, in_c=L1_ffn_in_c)
    a.update(constants())
    return a


def build(nc, ins, out):
    with ExitStack() as ctx:
        dram = lambda n, s, t=FP32: nc.dram_tensor("mid_" + n, s, t, kind="Internal").ap()
        d = {"shared": dram("shared", [NB, P, D]), "routed": dram("routed", [NSLOT, D]), "rec": dram("rec", [NB, P, REC], I32),
             "slot_token": dram("slot_token", [NSLOT, 1], I32), "hash_in": dram("hash_in", [NTOK, D]),
             "x1": dram("x1", [NB, P, D]), "r": dram("r", [NB, P, D]),
             "hash_out": dram("hash_out", [NTOK + 1, D])}
        keep = {"ident": ctx.enter_context(nc.sbuf_tensor("ident", [P, P], FP32)),
                "route": ctx.enter_context(nc.sbuf_tensor("route", [P, 2, RT], I32)),
                "order": ctx.enter_context(nc.sbuf_tensor("order", [1, 3, NB], I32))}
        stage_shared(nc, ins, d, keep)
        with ExitStack() as two:
            for n in ("wo_hi", "wo_lo"):
                keep[n] = two.enter_context(nc.sbuf_tensor(n, [P, 2, DC, D], FP32R))
            stage_routed(nc, ins, d, keep)
            stage_choose(nc, ins, d, keep)
            stage_ffn(nc, ins, d, keep)
        with ExitStack() as two:
            for n in ("wx_hi", "wx_lo"):
                keep[n] = two.enter_context(nc.sbuf_tensor(n, [P, 3, DC, D], FP32R))
            stage_hashed(nc, ins, d, keep)
            stage_recurrent(nc, ins, d, keep, out)


def kernel(**inputs):
    import numpy as np
    import concourse.bacc as bacc
    from concourse.bass_utils import run_bass_kernel_spmd

    nc = bacc.Bacc("TRN2", target_bir_lowering=False, num_devices=1)
    arrays = {"in_" + n: np.ascontiguousarray(a)
              for n, a in lay_out(**{n: np.asarray(a) for n, a in inputs.items()}).items()}
    ins = {n: nc.dram_tensor("in_" + n, shape, dtype, kind="ExternalInput").ap() for n, (shape, dtype) in SHAPES.items()}
    out = nc.dram_tensor("out", [NB, P, D], FP32, kind="ExternalOutput").ap()
    build(nc, ins, out)
    return run_bass_kernel_spmd(nc, [arrays], core_ids=[0]).results[0]["out"]
```

```python
import concourse.bass as bass
from concourse import mybir
from contextlib import ExitStack

FP32 = mybir.dt.float32
FP32R = mybir.dt.float32r
BF16 = mybir.dt.bfloat16
I32 = mybir.dt.int32
U32 = mybir.dt.uint32
ALU = mybir.AluOpType
ACT = mybir.ActivationFunctionType
AX = mybir.AxisListType.X

P = 128
NB = 32
NTOK = NB * P
D = 512
DC = D // P
HS = 1024
HC = HS // P
HR = 256
RC = HR // P
ER = 8
EH = 16
CAP = NTOK // EH
RT = 2 * NTOK // P + ER
NSLOT = RT * P
SLOT1, SLOT2, SLOTH, GATE1, GATE2, TOKEN = range(6)
REC = 6
EPS = 1e-9
DVE_BIG = 3.0e38


def wait_for(eng, sem, n):
    if isinstance(n, int) and n <= 0:
        return
    eng.wait_ge(sem, n)


def wait_apart(eng, sem, n):
    if isinstance(n, int) and n <= 0:
        return
    eng.wait_ge(sem, n)
    eng.nop(nofuse=True)


def software_pipeline(eng, tiles, stages, unroll=1):
    depth = max(lag for lag, _ in stages)
    head = -(-(depth + unroll) // unroll) * unroll

    def step(j, par, block=None):
        for lag, stage in stages:
            i = j - lag
            n = (par - lag) % unroll
            if not isinstance(i, int):
                stage(*((i, n, block + (par - lag - n) // unroll) if unroll > 1 else (i,)))
            elif 0 <= i < tiles:
                stage(*((i, n, i // unroll) if unroll > 1 else (i,)))

    for j in range(head):
        step(j, j % unroll)
    with eng.Fori(head // unroll, tiles // unroll) as block:
        for par in range(unroll):
            step(block * unroll + par, par, block)
    for j in range(tiles, tiles + depth):
        step(j, j % unroll)


def but_first(stage):
    return lambda i: None if isinstance(i, int) and i == 0 else stage(i)


def product(pe, out, a, w, first, last):
    (a_hi, a_lo), (w_hi, w_lo) = a, w
    pe.matmul(out, a_hi, w_hi, start=first, stop=False, skip_group_check=True)
    pe.matmul(out, a_hi, w_lo, start=False, stop=False, skip_group_check=True)
    return pe.matmul(out, a_lo, w_hi, start=False, stop=last, skip_group_check=True)


def sems(nc, ctx, prefix, names):
    own = {n[1:]: nc.alloc_semaphore(prefix + n[1:]) for n in names.split() if n[0] == "~"}
    names = " ".join(n for n in names.split() if n[0] != "~")
    made = {n: ctx.enter_context(nc.semaphore(prefix + n)) for n in names.split()}

    def clear():
        numbers = sorted(sem.num for sem in made.values())
        while numbers:
            run = 1
            while run < len(numbers) and numbers[run] == numbers[0] + run:
                run += 1
            nc.sync.sem_clear(range(numbers[0], numbers[0] + run))
            numbers = numbers[run:]

    ctx.callback(clear)
    return made | own



def stage_shared(nc, ins, d, keep):
    G = 8
    TG = NB // G
    NU = 12
    with ExitStack() as ctx:
        sb = lambda n, s, t=FP32: ctx.enter_context(nc.sbuf_tensor("s1_" + n, s, t))
        ps = lambda n, s, t=FP32: ctx.enter_context(nc.psum_tensor("s1_" + n, s, t))
        S = sems(nc, ctx, "s1_", "const late_const ~x_in0 ~x_in1 logits_t logits_sum logits bias_ps bias w_in0 w_in1 "
                 "w_hi w_lo ones sig dve pe_rank "
                 "~rec_out ~rec_in ~tokens_sent0 ~tokens_sent1 zeroed ~zero_out "
                 "xt_in xt_hi xt_lo gu silu hmul h_hi h_lo mm2 o_ready o_out ~lists hash_members hash_total_read hash_rank_read "
                 "rank_read members rec_done")

        x_grp = sb("x_grp", [P, 2, TG, DC, P])
        w_raw = sb("w_raw", [P, 2, HS])
        w_hi = sb("w_hi", [P, NU, HS], FP32R)
        w_lo = sb("w_lo", [P, NU, HS], FP32R)
        sw2_hi = w_hi[:, 8:12, :].rearrange("p u (a n) -> p (u a) n", a=2)
        sw2_lo = w_lo[:, 8:12, :].rearrange("p u (a n) -> p (u a) n", a=2)
        ident = keep["ident"]
        tri_f = sb("tri_f", [P, P])
        tri = sb("tri", [P, P], BF16)
        ones = sb("ones", [P, P], BF16)
        ones_f = sb("ones_f", [P, ER])
        expert_no = sb("expert_no", [P, EH, NB])
        new_run = sb("new_run", [P, EH, NB])
        tile_no = sb("tile_no", [P, RT, ER])
        token_no = sb("token_no", [P, NB], I32)
        ids = sb("ids", [P, NB], I32)
        hash_id = sb("hash_id", [P, NB], I32)
        cond_t = sb("cond_t", [P, DC, NB])
        rt_w = sb("rt_w", [P, DC, ER])
        r_w = sb("r_w", [P, DC, ER])
        r_bias = sb("r_bias", [P, ER])
        batch_bias = sb("batch_bias", [ER, NB])
        logits_sb = sb("logits_sb", [ER, 2, TG, P])
        score = sb("score", [P, ER, NB])
        sel = sb("sel", [P, ER, NB])
        t1 = sb("t1", [P, EH, NB])
        t2 = sb("t2", [P, EH, NB])
        oh1 = sb("oh1", [P, EH, NB])
        oh2 = sb("oh2", [P, ER, NB])
        member = sb("member", [P, EH, NB], BF16)
        col = sb("col", [P, 8, NB])
        cnt_i = sb("cnt_i", [P, ER], I32)
        cnt_f = sb("cnt_f", [P, 4, ER])
        tile_ge = x_grp[:, 1].rearrange("p i k n -> p (i k n)")[:, 0:RT * ER].rearrange("p (t e) -> p t e", e=ER)
        tile_e = sb("tile_e", [P, 3, RT])
        rec = sb("rec", [P, NB, REC], I32)
        rec_f = rec[:].bitcast(FP32)
        rec_tile = sb("rec_tile", [P, 2, REC], I32)
        zero = sb("zero", [P, D])
        izero = sb("izero", [P, RT], I32)

        x_raw = x_grp[:, 0]
        xt_hi = sb("xt_hi", [P, TG, DC, P], FP32R)
        xt_lo = sb("xt_lo", [P, TG, DC, P], FP32R)
        sg = sb("sg", [P, 2, TG, P])
        h = sb("h", [P, 2, TG, P])
        ht_hi = sb("ht_hi", [P, HC, TG, P], FP32R)
        ht_lo = sb("ht_lo", [P, HC, TG, P], FP32R)
        o_sb = sb("o_sb", [P, D])

        NG = 3
        gate_ps = [ps(f"gate{n}", [P, TG, P]) for n in range(NG)]
        up_ps = [ps(f"up{n}", [P, TG, P]) for n in range(NG)]
        first_ps = ps("first", [P, D])
        aux_ps = ps("aux", [P, D])
        o_ps = [first_ps, aux_ps]
        lg_ps = aux_ps[:, 0:ER * NB].rearrange("p (e i) -> p e i", e=ER)
        aux_h = aux_ps[:, :].rearrange("p (e i) -> p e i", e=EH)
        rank_ps = aux_ps[:, 0:256].rearrange("p (e i) -> p e i", e=ER)
        bias_ps = first_ps[0:ER, 0:NB]
        tot_ps = aux_ps[:, 256:512].rearrange("p (e i) -> p e i", e=ER)

        n_const, n_late = 8, 3

        block = ctx.enter_context(nc.Block())

        @block.sync
        def _(sp):
            for dst, src in ((rt_w[:], ins["rt_w"]), (cond_t[:], ins["cond_t"]), (r_w[:], ins["r_w"]),
                             (ids[:], ins["ids"]), (tri_f[:], ins["c_tri"]), (ident[:], ins["c_ident"]),
                             (expert_no[:], ins["c_expert"]), (new_run[:], ins["c_run"])):
                sp.dma_start(dst, src).then_inc(S["const"], 16)

            def units(u2):
                for n in range(2):
                    wait_for(sp, S["w_lo"], u2 * 2 + n - 1)
                    sp.dma_start(w_raw[:, n], ins["sw"][u2 * 2 + n]).then_inc(S[f"w_in{n}"], 16)

            units(0)
            for dst, src in ((tile_no[:], ins["c_tile"]), (token_no[:], ins["c_token"]),
                             (r_bias[:], ins["r_bias"].partition_broadcast(P))):
                sp.dma_start(dst, src).then_inc(S["late_const"], 16)
            with sp.Fori(1, NU // 2 - 1) as u2:
                units(u2)

            def load_x(g):
                if isinstance(g, int) and g == 0:
                    sp.wait_ge(S["logits_t"], G - 1)
                wait_for(sp, S["xt_lo"], g)
                sp.dma_start(x_raw, ins["xt_groups"][g]).then_inc(S["xt_in"], 16)

            def store_o(g):
                for m in range(TG):
                    sp.wait_ge(S["o_ready"], g * TG + m + 1)
                    sp.dma_start(d["shared"][g * TG + m], o_sb[:]).then_inc(S["o_out"], 16)

            load_x(0)
            units(NU // 2 - 1)
            software_pipeline(sp, G, [(0, but_first(load_x)), (1, store_o)])
            sp.wait_ge(S["o_out"], 16 * NB)

        @block.gpsimd
        def _(pool):
            for k in range(2):
                pool.dma_start(x_grp[:, k], ins["xt_groups"][k]).then_inc(S[f"x_in{k}"], 16)
            pool.memset(zero[:], 0.0).then_inc(S["zeroed"], 1)
            pool.memset(izero[:], 0).then_inc(S["zeroed"], 1)
            pool.wait_ge(S["zeroed"], 2)
            pool.dma_start(d["slot_token"].rearrange("(p j) o -> p (j o)", j=RT), izero[:]).then_inc(S["lists"], 16)
            pool.dma_start(d["hash_out"][NTOK:NTOK + 1, :], zero[0:1, :]).then_inc(S["zero_out"], 16)
            pool.wait_ge(S["lists"], 16)
            for g in range(2, G):
                pool.wait_ge(S["logits_t"], g - 1)
                pool.dma_start(x_grp[:, g % 2], ins["xt_groups"][g]).then_inc(S[f"x_in{g % 2}"], 16)
            pool.wait_ge(S["rec_done"], 1)
            pool.dma_start(d["rec"].rearrange("i p c -> p i c"), rec[:]).then_inc(S["rec_out"], 16)
            pool.wait_ge(S["rec_out"], 16)

            def enter_tokens(i2, first):
                for k in range(2):
                    if not first:
                        pool.wait_ge(S[f"tokens_sent{k}"], i2 * 32)
                    pool.dma_start(rec_tile[:, k], d["rec"][i2 * 2 + k]).then_inc(S["rec_in"], 16)
                    wait_apart(pool, S["rec_in"], i2 * 32 + 16 * k + 16)
                    for c in (SLOT1, SLOT2):
                        pool.indirect_dma_start(
                            d["slot_token"], bass.IndirectOffsetOnAxis(rec_tile[:, k, c:c + 1].bitcast(U32), 0),
                            rec_tile[:, k, TOKEN:TOKEN + 1], None).then_inc(S[f"tokens_sent{k}"], 16)
                    pool.dma_start(d["hash_in"][bass.ds((i2 * 2 + k) * P, P)], zero[:]).then_inc(S["zero_out"], 16)

            enter_tokens(0, True)
            with pool.Fori(1, NB // 2) as i2:
                enter_tokens(i2, False)
            for k in range(2):
                pool.wait_ge(S[f"tokens_sent{k}"], 16 * NB)
            pool.wait_ge(S["zero_out"], 16 * (NB + 1))

        @block.scalar
        def _(act):
            def split_units(u2):
                for n in range(2):
                    act.wait_ge(S[f"w_in{n}"], u2 * 16 + 16)
                    act.activation(w_hi[:, u2 * 2 + n, :], w_raw[:, n, :], ACT.Copy).then_inc(S["w_hi"], 1)

            def x_hi(g):
                act.wait_ge(S["xt_in"], g * 16 + 16)
                wait_for(act, S["gu"], g * HC)
                act.activation(xt_hi[:], x_raw, ACT.Copy).then_inc(S["xt_hi"], 1)

            def chunks(g):
                for c in range(HC + 1):
                    if c < HC:
                        act.wait_ge(S["gu"], g * HC + c + 1)
                        wait_for(act, S["hmul"], g * HC + c - 1)
                        act.activation(sg[:, c % 2], gate_ps[c % NG][:], ACT.Silu).then_inc(S["silu"], 1)
                    if c > 0:
                        act.wait_ge(S["hmul"], g * HC + c)
                        wait_for(act, S["mm2"], g * TG)
                        act.activation(ht_hi[:, c - 1], h[:, (c - 1) % 2], ACT.Copy).then_inc(S["h_hi"], 1)

            def o_out(g):
                for m in range(TG):
                    act.wait_ge(S["mm2"], g * TG + m + 1)
                    wait_for(act, S["o_out"], (g * TG + m) * 16)
                    act.activation(o_sb[:], o_ps[m % 2][:], ACT.Copy, scale=1.0 / 3.0).then_inc(S["o_ready"], 1)

            with act.Fori(0, NU // 2 - 1) as u2:
                split_units(u2)
            x_hi(0)
            act.wait_ge(S["logits"], G)
            act.activation(score[:], lg_ps, ACT.Sigmoid).then_inc(S["sig"], 1)
            split_units(NU // 2 - 1)
            software_pipeline(act, G, [(1, chunks), (0, but_first(x_hi)), (1, o_out)])

        @block.vector
        def _(dve):
            done = [0]

            def op(ins_):
                done[0] += 1
                ins_.then_inc(S["dve"], 1)
                dve.wait_ge(S["dve"], done[0])

            def signal(ins_, name):
                ins_.then_inc(S[name], 1)
                dve.wait_ge(S[name], 1)

            def ranks(experts, rank, off, incl, last_step):
                op(dve.tensor_tensor_scan(incl.rearrange("p e i -> p (e i)"),
                                          new_run[:, 0:experts].rearrange("p e i -> p (e i)"),
                                          off.rearrange("p e i -> p (e i)"), 0.0, ALU.mult, ALU.add))
                op(dve.tensor_tensor(off, incl, off, ALU.subtract))
                signal(dve.tensor_tensor(off, off, rank, ALU.add), last_step)

            dve.wait_ge(S["const"], 16 * n_const)
            dve.memset(ones[:], 1.0).then_inc(S["ones"], 1)
            dve.memset(ones_f[:], 1.0).then_inc(S["ones"], 1)
            dve.tensor_copy(tri[:], tri_f[:]).then_inc(S["ones"], 1)
            low = col[:, 0]
            hid = hash_id[:]
            op(dve.tensor_scalar(hid, ids[:], 15, None, ALU.bitwise_and))
            op(dve.tensor_copy(low, hid))
            op(dve.tensor_scalar(low, low, 11.0, None, ALU.mult))
            op(dve.tensor_copy(hid, low))
            op(dve.tensor_scalar(hid, hid, 15, None, ALU.bitwise_and))
            op(dve.tensor_copy(low, hid))
            op(dve.tensor_tensor(oh1[:], expert_no[:], low[:, None, :].to_broadcast([P, EH, NB]), ALU.is_equal))
            signal(dve.tensor_copy(member[:], oh1[:]), "hash_members")
            dve.wait_ge(S["pe_rank"], 1)
            signal(dve.tensor_copy(t1[:], aux_h), "hash_total_read")
            dve.wait_ge(S["pe_rank"], 2)
            ranks(EH, aux_h, t1[:], t2[:], "hash_rank_read")
            op(dve.tensor_tensor(t1[:], t1[:], oh1[:], ALU.mult))
            pos, keep_, slot = col[:, 2], col[:, 3], col[:, 4]
            op(dve.tensor_reduce(pos, t1[:].rearrange("p e i -> p i e"), AX, ALU.add))
            op(dve.tensor_scalar(keep_, pos, float(CAP), None, ALU.is_lt))
            op(dve.scalar_tensor_tensor(slot, low, float(CAP), pos, ALU.mult, ALU.add))
            op(dve.scalar_tensor_tensor(slot, slot, -float(NTOK), keep_, ALU.add, ALU.mult))
            op(dve.tensor_scalar(slot, slot, float(NTOK), None, ALU.add))
            op(dve.tensor_copy(rec[:, :, SLOTH], slot))
            dve.wait_ge(S["late_const"], 16 * n_late)
            op(dve.tensor_copy(rec[:, :, TOKEN], token_no[:]))
            dve.wait_ge(S["bias_ps"], 1)
            signal(dve.tensor_copy(batch_bias[:], bias_ps), "bias")

            def add_bias(g):
                dve.wait_ge(S["logits_t"], g + 1)
                wait_for(dve, S["logits"], g - 1)
                dve.tensor_tensor(logits_sb[:, g % 2], gate_ps[g % 2][0:ER],
                                  batch_bias[:, g * TG:(g + 1) * TG, None].to_broadcast([ER, TG, P]),
                                  ALU.add).then_inc(S["logits_sum"], 1)

            add_bias(0)
            def split_units(u2):
                for n in range(2):
                    u = u2 * 2 + n
                    dve.wait_ge(S["w_hi"], u + 1)
                    dve.tensor_tensor(w_lo[:, u, :], w_raw[:, n, :], w_hi[:, u, :], ALU.subtract).then_inc(S["w_lo"], 1)

            for u2, groups in enumerate(((1,), (2, 3), (4,), (5, 6), (7,))):
                split_units(u2)
                for g in groups:
                    add_bias(g)

            def x_lo(g):
                dve.wait_ge(S["xt_hi"], g + 1)
                dve.tensor_tensor(xt_lo[:], x_raw, xt_hi[:], ALU.subtract).then_inc(S["xt_lo"], 1)

            def chunks(g):
                for c in range(HC + 1):
                    if c < HC:
                        dve.wait_ge(S["silu"], g * HC + c + 1)
                        wait_for(dve, S["h_lo"], g * HC + c - 1)
                        dve.tensor_tensor(h[:, c % 2], sg[:, c % 2], up_ps[c % NG][:], ALU.mult).then_inc(S["hmul"], 1)
                    if c > 0:
                        dve.wait_ge(S["h_hi"], g * HC + c)
                        dve.tensor_tensor(ht_lo[:, c - 1], h[:, (c - 1) % 2], ht_hi[:, c - 1],
                                          ALU.subtract).then_inc(S["h_lo"], 1)

            x_lo(0)
            dve.wait_ge(S["sig"], 1)
            no8 = expert_no[:, 0:ER]
            op(dve.tensor_tensor(sel[:], score[:], r_bias[:, :, None].to_broadcast([P, ER, NB]), ALU.add))
            gate = []
            for c, one in ((0, oh1[:, 0:ER]), (1, oh2[:])):
                best, idx, g = col[:, c], col[:, 2 + c], col[:, 4 + c]
                op(dve.tensor_reduce(best, sel[:].rearrange("p e i -> p i e"), AX, ALU.max))
                op(dve.tensor_tensor(t1[:, 0:ER], sel[:], best[:, None, :].to_broadcast([P, ER, NB]), ALU.is_lt))
                op(dve.scalar_tensor_tensor(t1[:, 0:ER], t1[:, 0:ER], float(ER), no8, ALU.mult, ALU.add))
                op(dve.tensor_reduce(idx, t1[:, 0:ER].rearrange("p e i -> p i e"), AX, ALU.min))
                op(dve.tensor_tensor(one, no8, idx[:, None, :].to_broadcast([P, ER, NB]), ALU.is_equal))
                op(dve.tensor_tensor(t1[:, 0:ER], one, score[:], ALU.mult))
                op(dve.tensor_reduce(g, t1[:, 0:ER].rearrange("p e i -> p i e"), AX, ALU.add))
                if c == 0:
                    op(dve.scalar_tensor_tensor(sel[:], one, -DVE_BIG, sel[:], ALU.mult, ALU.add))
                gate.append(g)
            signal(dve.tensor_tensor(member[:, 0:ER], oh1[:, 0:ER], oh2[:], ALU.add), "members")

            tiles_f, end, base = cnt_f[:, 0], cnt_f[:, 1], cnt_f[:, 2]

            def after_ranks():
                den, inv, above = col[:, 0], col[:, 1], col[:, 2]
                op(dve.tensor_tensor(den, gate[0], gate[1], ALU.add))
                op(dve.tensor_scalar(above, den, EPS, None, ALU.is_gt))
                op(dve.tensor_scalar(den, den, EPS, None, ALU.add))
                op(dve.reciprocal(inv, den))
                for c, g in enumerate(gate):
                    op(dve.tensor_tensor(g, g, inv, ALU.mult))
                    op(dve.scalar_tensor_tensor(g, g, -0.5, above, ALU.add, ALU.mult))
                    op(dve.tensor_scalar(g, g, 0.5, 1.0 / 3.0, ALU.add, ALU.mult))
                    op(dve.tensor_copy(rec_f[:, :, GATE1 + c], g))
                dve.wait_ge(S["pe_rank"], 3)
                op(dve.tensor_copy(t1[:, 0:ER], tot_ps))
                ranks(ER, rank_ps, t1[:, 0:ER], t2[:, 0:ER], "rank_read")
                op(dve.tensor_scalar(tiles_f, t2[:, 0:ER, NB - 1], float(P - 1), None, ALU.add))
                op(dve.tensor_copy(cnt_i[:], tiles_f))
                op(dve.tensor_scalar(cnt_i[:], cnt_i[:], 7, None, ALU.arith_shift_right))
                op(dve.tensor_copy(tiles_f, cnt_i[:]))
                op(dve.tensor_tensor_scan(end, ones_f[:, 0:ER], tiles_f, 0.0, ALU.mult, ALU.add))
                op(dve.tensor_tensor(base, end, tiles_f, ALU.subtract))
                op(dve.tensor_scalar(base, base, float(P), None, ALU.mult))
                op(dve.tensor_tensor(t1[:, 0:ER], t1[:, 0:ER], base[:, :, None].to_broadcast([P, ER, NB]), ALU.add))
                for c, one in ((0, oh1[:, 0:ER]), (1, oh2[:])):
                    op(dve.tensor_tensor(t2[:, 0:ER], t1[:, 0:ER], one, ALU.mult))
                    op(dve.tensor_reduce(col[:, c], t2[:, 0:ER].rearrange("p e i -> p i e"), AX, ALU.add))
                    (op, lambda x: signal(x, "rec_done"))[c](dve.tensor_copy(rec[:, :, SLOT1 + c], col[:, c]))
            after_ranks()
            split_units(NU // 2 - 1)
            software_pipeline(dve, G, [(1, chunks), (0, but_first(x_lo))])
            op(dve.tensor_tensor(tile_ge, tile_no[:], end[:, None, :].to_broadcast([P, RT, ER]), ALU.is_ge))
            te, new = tile_e[:, 0], tile_e[:, 1]
            op(dve.tensor_reduce(te, tile_ge, AX, ALU.add))
            op(dve.tensor_scalar(te, te, float(ER - 1), None, ALU.min))
            op(dve.memset(new, 1.0))
            op(dve.tensor_tensor(new[:, 2:RT], te[:, 2:RT], te[:, 0:RT - 2], ALU.not_equal))
            op(dve.tensor_copy(keep["route"][:, 0], te))
            op(dve.tensor_copy(keep["route"][:, 1], new))

        @block.tensor
        def _(pe):
            pe.wait_ge(S["const"], 16 * n_const)
            for k in range(DC):
                mm = pe.matmul(bias_ps, rt_w[:, k], cond_t[:, k], start=(k == 0), stop=(k == DC - 1))
            mm.then_inc(S["bias_ps"], 1)
            pe.wait_ge(S["ones"], 3)
            pe.wait_ge(S["hash_members"], 1)
            flat = member[:].rearrange("p e i -> p (e i)")
            pe.matmul(aux_ps[:, :], ones[:], flat, start=True, stop=True).then_inc(S["pe_rank"], 1)
            pe.wait_ge(S["hash_total_read"], 1)
            pe.matmul(aux_ps[:, :], tri[:], flat, start=True, stop=True).then_inc(S["pe_rank"], 1)

            def score_t(g):
                pe.wait_ge(S[f"x_in{g % 2}"], g // 2 * 16 + 16)
                wait_for(pe, S["logits_sum"], g - 1)
                for k in range(DC):
                    mm = pe.matmul(gate_ps[g % 2][0:ER], r_w[:, k], x_grp[:, g % 2, :, k], start=(k == 0),
                                   stop=(k == DC - 1))
                mm.then_inc(S["logits_t"], 1)

            def turn_scores(g):
                pe.wait_ge(S["logits_sum"], g + 1)
                for tt in range(TG):
                    mm = pe.transpose(lg_ps[:, :, g * TG + tt], logits_sb[:, g % 2, tt], ident[0:ER, 0:ER])
                mm.then_inc(S["logits"], 1)

            score_t(0)
            pe.wait_ge(S["hash_rank_read"], 1)
            for g in range(1, G):
                score_t(g)
                turn_scores(g - 1)
            turn_scores(G - 1)

            def gate_up(g, first=0, last=HC):
                for c in range(first, last):
                    if c == 0:
                        pe.wait_ge(S["xt_lo"], g + 1)
                    wait_for(pe, S["hmul"], g * HC + (c - NG + 1 if c >= NG else 0))
                    for out, u0 in ((gate_ps[c % NG], 0), (up_ps[c % NG], DC)):
                        for k in range(DC):
                            w = slice(c * P, (c + 1) * P)
                            mm = product(pe, out[:], (w_hi[:, u0 + k, w], w_lo[:, u0 + k, w]),
                                         (xt_hi[:, :, k], xt_lo[:, :, k]), k == 0, k == DC - 1)
                    mm.then_inc(S["gu"], 1)

            def down(g):
                if isinstance(g, int) and g == 0:
                    pe.wait_ge(S["w_lo"], NU)
                for m in range(TG):
                    wait_for(pe, S["o_ready"], g * TG + m - 1)
                    for k in range(HC):
                        if m == 0:
                            pe.wait_ge(S["h_lo"], g * HC + k + 1)
                        mm = product(pe, o_ps[m % 2][:], (ht_hi[:, k, m], ht_lo[:, k, m]), (sw2_hi[:, k], sw2_lo[:, k]),
                                     k == 0, k == HC - 1)
                    mm.then_inc(S["mm2"], 1)

            pe.wait_ge(S["w_lo"], 2 * DC)
            gate_up(0, 0, 1)
            pe.wait_ge(S["members"], 1)
            flat8 = member[:, 0:ER].rearrange("p e i -> p (e i)")
            pe.matmul(aux_ps[:, 0:256], tri[:], flat8, start=True, stop=True)
            pe.matmul(aux_ps[:, 256:512], ones[:], flat8, start=True, stop=True,
                      skip_group_check=True).then_inc(S["pe_rank"], 1)
            gate_up(0, 1, NG)
            pe.wait_ge(S["rank_read"], 1)
            software_pipeline(pe, G, [(0, lambda g: gate_up(g, NG if isinstance(g, int) and g == 0 else 0)),
                                      (0, down)])




def stage_routed(nc, ins, d, keep):
    with ExitStack() as ctx:
        sb = lambda n, s, t=FP32: ctx.enter_context(nc.sbuf_tensor("s2_" + n, s, t))
        ps = lambda n, s, t=FP32: ctx.enter_context(nc.psum_tensor("s2_" + n, s, t))
        S = sems(nc, ctx, "s2_", "idx_in0 idx_in1 idx_in2 idx_in3 ~x_in0 ~x_in1 ~x_in2 ~x_in3 w1_in0 w1_in1 w2_in0 "
                 "w2_in1 wo_in wo_hi wo_lo w1_hi w1_lo w2_hi w2_lo tx x_hi x_lo mm1 "
                 "gelu th h_hi h_lo mm2 o_ready o_out0 o_out1 o_out2 o_out3")
        W1, W2 = DC * HR, RC * D
        route = keep["route"]
        ident = keep["ident"]
        NI = 4
        idx = sb("idx", [P, NI, 1], I32)
        x = sb("x", [P, NI, D])
        w_raw = sb("w_raw", [P, 2, W1 + W2])
        w_hi = sb("w_hi", [P, 2, W1 + W2], FP32R)
        w_lo = sb("w_lo", [P, 2, W1 + W2], FP32R)
        x_hi = sb("x_hi", [P, 2, DC, P], FP32R)
        x_lo = sb("x_lo", [P, 2, DC, P], FP32R)
        h = sb("h", [P, 2, HR])
        ht_hi = sb("ht_hi", [P, 2, RC, P], FP32R)
        ht_lo = sb("ht_lo", [P, 2, RC, P], FP32R)
        o_sb = sb("o_sb", [P, NI, D])
        wo_raw = sb("wo_raw", [P, 2, DC * D])
        flat = lambda w, n: w[:, n].rearrange("p k n -> p (k n)")
        tx_ps = [ps(f"tx{n}", [P, DC, P]) for n in range(2)]
        h_ps = [ps(f"h{n}", [P, HR]) for n in range(2)]
        th_ps = [ps(f"th{n}", [P, RC, P]) for n in range(2)]
        o_ps = [ps(f"o{n}", [P, D]) for n in range(2)]

        block = ctx.enter_context(nc.Block())

        @block.sync
        def _(sp):
            def load_idx(i, n, turn):
                wait_for(sp, S[f"x_in{n}"], turn * 16)
                sp.dma_start(idx[:, n], d["slot_token"][bass.ds(i * P, P)]).then_inc(S[f"idx_in{n}"], 16)

            def load_w(name, c):
                def stage(i, n, turn):
                    expert = sp.value_load(route[0:1, 0, bass.ds(i, 1)], min_val=0, max_val=ER - 1)
                    new = sp.value_load(route[0:1, 1, bass.ds(i, 1)], min_val=0, max_val=1)
                    wait_apart(sp, S[name + "_lo"], i - 1)
                    sp.dma_start(w_raw[:, n % 2, c], ins["rw"][expert, :, c],
                                 cond=new > 0).then_inc(S[f"{name}_in{n % 2}"], 16)
                return stage

            def store(i, n, turn):
                sp.wait_ge(S["o_ready"], i + 1)
                sp.dma_start(d["routed"][bass.ds(i * P, P)], o_sb[:, n]).then_inc(S[f"o_out{n}"], 16)

            def load_wo(i, n, turn):
                if isinstance(i, int) and i < 2:
                    sp.dma_start(wo_raw[:, i], ins["square"][i]).then_inc(S["wo_in"], 16)

            software_pipeline(sp, RT, [(0, load_idx), (2, load_w("w1", slice(0, W1))),
                                       (3, load_w("w2", slice(W1, W1 + W2))), (4, load_wo), (7, store)], NI)
            for n in range(NI):
                sp.wait_ge(S[f"o_out{n}"], 16 * RT // NI)

        @block.gpsimd
        def _(pool):
            def gather(i, n, turn):
                pool.wait_ge(S[f"idx_in{n}"], turn * 16 + 16)
                wait_apart(pool, S["tx"], i - NI + 1)
                pool.indirect_dma_start(x[:, n], None, ins["x_rows"],
                                        bass.IndirectOffsetOnAxis(idx[:, n].bitcast(U32), 0)
                                        ).then_inc(S[f"x_in{n}"], 16)

            software_pipeline(pool, RT, [(0, gather)], NI)

        @block.scalar
        def _(act):
            def w1_hi(i, n, turn):
                act.wait_ge(S[f"w1_in{n % 2}"], (turn * 2 + n // 2) * 16 + 16)
                wait_for(act, S["mm1"], i - 1)
                act.activation(w_hi[:, n % 2, 0:W1], w_raw[:, n % 2, 0:W1], ACT.Copy).then_inc(S["w1_hi"], 1)

            def w2_hi(i, n, turn):
                act.wait_ge(S[f"w2_in{n % 2}"], (turn * 2 + n // 2) * 16 + 16)
                wait_for(act, S["mm2"], i - 1)
                act.activation(w_hi[:, n % 2, W1:], w_raw[:, n % 2, W1:], ACT.Copy).then_inc(S["w2_hi"], 1)

            def x_hi_(i, n, turn):
                act.wait_ge(S["tx"], i + 1)
                wait_for(act, S["mm1"], i - 1)
                act.activation(x_hi[:, n % 2], tx_ps[n % 2][:], ACT.Copy).then_inc(S["x_hi"], 1)

            def gelu(i, n, turn):
                act.wait_ge(S["mm1"], i + 1)
                wait_for(act, S["th"], i - 1)
                act.activation(h[:, n % 2], h_ps[n % 2][:], ACT.Gelu).then_inc(S["gelu"], 1)

            def h_hi(i, n, turn):
                act.wait_ge(S["th"], i + 1)
                wait_for(act, S["mm2"], i - 1)
                act.activation(ht_hi[:, n % 2], th_ps[n % 2][:], ACT.Copy).then_inc(S["h_hi"], 1)

            def o_copy(i, n, turn):
                act.wait_ge(S["mm2"], i + 1)
                wait_for(act, S[f"o_out{n}"], turn * 16)
                act.activation(o_sb[:, n], o_ps[n % 2][:], ACT.Copy).then_inc(S["o_ready"], 1)

            def wo_hi(i, n, turn):
                if isinstance(i, int) and i < 2:
                    act.wait_ge(S["wo_in"], 32)
                    act.activation(flat(keep["wo_hi"], i), wo_raw[:, i], ACT.Copy).then_inc(S["wo_hi"], 1)

            software_pipeline(act, RT, [(2, gelu), (1, x_hi_), (0, w1_hi), (3, o_copy), (2, h_hi), (1, w2_hi),
                                        (3, wo_hi)], NI)

        @block.vector
        def _(dve):
            def w1_lo(i, n, turn):
                dve.wait_ge(S["w1_hi"], i + 1)
                dve.tensor_tensor(w_lo[:, n, 0:W1], w_raw[:, n, 0:W1], w_hi[:, n, 0:W1],
                                  ALU.subtract).then_inc(S["w1_lo"], 1)

            def w2_lo(i, n, turn):
                dve.wait_ge(S["w2_hi"], i + 1)
                dve.tensor_tensor(w_lo[:, n, W1:], w_raw[:, n, W1:], w_hi[:, n, W1:],
                                  ALU.subtract).then_inc(S["w2_lo"], 1)

            def x_lo_(i, n, turn):
                dve.wait_ge(S["x_hi"], i + 1)
                dve.tensor_tensor(x_lo[:, n], tx_ps[n][:], x_hi[:, n], ALU.subtract).then_inc(S["x_lo"], 1)

            def h_lo(i, n, turn):
                dve.wait_ge(S["h_hi"], i + 1)
                dve.tensor_tensor(ht_lo[:, n], th_ps[n][:], ht_hi[:, n], ALU.subtract).then_inc(S["h_lo"], 1)

            def wo_lo(i, n, turn):
                if isinstance(i, int) and i < 2:
                    dve.wait_ge(S["wo_hi"], i + 1)
                    dve.tensor_tensor(flat(keep["wo_lo"], i), wo_raw[:, i], flat(keep["wo_hi"], i),
                                      ALU.subtract).then_inc(S["wo_lo"], 1)

            software_pipeline(dve, RT, [(1, x_lo_), (0, w1_lo), (2, h_lo), (1, w2_lo), (3, wo_lo)], 2)

        @block.tensor
        def _(pe):
            def turn_x(i, n, turn):
                pe.wait_ge(S[f"x_in{n}"], turn * 16 + 16)
                wait_for(pe, S["x_lo"], i - 1)
                for k in range(DC):
                    mm = pe.transpose(tx_ps[n % 2][:, k], x[:, n, k * P:(k + 1) * P], ident[:])
                mm.then_inc(S["tx"], 1)

            def up(i, n, turn):
                pe.wait_ge(S["x_lo"], i + 1)
                pe.wait_ge(S["w1_lo"], i + 1)
                wait_for(pe, S["gelu"], i - 1)
                for k in range(DC):
                    c = slice(k * HR, (k + 1) * HR)
                    mm = product(pe, h_ps[n % 2][:], (x_hi[:, n % 2, k], x_lo[:, n % 2, k]),
                                 (w_hi[:, n % 2, c], w_lo[:, n % 2, c]), k == 0, k == DC - 1)
                mm.then_inc(S["mm1"], 1)

            def turn_h(i, n, turn):
                pe.wait_ge(S["gelu"], i + 1)
                wait_for(pe, S["h_lo"], i - 1)
                for k in range(RC):
                    mm = pe.transpose(th_ps[n % 2][:, k], h[:, n % 2, k * P:(k + 1) * P], ident[:])
                mm.then_inc(S["th"], 1)

            def down(i, n, turn):
                pe.wait_ge(S["h_lo"], i + 1)
                pe.wait_ge(S["w2_lo"], i + 1)
                wait_for(pe, S["o_ready"], i - 1)
                for k in range(RC):
                    c = slice(W1 + k * D, W1 + (k + 1) * D)
                    mm = product(pe, o_ps[n % 2][:], (ht_hi[:, n % 2, k], ht_lo[:, n % 2, k]),
                                 (w_hi[:, n % 2, c], w_lo[:, n % 2, c]), k == 0, k == RC - 1)
                mm.then_inc(S["mm2"], 1)

            software_pipeline(pe, RT, [(2, up), (1, turn_x), (3, down), (2, turn_h)], NI)



def stage_choose(nc, ins, d, keep):
    with ExitStack() as ctx:
        sb = lambda n, s, t=FP32: ctx.enter_context(nc.sbuf_tensor("s3_" + n, s, t))
        ps = lambda n, s, t=FP32: ctx.enter_context(nc.psum_tensor("s3_" + n, s, t))
        S = sems(nc, ctx, "s3_", "y_ready rec_in params_in ~rows_in dve turned turned_read nav nav_gelu logits shifted prob_e "
                 "key key_turned")
        ident = keep["ident"]
        order = keep["order"]
        rec = sb("rec", [NB, REC], I32)
        rec_f = rec[:].bitcast(FP32)
        shared = sb("shared", [NB, D])
        routed = [sb(f"routed{n}", [NB, D]) for n in range(2)]
        y = sb("y", [NB, D])
        y_t = sb("y_t", [P, DC, NB])
        wp1 = sb("wp1", [P, DC, P])
        wp2 = sb("wp2", [P, ER])
        bp1 = sb("bp1", [P, 1])
        bp2 = sb("bp2", [NB, ER])
        nav = sb("nav", [P, NB])
        number = sb("number", [NB, ER])
        batch_no = sb("batch_no", [NB, 1])
        v = sb("v", [NB, 4, ER])
        c = sb("c", [NB, 6])
        keys = sb("keys", [1, 2, NB])
        best = sb("best", [1, NB])
        key_i = sb("key_i", [1, 3, NB], I32)
        turned_ps = ps("turned", [P, DC, NB])
        nav_ps = ps("nav_ps", [P, NB])
        logit_ps = ps("logits_ps", [NB, ER])
        key_ps = ps("key_ps", [1, NB])

        block = ctx.enter_context(nc.Block())

        @block.sync
        def _(sp):
            sp.dma_start(rec[:], d["rec"][:, P - 1, :]).then_inc(S["rec_in"], 16)
            sp.dma_start(shared[:], d["shared"][:, P - 1, :]).then_inc(S["params_in"], 16)
            for dst, src in ((wp1[:], ins["wp1"]), (wp2[:], ins["wp2"]), (bp1[:], ins["bp1"]),
                             (bp2[:], ins["bp2"].partition_broadcast(NB)), (number[:], ins["c_eight"]),
                             (batch_no[:], ins["c_batch"])):
                sp.dma_start(dst, src).then_inc(S["params_in"], 16)

        @block.gpsimd
        def _(pool):
            pool.wait_ge(S["rec_in"], 16)
            for n, slot in enumerate((SLOT1, SLOT2)):
                pool.indirect_dma_start(routed[n][:], None, d["routed"],
                                        bass.IndirectOffsetOnAxis(rec[:, slot:slot + 1].bitcast(U32), 0)
                                        ).then_inc(S["rows_in"], 16)

        @block.scalar
        def _(act):
            act.wait_ge(S["nav"], 1)
            act.activation(nav[:], nav_ps[:], ACT.Gelu, bias=bp1[:]).then_inc(S["nav_gelu"], 1)
            act.wait_ge(S["shifted"], 1)
            act.activation(v[:, 1], v[:, 0], ACT.Exp, accum_out=c[:, 1:2]).then_inc(S["prob_e"], 1)

        @block.vector
        def _(dve):
            done = [0]

            def op(ins_):
                done[0] += 1
                ins_.then_inc(S["dve"], 1)
                dve.wait_ge(S["dve"], done[0])

            def signal(ins_, name):
                ins_.then_inc(S[name], 1)
                dve.wait_ge(S[name], 1)

            dve.wait_ge(S["params_in"], 16 * 7)
            dve.wait_ge(S["rows_in"], 32)
            op(dve.scalar_tensor_tensor(y[:], routed[0][:], rec_f[:, GATE1:GATE1 + 1], shared[:], ALU.mult, ALU.add))
            signal(dve.scalar_tensor_tensor(y[:], routed[1][:], rec_f[:, GATE2:GATE2 + 1], y[:], ALU.mult, ALU.add),
                   "y_ready")
            dve.wait_ge(S["turned"], 1)
            signal(dve.tensor_copy(y_t[:], turned_ps[:]), "turned_read")
            dve.wait_ge(S["logits"], 1)
            op(dve.tensor_tensor(v[:, 2], logit_ps[:], bp2[:], ALU.add))
            op(dve.tensor_reduce(c[:, 0:1], v[:, 2], AX, ALU.max))
            signal(dve.tensor_scalar(v[:, 0], v[:, 2], c[:, 0:1], None, ALU.subtract), "shifted")
            dve.wait_ge(S["prob_e"], 1)
            op(dve.reciprocal(c[:, 2:3], c[:, 1:2]))
            op(dve.tensor_scalar(v[:, 3], v[:, 1], c[:, 2:3], None, ALU.mult))
            op(dve.tensor_reduce(c[:, 3:4], v[:, 3], AX, ALU.max))
            op(dve.tensor_scalar(v[:, 2], v[:, 3], c[:, 3:4], float(ER), ALU.is_lt, ALU.mult))
            op(dve.tensor_tensor(v[:, 2], v[:, 2], number[:], ALU.add))
            op(dve.tensor_reduce(c[:, 4:5], v[:, 2], AX, ALU.min))
            signal(dve.scalar_tensor_tensor(c[:, 5:6], c[:, 4:5], float(NB), batch_no[:], ALU.mult, ALU.add), "key")
            dve.wait_ge(S["key_turned"], 1)
            op(dve.tensor_copy(keys[:, 0], key_ps[:]))
            for r in range(NB // 8):
                eight = best[:, 8 * r:8 * r + 8]
                op(dve.max(eight, keys[:, r % 2]))
                if r < NB // 8 - 1:
                    op(dve.match_replace(keys[:, 1 - r % 2], eight, keys[:, r % 2], -1.0))
            op(dve.tensor_copy(key_i[:, 0], best[:]))
            op(dve.tensor_scalar(order[:, 0], key_i[:, 0], 5, None, ALU.arith_shift_right))
            op(dve.tensor_scalar(order[:, 1], key_i[:, 0], NB - 1, None, ALU.bitwise_and))
            op(dve.memset(order[:, 2], 1))
            op(dve.tensor_tensor(order[:, 2, 1:NB], order[:, 0, 1:NB], order[:, 0, 0:NB - 1], ALU.not_equal))

        @block.tensor
        def _(pe):
            pe.wait_ge(S["y_ready"], 1)
            for k in range(DC):
                mm = pe.transpose(turned_ps[:, k], y[:, k * P:(k + 1) * P], ident[0:NB, 0:NB])
            mm.then_inc(S["turned"], 1)
            pe.wait_ge(S["turned_read"], 1)
            for k in range(DC):
                mm = pe.matmul(nav_ps[:], wp1[:, k], y_t[:, k], start=(k == 0), stop=(k == DC - 1))
            mm.then_inc(S["nav"], 1)
            pe.wait_ge(S["nav_gelu"], 1)
            pe.matmul(logit_ps[:], nav[:], wp2[:], start=True, stop=True).then_inc(S["logits"], 1)
            pe.wait_ge(S["key"], 1)
            pe.transpose(key_ps[:], c[:, 5:6], ident[0:NB, 0:NB]).then_inc(S["key_turned"], 1)



def stage_ffn(nc, ins, d, keep):
    with ExitStack() as ctx:
        sb = lambda n, s, t=FP32: ctx.enter_context(nc.sbuf_tensor("s4_" + n, s, t))
        ps = lambda n, s, t=FP32: ctx.enter_context(nc.psum_tensor("s4_" + n, s, t))
        S = sems(nc, ctx, "s4_", "params_in rec_in hrec_in shared_in x_in ~routed1_in ~routed2_in b1_in b2_in w1_in "
                 "w2_in0 w2_in1 w1_hi w1_lo w2_hi w2_lo part_y y base x_plus_y bo_scaled ty y_hi y_lo h_ps h_add gelu th h_hi "
                 "h_lo mm2 z_add tz z_hi z_lo mmo x1 x1_out prev_in dx k_part xk r_part xr ~xk_sent txr xr_hi "
                 "xr_lo mmr r_ready r_out")
        ident = keep["ident"]
        order = keep["order"]
        rec = sb("rec", [P, REC], I32)
        rec_f = rec[:].bitcast(FP32)
        hrec = sb("hrec", [P, REC], I32)
        shared = sb("shared", [P, D])
        x = sb("x", [P, D])
        routed = [sb(f"routed{n}", [P, D]) for n in range(2)]
        y_part = sb("y_part", [P, D])
        y = sb("y", [P, D])
        base_part = sb("base_part", [P, D])
        base = sb("base", [P, 2, D])
        b1 = sb("b1", [P, HS])
        b2 = sb("b2", [P, D])
        bo = sb("bo", [P, D])
        maa_k = sb("maa_k", [P, D])
        maa_r = sb("maa_r", [P, D])
        w1_raw = sb("w1_raw", [P, DC, HS])
        w2_raw = sb("w2_raw", [P, DC, HS])
        w1_hi = sb("w1_hi", [P, DC, HS], FP32R)
        w1_lo = sb("w1_lo", [P, DC, HS], FP32R)
        w2_hi = sb("w2_hi", [P, DC, HS], FP32R)
        w2_lo = sb("w2_lo", [P, DC, HS], FP32R)
        wo_hi, wo_lo = keep["wo_hi"], keep["wo_lo"]
        y_hi = sb("y_hi", [P, DC, P], FP32R)
        y_lo = sb("y_lo", [P, DC, P], FP32R)
        h_pre = sb("h_pre", [P, 2, D])
        h = sb("h", [P, 2, D])
        ht_hi = sb("ht_hi", [P, HC, P], FP32R)
        ht_lo = sb("ht_lo", [P, HC, P], FP32R)
        z = sb("z", [P, D])
        z_hi = sb("z_hi", [P, DC, P], FP32R)
        z_lo = sb("z_lo", [P, DC, P], FP32R)
        x1 = sb("x1", [P, D])
        prev = sb("prev", [P, D])
        dx = sb("dx", [P, D])
        k_part = sb("k_part", [P, D])
        xk = sb("xk", [P, D])
        xr = sb("xr", [P, D])
        xr_hi = sb("xr_hi", [P, DC, P], FP32R)
        xr_lo = sb("xr_lo", [P, DC, P], FP32R)
        r = sb("r", [P, D])
        h_ps = [ps(f"h_ps{n}", [P, D]) for n in range(2)]
        th_ps = [ps(f"th_ps{n}", [P, DC, P]) for n in range(2)]
        ty_ps = ps("ty_ps", [P, DC, P])
        tz_ps = ps("tz_ps", [P, DC, P])
        z_ps = ps("z_ps", [P, D])
        square_ps = ps("square_ps", [P, D])

        block = ctx.enter_context(nc.Block())
        w2_chunk = lambda w, k: w[:, k // 2, (k % 2) * D:(k % 2 + 1) * D]

        @block.sync
        def _(sp):
            def batch(i):
                return sp.value_load(order[0:1, 1, bass.ds(i, 1)], min_val=0, max_val=NB - 1)

            def expert(i):
                return sp.value_load(order[0:1, 0, bass.ds(i, 1)], min_val=0, max_val=ER - 1)

            def is_new(i):
                return sp.value_load(order[0:1, 2, bass.ds(i, 1)], min_val=0, max_val=1) > 0

            def load_rec(i):
                b = batch(i)
                wait_for(sp, S["y"], i)
                sp.dma_start(rec[:], d["rec"][b]).then_inc(S["rec_in"], 16)
                sp.dma_start(shared[:], d["shared"][b]).then_inc(S["shared_in"], 16)

            def load_x(i):
                b = batch(i)
                wait_apart(sp, S["base"], i)
                sp.dma_start(x[:], ins["x_rows"].rearrange("(b p) n -> b p n", p=P)[b]).then_inc(S["x_in"], 16)

            def load_params(i):
                if isinstance(i, int) and i == 0:
                    for dst, src in ((bo, "bo"), (maa_k, "maa_k"), (maa_r, "maa_r")):
                        sp.dma_start(dst[:], ins[src].partition_broadcast(P)).then_inc(S["params_in"], 16)

            def load_w1(i):
                e, new = expert(i), is_new(i)
                wait_apart(sp, S["w1_lo"], i * DC)
                sp.dma_start(w1_raw[:], ins["w1"][e], cond=new).then_inc(S["w1_in"], 16)

            def load_w2(half):
                def stage(i):
                    e, new = expert(i), is_new(i)
                    c = slice(half * DC // 2, (half + 1) * DC // 2)
                    wait_apart(sp, S["w2_lo"], i * DC - (1 - half) * DC // 2)
                    sp.dma_start(w2_raw[:, c], ins["w2"][e, :, c], cond=new).then_inc(S[f"w2_in{half}"], 16)
                return stage

            def load_b1(i):
                e = expert(i)
                wait_for(sp, S["h_add"], 2 * i)
                sp.dma_start(b1[:], ins["b1"][e].partition_broadcast(P)).then_inc(S["b1_in"], 16)

            def load_b2(i):
                e = expert(i)
                wait_for(sp, S["z_add"], i)
                sp.dma_start(b2[:], ins["b2"][e].partition_broadcast(P)).then_inc(S["b2_in"], 16)

            def store_x1(i):
                b = batch(i)
                wait_apart(sp, S["x1"], i + 1)
                wait_apart(sp, S["dx"], i)
                sp.dma_start(prev[1:P], x1[0:P - 1]).then_inc(S["prev_in"], 16)
                sp.dma_start(prev[0:1], ins["cond"][bass.ds(b, 1)]).then_inc(S["prev_in"], 16)
                sp.dma_start(d["x1"][b], x1[:]).then_inc(S["x1_out"], 16)
                wait_apart(sp, S["xk_sent"], i * 16)
                sp.dma_start(hrec[:], d["rec"][b]).then_inc(S["hrec_in"], 16)

            def store_r(i):
                b = batch(i)
                sp.wait_ge(S["r_ready"], i + 1)
                sp.dma_start(d["r"][b], r[:]).then_inc(S["r_out"], 16)

            software_pipeline(sp, NB, [(2, load_b2), (1, load_w1), (5, store_r), (0, load_rec), (0, load_params),
                                       (1, load_w2(0)), (1, load_b1), (3, store_x1), (0, load_x), (1, load_w2(1))])
            sp.wait_ge(S["x1_out"], 16 * NB)
            sp.wait_ge(S["r_out"], 16 * NB)

        @block.gpsimd
        def _(pool):
            def gather(i):
                pool.wait_ge(S["rec_in"], i * 16 + 16)
                for n, slot in enumerate((SLOT1, SLOT2)):
                    wait_apart(pool, S[("part_y", "y")[n]], i)
                    pool.indirect_dma_start(routed[n][:], None, d["routed"],
                                            bass.IndirectOffsetOnAxis(rec[:, slot:slot + 1].bitcast(U32), 0)
                                            ).then_inc(S[f"routed{n + 1}_in"], 16)

            def add_base(i):
                pool.wait_ge(S["x_in"], i * 16 + 16)
                pool.wait_ge(S["y"], i + 1)
                pool.tensor_tensor(base_part[:], x[:], y[:], ALU.add).then_inc(S["x_plus_y"], 1)
                pool.wait_ge(S["x_plus_y"], i + 1)
                wait_for(pool, S["x1"], i - 1)
                pool.tensor_tensor(base[:, i % 2], base_part[:], bo[:], ALU.add).then_inc(S["base"], 1)

            def mix(i):
                pool.wait_ge(S["prev_in"], i * 32 + 32)
                pool.tensor_tensor(dx[:], prev[:], x1[:], ALU.subtract).then_inc(S["dx"], 1)
                pool.wait_ge(S["dx"], i + 1)
                pool.tensor_tensor(k_part[:], dx[:], maa_r[:], ALU.mult).then_inc(S["r_part"], 1)
                pool.wait_ge(S["r_part"], i + 1)
                wait_for(pool, S["txr"], i)
                pool.tensor_tensor(xr[:], k_part[:], x1[:], ALU.add).then_inc(S["xr"], 1)
                pool.wait_ge(S["xr"], i + 1)
                pool.tensor_tensor(k_part[:], dx[:], maa_k[:], ALU.mult).then_inc(S["k_part"], 1)
                pool.wait_ge(S["k_part"], i + 1)
                wait_for(pool, S["xk_sent"], i * 16)
                pool.tensor_tensor(xk[:], k_part[:], x1[:], ALU.add).then_inc(S["xk"], 1)
                pool.wait_ge(S["hrec_in"], i * 16 + 16)
                wait_apart(pool, S["xk"], i + 1)
                pool.indirect_dma_start(d["hash_in"], bass.IndirectOffsetOnAxis(hrec[:, SLOTH:SLOTH + 1].bitcast(U32), 0),
                                        xk[:], None, bounds_check=NTOK - 1, oob_is_err=False).then_inc(S["xk_sent"], 16)

            def scale_bo(i):
                if isinstance(i, int) and i == 0:
                    pool.wait_ge(S["params_in"], 48)
                    pool.tensor_scalar(bo[:], bo[:], 0.3, None, ALU.mult).then_inc(S["bo_scaled"], 1)
                    pool.wait_ge(S["bo_scaled"], 1)

            software_pipeline(pool, NB, [(0, gather), (0, scale_bo), (1, add_base), (3, mix)])
            pool.wait_ge(S["xk_sent"], 16 * NB)

        @block.scalar
        def _(act):
            def split_w(name, raw, hi, mm, per, c0, c1):
                def stage(i):
                    if name == "w2":
                        act.wait_ge(S[f"w2_in{c0 // 2}"], i * 16 + 16)
                    elif c0 == 0:
                        act.wait_ge(S["w1_in"], i * 16 + 16)
                    if c0 == 0:
                        wait_for(act, S[mm], i * per)
                    for c in range(c0, c1):
                        act.activation(hi[:, c], raw[:, c], ACT.Copy).then_inc(S[name + "_hi"], 1)
                return stage

            def gelu(n):
                def stage(i):
                    act.wait_ge(S["h_add"], 2 * i + n + 1)
                    wait_for(act, S["th"], 2 * i + n - 1)
                    act.activation(h[:, n], h_pre[:, n], ACT.Gelu).then_inc(S["gelu"], 1)
                return stage

            def h_hi(n):
                def stage(i):
                    act.wait_ge(S["th"], 2 * i + n + 1)
                    wait_for(act, S["mm2"], i)
                    act.activation(ht_hi[:, n * DC:(n + 1) * DC], th_ps[n][:], ACT.Copy).then_inc(S["h_hi"], 1)
                return stage

            def part_hi(dst, src, turned, used, name):
                def stage(i):
                    act.wait_ge(S[turned], i + 1)
                    wait_for(act, S[used], i if used != "h_ps" else 2 * i)
                    act.activation(dst[:], src[:], ACT.Copy).then_inc(S[name], 1)
                return stage

            def copy_r(i):
                act.wait_ge(S["mmr"], i + 1)
                wait_for(act, S["r_out"], i * 16)
                act.activation(r[:], square_ps[:], ACT.Copy).then_inc(S["r_ready"], 1)

            w1 = lambda c0, c1: split_w("w1", w1_raw, w1_hi, "h_ps", 2, c0, c1)
            w2 = lambda c0, c1: split_w("w2", w2_raw, w2_hi, "mm2", 1, c0, c1)
            software_pipeline(act, NB, [
                (1, w2(0, 2)), (4, copy_r), (1, gelu(0)), (2, part_hi(z_hi, tz_ps, "tz", "mmo", "z_hi")), (1, gelu(1)),
                (1, h_hi(0)), (1, w2(2, 3)), (1, h_hi(1)), (3, part_hi(xr_hi, tz_ps, "txr", "mmr", "xr_hi")),
                (1, w2(3, 4)), (0, w1(0, 2)), (0, part_hi(y_hi, ty_ps, "ty", "h_ps", "y_hi")), (0, w1(2, 4))])

        @block.vector
        def _(dve):
            def split_w(name, raw, hi, lo, c0, c1):
                def stage(i):
                    for c in range(c0, c1):
                        dve.wait_ge(S[name + "_hi"], i * DC + c + 1)
                        dve.tensor_tensor(lo[:, c], raw[:, c], hi[:, c], ALU.subtract).then_inc(S[name + "_lo"], 1)
                return stage

            def h_add(n):
                def stage(i):
                    dve.wait_ge(S["h_ps"], 2 * i + n + 1)
                    if n == 0:
                        dve.wait_ge(S["b1_in"], i * 16 + 16)
                    wait_for(dve, S["gelu"], 2 * i + n - 1)
                    dve.tensor_tensor(h_pre[:, n], h_ps[n][:], b1[:, n * D:(n + 1) * D],
                                      ALU.add).then_inc(S["h_add"], 1)
                return stage

            def h_lo(n):
                def stage(i):
                    dve.wait_ge(S["h_hi"], 2 * i + n + 1)
                    dve.tensor_tensor(ht_lo[:, n * DC:(n + 1) * DC], th_ps[n][:], ht_hi[:, n * DC:(n + 1) * DC],
                                      ALU.subtract).then_inc(S["h_lo"], 1)
                return stage

            def part_lo(dst, src, hi, hi_done, name):
                def stage(i):
                    dve.wait_ge(S[hi_done], i + 1)
                    dve.tensor_tensor(dst[:], src[:], hi[:], ALU.subtract).then_inc(S[name], 1)
                return stage

            def z_add(i):
                dve.wait_ge(S["mm2"], i + 1)
                dve.wait_ge(S["b2_in"], i * 16 + 16)
                wait_for(dve, S["tz"], i)
                dve.tensor_tensor(z[:], z_ps[:], b2[:], ALU.add).then_inc(S["z_add"], 1)

            def x1_(i):
                dve.wait_ge(S["mmo"], i + 1)
                dve.wait_ge(S["base"], i + 1)
                wait_for(dve, S["xk"], i)
                wait_for(dve, S["x1_out"], i * 16)
                dve.scalar_tensor_tensor(x1[:], square_ps[:], 0.3, base[:, i % 2], ALU.mult, ALU.add).then_inc(S["x1"], 1)

            def combine(i):
                dve.wait_ge(S["rec_in"], i * 16 + 16)
                dve.wait_ge(S["shared_in"], i * 16 + 16)
                dve.wait_ge(S["routed1_in"], i * 16 + 16)
                dve.scalar_tensor_tensor(y_part[:], routed[0][:], rec_f[:, GATE1:GATE1 + 1], shared[:],
                                         ALU.mult, ALU.add).then_inc(S["part_y"], 1)
                dve.wait_ge(S["part_y"], i + 1)
                dve.wait_ge(S["routed2_in"], i * 16 + 16)
                wait_for(dve, S["ty"], i)
                wait_for(dve, S["x_plus_y"], i)
                dve.scalar_tensor_tensor(y[:], routed[1][:], rec_f[:, GATE2:GATE2 + 1], y_part[:],
                                         ALU.mult, ALU.add).then_inc(S["y"], 1)

            w1 = lambda c0, c1: split_w("w1", w1_raw, w1_hi, w1_lo, c0, c1)
            w2 = lambda c0, c1: split_w("w2", w2_raw, w2_hi, w2_lo, c0, c1)
            software_pipeline(dve, NB, [
                (2, w2(0, 2)), (2, h_add(0)), (1, combine), (3, part_lo(z_lo, tz_ps, z_hi, "z_hi", "z_lo")), (2, h_add(1)),
                (2, h_lo(0)), (3, x1_), (2, w2(2, 3)), (2, h_lo(1)),
                (4, part_lo(xr_lo, tz_ps, xr_hi, "xr_hi", "xr_lo")), (2, w2(3, 4)), (1, w1(0, 2)), (1, part_lo(y_lo, ty_ps, y_hi, "y_hi", "y_lo")),
                (1, w1(2, 4)), (2, z_add)])

        @block.tensor
        def _(pe):
            def up(n):
                def stage(i):
                    if n == 0:
                        pe.wait_ge(S["y_lo"], i + 1)
                    wait_for(pe, S["h_add"], 2 * i + n - 1)
                    for k in range(DC):
                        if n == 0:
                            pe.wait_ge(S["w1_lo"], i * DC + k + 1)
                        mm = product(pe, h_ps[n][:], (y_hi[:, k], y_lo[:, k]),
                                     (w1_hi[:, k, n * D:(n + 1) * D], w1_lo[:, k, n * D:(n + 1) * D]),
                                     k == 0, k == DC - 1)
                    mm.then_inc(S["h_ps"], 1)
                return stage

            def turn_h(n):
                def stage(i):
                    pe.wait_ge(S["gelu"], 2 * i + n + 1)
                    wait_for(pe, S["h_lo"], 2 * i + n - 1)
                    for k in range(DC):
                        mm = pe.transpose(th_ps[n][:, k], h[:, n, k * P:(k + 1) * P], ident[:])
                    mm.then_inc(S["th"], 1)
                return stage

            def turn(src, ready, dst, free, free_lag, name):
                def stage(i):
                    pe.wait_ge(S[ready], i + 1)
                    wait_for(pe, S[free], min(i - free_lag, NB) if isinstance(i, int) else i - free_lag)
                    for k in range(DC):
                        mm = pe.transpose(dst[:, k], src[:, k * P:(k + 1) * P], ident[:])
                    mm.then_inc(S[name], 1)
                return stage

            def down(i):
                wait_for(pe, S["z_add"], i)
                for k in range(HC):
                    if k % DC == 0:
                        pe.wait_ge(S["h_lo"], 2 * i + k // DC + 1)
                    if k % 2 == 0:
                        pe.wait_ge(S["w2_lo"], i * DC + k // 2 + 1)
                    mm = product(pe, z_ps[:], (ht_hi[:, k], ht_lo[:, k]), (w2_chunk(w2_hi, k), w2_chunk(w2_lo, k)),
                                 k == 0, k == HC - 1)
                mm.then_inc(S["mm2"], 1)

            def square(n, parts, name):
                for k in range(DC):
                    mm = product(pe, square_ps[:], (parts[0][:, k], parts[1][:, k]), (wo_hi[:, n, k], wo_lo[:, n, k]),
                                 k == 0, k == DC - 1)
                mm.then_inc(S[name], 1)

            def times_wo(i):
                pe.wait_ge(S["z_lo"], i + 1)
                wait_for(pe, S["r_ready"], i - 1)
                square(0, (z_hi, z_lo), "mmo")

            def receptance(i):
                pe.wait_ge(S["xr_lo"], i + 1)
                pe.wait_ge(S["x1"], min(i + 2, NB) if isinstance(i, int) else i + 2)
                square(1, (xr_hi, xr_lo), "mmr")

            software_pipeline(pe, NB, [
                (1, up(0)), (2, turn(z, "z_add", tz_ps, "xr_lo", 1, "tz")), (1, up(1)), (1, turn_h(0)),
                (2, times_wo), (1, turn_h(1)),
                (3, turn(xr, "xr", tz_ps, "z_lo", -2, "txr")), (0, turn(y, "y", ty_ps, "y_lo", 0, "ty")),
                (1, down), (3, receptance)])



def stage_hashed(nc, ins, d, keep):
    with ExitStack() as ctx:
        sb = lambda n, s, t=FP32: ctx.enter_context(nc.sbuf_tensor("s5_" + n, s, t))
        ps = lambda n, s, t=FP32: ctx.enter_context(nc.psum_tensor("s5_" + n, s, t))
        S = sems(nc, ctx, "s5_", "x_in0 x_in1 w1_in w2_in w1_hi w1_lo w2_hi w2_lo tx0 tx1 x_hi0 x_hi1 x_lo0 x_lo1 "
                 "g_in g_hi g_lo h_ps pos relu h_hi h_lo mm2 o_ready0 o_ready1 o_out0 o_out1")
        ident = keep["ident"]
        GP = 3 * DC * D // EH
        g_raw = sb("g_raw", [P, GP])
        part = lambda w, e: w[:].rearrange("p g k n -> p (g k n)")[:, bass.ds(e * GP, GP)]
        w1_raw = sb("w1_raw", [P, DC, HS])
        w2_raw = sb("w2_raw", [P, DC, HS])
        w1_hi = sb("w1_hi", [P, DC, HS], FP32R)
        w1_lo = sb("w1_lo", [P, DC, HS], FP32R)
        w2_hi = sb("w2_hi", [P, DC, HS], FP32R)
        w2_lo = sb("w2_lo", [P, DC, HS], FP32R)
        x = sb("x", [P, 2, D])
        x_hi = sb("x_hi", [P, DC, CAP], FP32R)
        x_lo = sb("x_lo", [P, DC, CAP], FP32R)
        NQ = 4
        pos = sb("pos", [P, 2, 2, CAP])
        h = sb("h", [P, HC, CAP])
        ht_hi = sb("ht_hi", [P, HC, CAP], FP32R)
        ht_lo = sb("ht_lo", [P, HC, CAP], FP32R)
        quarter = lambda w, q: w[:, 2 * q:2 * q + 2]
        rows = lambda m: slice(m * P, (m + 1) * P)
        o_sb = sb("o_sb", [P, 2, D])
        h_ps = [ps(f"h_ps{q}", [P, 2, CAP]) for q in range(NQ)]
        tx_ps = [ps(f"tx_ps{n}", [P, DC, P]) for n in range(2)]
        o_ps = [ps(f"o_ps{n}", [P, D]) for n in range(2)]
        w2_chunk = lambda w, k: w[:, k // 2, (k % 2) * D:(k % 2 + 1) * D]

        block = ctx.enter_context(nc.Block())

        @block.sync
        def _(sp):
            def load_x(m):
                def stage(e):
                    wait_for(sp, S[f"tx{m}"], e)
                    sp.dma_start(x[:, m], d["hash_in"][bass.ds(e * CAP + m * P, P)]).then_inc(S[f"x_in{m}"], 16)
                return stage

            def load_w(name, raw):
                def stage(e):
                    wait_for(sp, S[name + "_lo"], e * DC)
                    sp.dma_start(raw[:], ins[name + "h"][e]).then_inc(S[name + "_in"], 16)
                return stage

            def store(m):
                def stage(e):
                    sp.wait_ge(S[f"o_ready{m}"], e + 1)
                    sp.dma_start(d["hash_out"][bass.ds(e * CAP + m * P, P)], o_sb[:, m]).then_inc(S[f"o_out{m}"], 16)
                return stage

            def load_g(e):
                wait_for(sp, S["g_lo"], e)
                sp.dma_start(g_raw[:], ins["gate_x"][e]).then_inc(S["g_in"], 16)

            software_pipeline(sp, EH, [(0, load_w("w1", w1_raw)), (0, load_x(0)), (0, load_x(1)), (2, store(1)),
                                       (0, load_w("w2", w2_raw)), (1, store(0)), (1, load_g)])
            for m in range(2):
                sp.wait_ge(S[f"o_out{m}"], 16 * EH)

        @block.scalar
        def _(act):
            def split_w(name, raw, hi, used, per, c0, c1):
                def stage(e):
                    if c0 == 0:
                        act.wait_ge(S[name + "_in"], e * 16 + 16)
                        wait_for(act, S[used], e * per)
                    for c in range(c0, c1):
                        act.activation(hi[:, c], raw[:, c], ACT.Copy).then_inc(S[name + "_hi"], 1)
                return stage

            def g_hi(e):
                wait_apart(act, S["g_in"], e * 16 + 16)
                act.activation(part(keep["wx_hi"], e), g_raw[:], ACT.Copy).then_inc(S["g_hi"], 1)

            def x_hi_(m):
                def stage(e):
                    act.wait_ge(S[f"tx{m}"], e + 1)
                    wait_for(act, S["h_ps"], NQ * e)
                    act.activation(x_hi[:, :, rows(m)], tx_ps[m][:], ACT.Copy).then_inc(S[f"x_hi{m}"], 1)
                return stage

            def relu(q):
                def stage(e):
                    act.wait_ge(S["h_ps"], NQ * e + q + 1)
                    wait_for(act, S["relu"], NQ * e + q - 1)
                    act.activation(pos[:, q % 2], h_ps[q][:], ACT.Relu).then_inc(S["pos"], 1)
                return stage

            def h_hi(q):
                def stage(e):
                    act.wait_ge(S["relu"], NQ * e + q + 1)
                    wait_for(act, S["mm2"], 2 * e)
                    act.activation(quarter(ht_hi, q), quarter(h, q), ACT.Copy).then_inc(S["h_hi"], 1)
                return stage

            def out(m):
                def stage(e):
                    act.wait_ge(S["mm2"], 2 * e + m + 1)
                    wait_for(act, S[f"o_out{m}"], e * 16)
                    act.activation(o_sb[:, m], o_ps[m][:], ACT.Copy).then_inc(S[f"o_ready{m}"], 1)
                return stage

            w1 = lambda c0, c1: split_w("w1", w1_raw, w1_hi, "h_ps", NQ, c0, c1)
            w2 = lambda c0, c1: split_w("w2", w2_raw, w2_hi, "mm2", 2, c0, c1)
            software_pipeline(act, EH, [
                (2, out(1)), (1, w2(0, 2)), (1, relu(0)), (1, w2(2, 3)), (1, relu(1)), (1, h_hi(0)), (1, w2(3, 4)),
                (1, relu(2)), (1, h_hi(1)), (1, relu(3)), (1, h_hi(2)), (1, h_hi(3)), (0, x_hi_(0)), (0, x_hi_(1)),
                (0, w1(0, 4)), (2, g_hi), (1, out(0))])

        @block.vector
        def _(dve):
            def split_w(name, raw, hi, lo, c0, c1):
                def stage(e):
                    for c in range(c0, c1):
                        dve.wait_ge(S[name + "_hi"], e * DC + c + 1)
                        dve.tensor_tensor(lo[:, c], raw[:, c], hi[:, c], ALU.subtract).then_inc(S[name + "_lo"], 1)
                return stage

            def g_lo(e):
                dve.wait_ge(S["g_hi"], e + 1)
                dve.tensor_tensor(part(keep["wx_lo"], e), g_raw[:], part(keep["wx_hi"], e),
                                  ALU.subtract).then_inc(S["g_lo"], 1)

            def relu2(q):
                def stage(e):
                    dve.wait_ge(S["pos"], NQ * e + q + 1)
                    wait_for(dve, S["h_lo"], NQ * (e - 1) + q + 1)
                    dve.tensor_tensor(quarter(h, q), pos[:, q % 2], h_ps[q][:], ALU.mult).then_inc(S["relu"], 1)
                return stage

            def h_lo(q):
                def stage(e):
                    dve.wait_ge(S["h_hi"], NQ * e + q + 1)
                    dve.tensor_tensor(quarter(ht_lo, q), quarter(h, q), quarter(ht_hi, q),
                                      ALU.subtract).then_inc(S["h_lo"], 1)
                return stage

            def x_lo_(m):
                def stage(e):
                    dve.wait_ge(S[f"x_hi{m}"], e + 1)
                    dve.tensor_tensor(x_lo[:, :, rows(m)], tx_ps[m][:], x_hi[:, :, rows(m)],
                                      ALU.subtract).then_inc(S[f"x_lo{m}"], 1)
                return stage

            w1 = lambda c0, c1: split_w("w1", w1_raw, w1_hi, w1_lo, c0, c1)
            w2 = lambda c0, c1: split_w("w2", w2_raw, w2_hi, w2_lo, c0, c1)
            software_pipeline(dve, EH, [
                (1, w2(0, 2)), (1, relu2(0)), (1, w2(2, 3)), (1, relu2(1)), (1, h_lo(0)), (1, w2(3, 4)),
                (1, relu2(2)), (1, h_lo(1)), (1, relu2(3)), (1, h_lo(2)), (1, h_lo(3)), (0, x_lo_(0)), (0, x_lo_(1)),
                (0, w1(0, 4)), (2, g_lo)])

        @block.tensor
        def _(pe):
            def turn_x(m):
                def stage(e):
                    pe.wait_ge(S[f"x_in{m}"], e * 16 + 16)
                    wait_for(pe, S[f"x_lo{m}"], e)
                    for k in range(DC):
                        mm = pe.transpose(tx_ps[m][:, k], x[:, m, k * P:(k + 1) * P], ident[:])
                    mm.then_inc(S[f"tx{m}"], 1)
                return stage

            def up(q):
                def stage(e):
                    if q == 0:
                        for m in range(2):
                            pe.wait_ge(S[f"x_lo{m}"], e + 1)
                        pe.wait_ge(S["w1_lo"], e * DC + DC)
                    wait_for(pe, S["relu"], NQ * (e - 1) + q + 1)
                    for c in range(2):
                        chunk = slice((2 * q + c) * P, (2 * q + c + 1) * P)
                        for k in range(DC):
                            mm = product(pe, h_ps[q][:, c], (w1_hi[:, k, chunk], w1_lo[:, k, chunk]),
                                         (x_hi[:, k], x_lo[:, k]), k == 0, k == DC - 1)
                    mm.then_inc(S["h_ps"], 1)
                return stage

            def down(m):
                def stage(e):
                    wait_for(pe, S[f"o_ready{m}"], e)
                    for k in range(HC):
                        if k % 2 == 0:
                            pe.wait_ge(S["w2_lo"], e * DC + k // 2 + 1)
                            pe.wait_ge(S["h_lo"], NQ * e + k // 2 + 1)
                        mm = product(pe, o_ps[m][:], (ht_hi[:, k, rows(m)], ht_lo[:, k, rows(m)]),
                                     (w2_chunk(w2_hi, k), w2_chunk(w2_lo, k)), k == 0, k == HC - 1)
                    mm.then_inc(S["mm2"], 1)
                return stage

            software_pipeline(pe, EH, [
                (1, up(0)), (1, up(1)), (1, up(2)), (1, up(3)), (0, turn_x(0)), (0, turn_x(1)), (1, down(0)),
                (1, down(1))])



def stage_recurrent(nc, ins, d, keep, out):
    with ExitStack() as ctx:
        sb = lambda n, s, t=FP32: ctx.enter_context(nc.sbuf_tensor("s6_" + n, s, t))
        ps = lambda n, s, t=FP32: ctx.enter_context(nc.psum_tensor("s6_" + n, s, t))
        S = sems(nc, ctx, "s6_", "params_in w_in wo_in wo_hi wo_lo w_hi w_lo rec_in ~y_in r_in r_sig x2 tx x_raw x_hi x_lo xpart "
                 "gates added acted ig fc c tc c_hi c_lo uo_in ct_ready const_ps const "
                 "p_hi p_lo p_ps p_add p_tanh x1_in0 x1_in1 x1_in2 x1_in3 p_out out0 out1 out2 out3")
        NG = 3
        G_G, G_I, G_F = range(NG)
        ident = keep["ident"]
        NU = 2 * NG
        wx_hi, wx_lo = keep["wx_hi"], keep["wx_lo"]
        w_hi = sb("w_hi", [P, NG, DC, D], FP32R)
        w_lo = sb("w_lo", [P, NG, DC, D], FP32R)
        unit = lambda w, u: w[:].rearrange("p m k n -> p (m k n)")[:, u * HS:(u + 1) * HS]
        raw = sb("raw", [P, 2, HS])
        uo = raw[:].rearrange("p u (k n) -> p (u k) n", n=D)
        wo_hi, wo_lo = wx_hi[:, 0], wx_lo[:, 0]
        x2t = sb("x2t", [P, NB, DC, P])
        staged = x2t[:, NB - 2 * NU:NB].rearrange("p (u i) k n -> p u (i k n)", u=NU)
        bias = sb("bias", [P, NG, D])
        bo = sb("bo", [P, D])
        gate = sb("gate", [P, NG, D])
        c = sb("c", [P, D])
        c_hi = sb("c_hi", [P, DC, P], FP32R)
        c_lo = sb("c_lo", [P, DC, P], FP32R)
        x_hi = sb("x_hi", [P, 2, DC, P], FP32R)
        x_lo = sb("x_lo", [P, 2, DC, P], FP32R)
        rec = sb("rec", [P, REC], I32)
        y = sb("y", [P, D])
        r = sb("r", [P, D])
        x2 = sb("x2", [P, D])
        ct = x2
        g_ps = [[ps(f"g{n}_{g}", [P, D]) for g in range(NG)] for n in range(2)]
        tx_ps = ps("tx_ps", [P, DC, P])
        tc_ps = ps("tc_ps", [P, DC, P])

        NO = 4
        c_x1 = [bias[:, 0], bias[:, 1], bias[:, 2], gate[:, 0]]
        p_out = [r[:], y[:], gate[:, 1], c[:]]
        p_sum = [x2[:], gate[:, 2]]

        block = ctx.enter_context(nc.Block())

        @block.sync
        def _(sp):
            def load(i):
                wait_for(sp, S["x2"], i)
                sp.dma_start(rec[:], d["rec"][i]).then_inc(S["rec_in"], 16)
                sp.dma_start(r[:], d["r"][i]).then_inc(S["r_in"], 16)

            load(0)
            sp.dma_start(c[:], ins["in_c"].partition_broadcast(P)).then_inc(S["params_in"], 16)
            for g in range(NG):
                sp.dma_start(bias[:, g], ins["gate_bias"][g].partition_broadcast(P)).then_inc(S["params_in"], 16)
            sp.dma_start(bo[:], ins["bo_r"].partition_broadcast(P)).then_inc(S["params_in"], 16)

            sp.dma_start(staged, ins["gate_w"][0:NU].rearrange("u p n -> p u n")).then_inc(S["w_in"], 16)
            sp.dma_start(raw[:], ins["gate_w"][NU:NU + 2].rearrange("u p n -> p u n")).then_inc(S["wo_in"], 16)
            with sp.Fori(1, NB) as i:
                load(i)
            sp.wait_ge(S["wo_lo"], 1)
            sp.dma_start(raw[:].rearrange("p u n -> p (u n)"), ins["uo"]).then_inc(S["uo_in"], 16)

            def load_x1(i, n, turn):
                wait_for(sp, S["p_out"], i - NO + 1)
                sp.dma_start(c_x1[n], d["x1"][i]).then_inc(S[f"x1_in{n}"], 16)

            def store(i, n, turn):
                sp.wait_ge(S["p_out"], i + 1)
                sp.dma_start(out[i], p_out[n]).then_inc(S[f"out{n}"], 16)

            sp.wait_ge(S["c"], NB + 1)
            software_pipeline(sp, NB, [(0, load_x1), (3, store)], NO)
            for n in range(NO):
                sp.wait_ge(S[f"out{n}"], 16 * NB // NO)

        @block.gpsimd
        def _(pool):
            def fetch(i):
                pool.wait_ge(S["rec_in"], i * 16 + 16)
                wait_apart(pool, S["x2"], i)
                pool.indirect_dma_start(y[:], None, d["hash_out"],
                                        bass.IndirectOffsetOnAxis(rec[:, SLOTH:SLOTH + 1].bitcast(U32), 0)
                                        ).then_inc(S["y_in"], 16)
                pool.wait_ge(S["y_in"], i * 16 + 16)
                pool.wait_ge(S["r_sig"], i + 1)
                wait_for(pool, S["tx"], i)
                pool.tensor_tensor(x2[:], y[:], r[:], ALU.mult).then_inc(S["x2"], 1)

            fetch(0)
            with pool.Fori(1, NB) as i:
                fetch(i)

        @block.scalar
        def _(act):
            def r_sigmoid(i):
                act.wait_ge(S["r_in"], i * 16 + 16)
                act.activation(r[:], r[:], ACT.Sigmoid).then_inc(S["r_sig"], 1)

            def x_parts(i):
                act.wait_ge(S["tx"], i + 1)
                act.activation(x2t[:, i], tx_ps[:], ACT.Copy).then_inc(S["x_raw"], 1)
                act.wait_ge(S["x_raw"], i + 1)
                wait_apart(act, S["xpart"], i * NG)
                act.activation(x_hi[:, 0], x2t[:, i], ACT.Copy).then_inc(S["x_hi"], 1)

            def gates(i, n, turn):
                for g, f in ((G_G, ACT.Tanh), (G_I, ACT.Sigmoid), (G_F, ACT.Sigmoid)):
                    act.wait_ge(S["added"], i * NG + g + 1)
                    act.activation(gate[:, g], gate[:, g], f).then_inc(S["acted"], 1)

            def p_hi(i, n, turn, early=False):
                if isinstance(i, int) and i < 2 and not early:
                    return
                wait_apart(act, S["p_ps"], i - 1)
                act.activation(x_hi[:, n], x2t[:, i], ACT.Copy).then_inc(S["p_hi"], 1)

            def before_output(i, n, turn):
                if isinstance(i, int) and i == NB - 1:
                    act.wait_ge(S["wo_in"], 16)
                    act.wait_ge(S["xpart"], NB * NG)
                    act.activation(wo_hi.rearrange("p k n -> p (k n)"), raw[:].rearrange("p u n -> p (u n)"),
                                   ACT.Copy).then_inc(S["wo_hi"], 1)
                    act.wait_ge(S["x_raw"], NB)
                    for t in range(2):
                        p_hi(t, t, 0, early=True)

            def c_part(s):
                if isinstance(s, int) and s == NB:
                    return
                act.wait_ge(S["tc"], s + 1)
                act.activation(c_hi[:], tc_ps[:], ACT.Copy).then_inc(S["c_hi"], 1)

            def state_units(i, n, turn):
                if isinstance(i, int) and i == 0:
                    act.wait_ge(S["w_in"], 16)
                    for u in range(NU):
                        act.activation(unit(w_hi, u), staged[:, u], ACT.Copy).then_inc(S["w_hi"], 1)

            c_part(0)
            software_pipeline(act, NB, [
                (0, lambda i, n, turn: r_sigmoid(i)), (2, before_output), (2, gates),
                (2, lambda i, n, turn: c_part(i + 1)), (0, lambda i, n, turn: x_parts(i)), (0, state_units)], 2)
            act.wait_ge(S["tc"], NB + 1)
            act.activation(ct[:], tc_ps[:].rearrange("p k n -> p (k n)"), ACT.Copy).then_inc(S["ct_ready"], 1)
            def p_tanh(i, n, turn):
                act.wait_ge(S["p_add"], i + 1)
                act.activation(p_sum[n], p_sum[n], ACT.Tanh).then_inc(S["p_tanh"], 1)

            software_pipeline(act, NB, [(0, p_hi), (1, p_tanh)], 2)

        @block.vector
        def _(dve):
            def x_lo_(i, n, turn):
                dve.wait_ge(S["x_hi"], i + 1)
                dve.tensor_tensor(x_lo[:, 0], x2t[:, i], x_hi[:, 0], ALU.subtract).then_inc(S["x_lo"], 1)

            def gates(i, n, turn):
                for g in (G_G, G_I, G_F):
                    dve.wait_ge(S["gates"], i * NG + g + 1)
                    dve.wait_ge(S["c"], i + 1)
                    dve.tensor_tensor(gate[:, g], g_ps[n][g][:], bias[:, g], ALU.add).then_inc(S["added"], 1)
                dve.wait_ge(S["acted"], i * NG + 2)
                dve.tensor_tensor(gate[:, G_I], gate[:, G_I], gate[:, G_G], ALU.mult).then_inc(S["ig"], 1)
                dve.wait_ge(S["acted"], i * NG + 3)
                dve.tensor_tensor(gate[:, G_F], gate[:, G_F], c[:], ALU.mult).then_inc(S["fc"], 1)
                dve.wait_ge(S["ig"], i + 1)
                dve.wait_ge(S["fc"], i + 1)
                dve.wait_ge(S["tc"], i + 1)
                dve.tensor_tensor(c[:], gate[:, G_F], gate[:, G_I], ALU.add).then_inc(S["c"], 1)

            def p_lo(i, n, turn, early=False):
                if isinstance(i, int) and i < 2 and not early:
                    return
                n = n % 2
                dve.wait_ge(S["p_hi"], i + 1)
                dve.tensor_tensor(x_lo[:, n], x2t[:, i], x_hi[:, n], ALU.subtract).then_inc(S["p_lo"], 1)

            def before_output(i, n, turn):
                if isinstance(i, int) and i == NB - 1:
                    dve.wait_ge(S["wo_hi"], 1)
                    dve.tensor_tensor(wo_lo.rearrange("p k n -> p (k n)"), raw[:].rearrange("p u n -> p (u n)"),
                                      wo_hi.rearrange("p k n -> p (k n)"), ALU.subtract).then_inc(S["wo_lo"], 1)
                    for t in range(2):
                        p_lo(t, t, 0, early=True)

            def c_part(s):
                if isinstance(s, int) and s == NB:
                    return
                dve.wait_ge(S["c_hi"], s + 1)
                dve.tensor_tensor(c_lo[:], tc_ps[:], c_hi[:], ALU.subtract).then_inc(S["c_lo"], 1)

            dve.wait_ge(S["params_in"], 80)
            dve.tensor_copy(c[:], c[:]).then_inc(S["c"], 1)
            def state_units(i, n, turn):
                if isinstance(i, int) and i == 0:
                    for u in range(NU):
                        dve.wait_ge(S["w_hi"], u + 1)
                        dve.tensor_tensor(unit(w_lo, u), staged[:, u], unit(w_hi, u),
                                          ALU.subtract).then_inc(S["w_lo"], 1)

            c_part(0)
            software_pipeline(dve, NB, [(2, before_output), (2, gates), (2, lambda i, n, turn: c_part(i + 1)), (0, x_lo_),
                                        (0, state_units)], 2)
            dve.wait_ge(S["const_ps"], 1)
            dve.tensor_tensor(bo[:], g_ps[0][2][:], bo[:], ALU.add).then_inc(S["const"], 1)
            dve.wait_ge(S["const"], 1)

            def p_add(i, n, turn):
                dve.wait_ge(S["p_ps"], i + 1)
                wait_for(dve, S["p_out"], i - 1)
                dve.tensor_tensor(p_sum[n % 2], g_ps[n % 2][0][:], bo[:], ALU.add).then_inc(S["p_add"], 1)

            def p_out_(i, n, turn):
                dve.wait_ge(S["p_tanh"], i + 1)
                dve.wait_ge(S[f"x1_in{n}"], turn * 16 + 16)
                wait_for(dve, S[f"out{n}"], turn * 16)
                dve.tensor_tensor(p_out[n], p_sum[n % 2], c_x1[n], ALU.add).then_inc(S["p_out"], 1)

            software_pipeline(dve, NB, [(0, p_lo), (1, p_add), (2, p_out_)], NO)

        @block.tensor
        def _(pe):
            def turn_x(i, n, turn):
                pe.wait_ge(S["x2"], i + 1)
                wait_for(pe, S["x_raw"], i)
                for k in range(DC):
                    mm = pe.transpose(tx_ps[:, k], x2[:, k * P:(k + 1) * P], ident[:])
                mm.then_inc(S["tx"], 1)

            def x_part(gs):
                def stage(i, n, turn):
                    pe.wait_ge(S["x_lo"], i + 1)
                    for g in gs:
                        wait_for(pe, S["added"], (i - 2) * NG + g + 1)
                        for k in range(DC):
                            mm = product(pe, g_ps[n][g][:], (x_hi[:, 0, k], x_lo[:, 0, k]),
                                         (wx_hi[:, g, k], wx_lo[:, g, k]), k == 0, False)
                        mm.then_inc(S["xpart"], 1)
                return stage

            def c_part(i, n, turn):
                pe.wait_ge(S["c_lo"], i + 1)
                for g in range(NG):
                    if isinstance(i, int) and i == 0:
                        pe.wait_ge(S["w_lo"], 2 * g + 2)
                    for k in range(DC):
                        mm = product(pe, g_ps[n][g][:], (c_hi[:, k], c_lo[:, k]),
                                     (w_hi[:, g, k], w_lo[:, g, k]), False, k == DC - 1)
                    mm.then_inc(S["gates"], 1)

            def turn_c(s):
                pe.wait_ge(S["c"], s + 1)
                wait_for(pe, S["c_lo"], s)
                for k in range(DC):
                    mm = pe.transpose(tc_ps[:, k], c[:, k * P:(k + 1) * P], ident[:])
                mm.then_inc(S["tc"], 1)

            def p(i, n, turn, early=False):
                if isinstance(i, int) and i < 2 and not early:
                    return
                pe.wait_ge(S["p_lo"], i + 1)
                wait_for(pe, S["p_add"], i - 1)
                for k in range(DC):
                    mm = product(pe, g_ps[n][0][:], (x_hi[:, n, k], x_lo[:, n, k]), (wo_hi[:, k], wo_lo[:, k]),
                                 k == 0, k == DC - 1)
                mm.then_inc(S["p_ps"], 1)

            def first_outputs(i, n, turn):
                if isinstance(i, int) and i == NB - 1:
                    pe.wait_ge(S["wo_lo"], 1)
                    pe.wait_ge(S["added"], i * NG + 1)
                    for t in range(2):
                        p(t, t, 0, early=True)

            turn_c(0)
            software_pipeline(pe, NB, [
                (2, c_part), (1, x_part((0, 1))), (2, first_outputs), (2, lambda i, n, turn: turn_c(i + 1)),
                (1, x_part((2,))),
                (0, turn_x)], 2)
            pe.wait_ge(S["ct_ready"], 1)
            pe.wait_ge(S["uo_in"], 16)
            for k in range(DC):
                mm = pe.matmul(g_ps[0][2][:], ct[:, k * P:(k + 1) * P], uo[:, k],
                               start=(k == 0), stop=(k == DC - 1))
            mm.then_inc(S["const_ps"], 1)

            software_pipeline(pe, NB, [(1, p)], 2)


SHAPES = {
    "x_rows": ([NTOK, D], FP32), "xt_groups": ([8, P, NB // 8, DC, P], FP32),
    "ids": ([P, NB], I32), "cond_t": ([P, DC, NB], FP32), "rt_w": ([P, DC, ER], FP32), "r_w": ([P, DC, ER], FP32),
    "r_bias": ([ER], FP32), "rw": ([ER, P, DC * HR + RC * D], FP32), "sw": ([12, P, HS], FP32),
    "wp1": ([P, DC, P], FP32), "wp2": ([P, ER], FP32), "bp1": ([P, 1], FP32), "bp2": ([ER], FP32),
    "w1": ([ER, P, DC, HS], FP32), "w2": ([ER, P, DC, HS], FP32), "b1": ([ER, HS], FP32), "b2": ([ER, D], FP32),
    "square": ([2, P, DC * D], FP32), "bo": ([D], FP32), "maa_k": ([D], FP32),
    "maa_r": ([D], FP32), "cond": ([NB, D], FP32), "w1h": ([EH, P, DC, HS], FP32),
    "w2h": ([EH, P, DC, HS], FP32), "gate_x": ([EH, P, 3 * DC * D // EH], FP32), "gate_w": ([8, P, HS], FP32), "gate_bias": ([3, D], FP32),
    "uo": ([P, 2 * HS], FP32), "bo_r": ([D], FP32), "in_c": ([D], FP32),
    "c_batch": ([NB, 1], FP32), "c_eight": ([NB, ER], FP32),
    "c_tri": ([P, P], FP32), "c_ident": ([P, P], FP32), "c_expert": ([P, EH, NB], FP32), "c_run": ([P, EH, NB], FP32),
    "c_tile": ([P, RT, ER], FP32), "c_token": ([P, NB], I32),
}


def constants():
    import numpy as np
    i = np.arange(NB)
    p = np.arange(P)
    return {
        "c_tri": (p[:, None] < p[None, :]).astype(np.float32),
        "c_batch": i[:, None].astype(np.float32),
        "c_eight": np.broadcast_to(np.arange(ER, dtype=np.float32), (NB, ER)),
        "c_ident": np.eye(P, dtype=np.float32),
        "c_expert": np.broadcast_to(np.arange(EH, dtype=np.float32)[None, :, None], (P, EH, NB)),
        "c_run": np.broadcast_to((i > 0).astype(np.float32), (P, EH, NB)),
        "c_tile": np.broadcast_to(np.arange(RT, dtype=np.float32)[None, :, None], (P, RT, ER)),
        "c_token": (i[None, :] * P + p[:, None]).astype(np.int32),
    }


def chunked(w):
    return w.reshape(-1, P, w.shape[-1]).swapaxes(0, 1)


def lay_out(x, cond_1024, itok_BxS_2_50255, L0_cond_router_w, L0_cond_router_t_w, L0_cond_router_bias, L0_cond_sw1,
            L0_cond_sw3, L0_cond_sw2, L0_cond_rw1, L0_cond_rw2, L0_ffn_Wp1, L0_ffn_bp1, L0_ffn_Wp2, L0_ffn_bp2,
            L0_ffn_W1, L0_ffn_b1, L0_ffn_W2, L0_ffn_b2, L0_ffn_Wo, L0_ffn_bo, L1_cond_time_maa_k,
            L1_cond_time_maa_r, L1_cond_w_recept, L1_cond_w_key, L1_cond_w_value, L1_ffn_wf, L1_ffn_uf, L1_ffn_bf,
            L1_ffn_wi, L1_ffn_ui, L1_ffn_bi, L1_ffn_wc, L1_ffn_uc, L1_ffn_bc, L1_ffn_wo, L1_ffn_uo, L1_ffn_bo,
            L1_ffn_in_c):
    import numpy as np
    a = {
        "x_rows": x.reshape(NTOK, D),
        "xt_groups": x.reshape(NB, P, DC, P).transpose(0, 3, 2, 1).reshape(8, NB // 8, P, DC, P).swapaxes(1, 2),
        "ids": itok_BxS_2_50255.T,
        "cond_t": chunked(cond_1024.T),
        "rt_w": chunked(L0_cond_router_t_w.T),
        "r_w": chunked(L0_cond_router_w.T),
        "r_bias": L0_cond_router_bias,
        "sw": np.concatenate([L0_cond_sw1.T.reshape(DC, P, HS), L0_cond_sw3.T.reshape(DC, P, HS),
                              L0_cond_sw2.T.reshape(HC // 2, 2, P, D).swapaxes(1, 2).reshape(HC // 2, P, HS)]),
    }
    a["rw"] = np.concatenate([L0_cond_rw1.reshape(ER, HR, DC, P).transpose(0, 3, 2, 1).reshape(ER, P, DC * HR),
                              L0_cond_rw2.reshape(ER, D, RC, P).transpose(0, 3, 2, 1).reshape(ER, P, RC * D)], 2)
    def by_expert(w):
        return w.reshape(w.shape[0], -1, P, w.shape[-1]).swapaxes(1, 2).reshape(w.shape[0], P, -1, HS)

    def square(w):
        return chunked(w).reshape(P, DC * D)

    a.update(wp1=chunked(L0_ffn_Wp1), wp2=L0_ffn_Wp2, bp1=L0_ffn_bp1[:, None], bp2=L0_ffn_bp2,
             w1=by_expert(L0_ffn_W1), w2=by_expert(L0_ffn_W2), b1=L0_ffn_b1, b2=L0_ffn_b2,
             square=np.stack([square(L0_ffn_Wo), square(L1_cond_w_recept.T)]), bo=L0_ffn_bo, maa_k=L1_cond_time_maa_k,
             maa_r=L1_cond_time_maa_r, cond=cond_1024)
    gate_x = np.concatenate([square(w.T) for w in (L1_ffn_wc, L1_ffn_wi, L1_ffn_wf)], 1)
    gate_w = [L1_ffn_uc, L1_ffn_ui, L1_ffn_uf, L1_ffn_wo]
    a.update(w1h=by_expert(L1_cond_w_key), w2h=by_expert(L1_cond_w_value),
             gate_x=gate_x.reshape(P, EH, -1).swapaxes(0, 1),
             gate_w=np.stack([square(w.T).reshape(P, 2, HS) for w in gate_w]).swapaxes(1, 2).reshape(-1, P, HS),
             gate_bias=np.stack([L1_ffn_bc, L1_ffn_bi, L1_ffn_bf]), uo=chunked(L1_ffn_uo.T).reshape(P, -1),
             bo_r=L1_ffn_bo, in_c=L1_ffn_in_c)
    a.update(constants())
    return a


def build(nc, ins, out):
    with ExitStack() as ctx:
        dram = lambda n, s, t=FP32: nc.dram_tensor("mid_" + n, s, t, kind="Internal").ap()
        d = {"shared": dram("shared", [NB, P, D]), "routed": dram("routed", [NSLOT, D]), "rec": dram("rec", [NB, P, REC], I32),
             "slot_token": dram("slot_token", [NSLOT, 1], I32), "hash_in": dram("hash_in", [NTOK, D]),
             "x1": dram("x1", [NB, P, D]), "r": dram("r", [NB, P, D]),
             "hash_out": dram("hash_out", [NTOK + 1, D])}
        keep = {"ident": ctx.enter_context(nc.sbuf_tensor("ident", [P, P], FP32)),
                "route": ctx.enter_context(nc.sbuf_tensor("route", [P, 2, RT], I32)),
                "order": ctx.enter_context(nc.sbuf_tensor("order", [1, 3, NB], I32))}
        stage_shared(nc, ins, d, keep)
        with ExitStack() as two:
            for n in ("wo_hi", "wo_lo"):
                keep[n] = two.enter_context(nc.sbuf_tensor(n, [P, 2, DC, D], FP32R))
            stage_routed(nc, ins, d, keep)
            stage_choose(nc, ins, d, keep)
            stage_ffn(nc, ins, d, keep)
        with ExitStack() as two:
            for n in ("wx_hi", "wx_lo"):
                keep[n] = two.enter_context(nc.sbuf_tensor(n, [P, 3, DC, D], FP32R))
            stage_hashed(nc, ins, d, keep)
            stage_recurrent(nc, ins, d, keep, out)


def kernel(**inputs):
    import numpy as np
    import concourse.bacc as bacc
    from concourse.bass_utils import run_bass_kernel_spmd

    nc = bacc.Bacc("TRN2", target_bir_lowering=False, num_devices=1)
    arrays = {"in_" + n: np.ascontiguousarray(a)
              for n, a in lay_out(**{n: np.asarray(a) for n, a in inputs.items()}).items()}
    ins = {n: nc.dram_tensor("in_" + n, shape, dtype, kind="ExternalInput").ap() for n, (shape, dtype) in SHAPES.items()}
    out = nc.dram_tensor("out", [NB, P, D], FP32, kind="ExternalOutput").ap()
    build(nc, ins, out)
    return run_bass_kernel_spmd(nc, [arrays], core_ids=[0]).results[0]["out"]
```
